# Optimizing a Trainium2 kernel written in Bass

```python
import numpy as np
import jax
import jax.numpy as jnp

def _softmax(x, axis=-1):
    return jax.nn.softmax(x, axis=axis)

def _gelu(x):
    return jax.nn.gelu(x, approximate=True)

def _silu(x):
    return jax.nn.silu(x)

def _sigmoid(x):
    return jax.nn.sigmoid(x)

def _layernorm(x, axis=-1, eps=1e-05):
    m = jnp.mean(x, axis=axis, keepdims=True)
    v = jnp.var(x, axis=axis, keepdims=True)
    return (x - m) / jnp.sqrt(v + eps)

def _scatter_add(tgt, idx, src, axis=0):
    return tgt.at[idx].add(src)

def _segment_sum(src, seg, n):
    return jax.ops.segment_sum(src, seg, n)
kernel_name = 'mk_decoder_preln_d2_seqx_r8_204d01'

def setup_inputs(seed: int=0):
    np.random.seed(seed)
    _w = jnp.asarray

    def _rec_inputs():
        import jax
        import jax.numpy as jnp
        _rk = jax.random.key(seed)
        x = -0.000125 + 0.9999 * jax.random.normal(jax.random.fold_in(_rk, 1), (16, 128, 256), jnp.float32)
        _lenS = 128 - jax.random.randint(jax.random.fold_in(_rk, 7), (16,), 0, max(1, 128 // 4) + 1, jnp.int32)
        _lenS2 = 128 - jax.random.randint(jax.random.fold_in(_rk, 8), (16,), 0, max(1, 128 // 4) + 1, jnp.int32)
        _ctx_2048P = jax.random.normal(jax.random.fold_in(_rk, 11), (16, 16, 256), jnp.float32)
        _ctx_2048c = jax.random.dirichlet(jax.random.fold_in(_rk, 511), 0.3 * jnp.ones((16,), jnp.float32), (16, 128))
        _ctx_2048t = jnp.einsum('bsk,bkd->bsd', _ctx_2048c, _ctx_2048P)
        _ctx_2048t = _ctx_2048t * jax.lax.rsqrt(jnp.mean(jnp.square(_ctx_2048t)) + 1e-12) * 0.953939
        ctx_2048 = 1.72703e-05 + 1.00003 * (_ctx_2048t + 0.3 * jax.random.normal(jax.random.fold_in(_rk, 611), (16, 128, 256), jnp.float32))
        return (x, ctx_2048)
    x, ctx_2048 = _rec_inputs()

    def _L0_attn_setup():
        import jax, jax.numpy as jnp
        import numpy as np
        B, T, HID = (2, 256, 256)
        H, KV, D = (32, 8, 64)
        G = H // KV
        WINDOW = 32
        THETA = 10000.0

        def _rotate_half(u):
            u1, u2 = (u[..., :D // 2], u[..., D // 2:])
            return jnp.concatenate([-u2, u1], axis=-1)
        key = jax.random.key(seed)
        ks = jax.random.split(key, 10)
        s_in = 1.0 / np.sqrt(HID)
        s_o = 1.0 / np.sqrt(H * D)
        return {'x': jax.random.normal(ks[0], (B, T, HID), jnp.float32), 'Wq': jax.random.normal(ks[1], (HID, H * D), jnp.float32) * s_in, 'bq': jax.random.normal(ks[2], (H * D,), jnp.float32) * 0.01, 'Wk': jax.random.normal(ks[3], (HID, KV * D), jnp.float32) * s_in, 'bk': jax.random.normal(ks[4], (KV * D,), jnp.float32) * 0.01, 'Wv': jax.random.normal(ks[5], (HID, KV * D), jnp.float32) * s_in, 'bv': jax.random.normal(ks[6], (KV * D,), jnp.float32) * 0.01, 'Wo': jax.random.normal(ks[7], (H * D, HID), jnp.float32) * s_o, 'bo': jax.random.normal(ks[8], (HID,), jnp.float32) * 0.01, 'sinks': jax.random.normal(ks[9], (H,), jnp.float32) * 0.1}
    _L0_attn_all = _L0_attn_setup()
    _L0_attn_in = {k: v for k, v in _L0_attn_all.items() if k in ('Wq', 'bq', 'Wk', 'bk', 'Wv', 'bv', 'Wo', 'bo', 'sinks')}
    del _L0_attn_all

    def _L0_xattn_setup():
        import jax, jax.numpy as jnp
        import numpy as np
        DIM = 256
        NH = 16
        HD = DIM // NH
        EPS = 1e-06
        IMG_LEN = 257

        def rms_norm(x, w, eps=EPS):
            xf = x.astype(jnp.float32)
            y = xf * jax.lax.rsqrt(jnp.mean(xf * xf, axis=-1, keepdims=True) + eps)
            return y.astype(x.dtype) * w

        def linear(x, w, b):
            return jnp.einsum('blc,oc->blo', x, w) + b

        def attention(q, k, v):
            scale = 1.0 / jnp.sqrt(jnp.asarray(HD, q.dtype))
            scores = jnp.einsum('bqhd,bkhd->bhqk', q, k) * scale
            probs = jax.nn.softmax(scores, axis=-1)
            return jnp.einsum('bhqk,bkhd->bqhd', probs, v)
        key = jax.random.key(seed)
        ks = jax.random.split(key, 12)
        B, L = (2, 1024)
        s = 0.02
        inp = {'x': jax.random.normal(ks[0], (B, L, DIM), jnp.float32), 'context': jax.random.normal(ks[1], (B, 769, DIM), jnp.float32), 'q_w': jax.random.normal(ks[2], (DIM, DIM), jnp.float32) * s, 'q_b': jnp.zeros((DIM,), jnp.float32), 'k_w': jax.random.normal(ks[3], (DIM, DIM), jnp.float32) * s, 'k_b': jnp.zeros((DIM,), jnp.float32), 'v_w': jax.random.normal(ks[4], (DIM, DIM), jnp.float32) * s, 'v_b': jnp.zeros((DIM,), jnp.float32), 'k_img_w': jax.random.normal(ks[5], (DIM, DIM), jnp.float32) * s, 'k_img_b': jnp.zeros((DIM,), jnp.float32), 'v_img_w': jax.random.normal(ks[6], (DIM, DIM), jnp.float32) * s, 'v_img_b': jnp.zeros((DIM,), jnp.float32), 'o_w': jax.random.normal(ks[7], (DIM, DIM), jnp.float32) * s, 'o_b': jnp.zeros((DIM,), jnp.float32), 'norm_q_w': jnp.ones((DIM,), jnp.float32), 'norm_k_w': jnp.ones((DIM,), jnp.float32), 'norm_k_img_w': jnp.ones((DIM,), jnp.float32)}
        return inp
    _L0_xattn_all = _L0_xattn_setup()
    _L0_xattn_in = {k: v for k, v in _L0_xattn_all.items() if k in ('q_w', 'q_b', 'k_w', 'k_b', 'v_w', 'v_b', 'k_img_w', 'k_img_b', 'v_img_w', 'v_img_b', 'o_w', 'o_b', 'norm_q_w', 'norm_k_w', 'norm_k_img_w')}
    del _L0_xattn_all

    def _L0_ffn_setup():
        import jax, jax.numpy as jnp
        import numpy as np
        TOP_K = 8
        key = jax.random.key(seed)
        k1, k2, k3 = jax.random.split(key, 3)
        B, S, H, E = (4, 512, 256, 64)
        hidden_states = jax.random.normal(k1, (B, S, H), dtype=jnp.float32)
        router_weight = jax.random.normal(k2, (E, H), dtype=jnp.float32)
        router_bias = jnp.zeros((E,), dtype=jnp.float32)
        expert_bias = jax.random.normal(k3, (E, H), dtype=jnp.float32) * 0.1
        return {'hidden_states': hidden_states, 'router_weight': router_weight, 'router_bias': router_bias, 'expert_bias': expert_bias}
    _L0_ffn_all = _L0_ffn_setup()
    _L0_ffn_in = {k: v for k, v in _L0_ffn_all.items() if k in ('router_weight', 'router_bias', 'expert_bias')}
    del _L0_ffn_all

    def _L1_attn_setup():
        import jax, jax.numpy as jnp
        import numpy as np
        D_MODEL = 256
        N_QUERY = 4
        N_HEAD = 8
        D_HEAD = D_MODEL // (N_QUERY * N_HEAD)
        D_KV = D_HEAD * N_HEAD
        BATCH, SEQ = (2, 256)
        key = jax.random.key(seed)
        ks = jax.random.split(key, 5)
        w_scale = 1.0 / np.sqrt(D_MODEL).astype(np.float32)
        x = jax.random.normal(ks[0], (BATCH, SEQ, D_MODEL), jnp.float32)
        Wq = jax.random.normal(ks[1], (D_MODEL, D_MODEL), jnp.float32) * w_scale
        Wk = jax.random.normal(ks[2], (D_KV, D_MODEL), jnp.float32) * w_scale
        Wv = jax.random.normal(ks[3], (D_KV, D_MODEL), jnp.float32) * w_scale
        memory = jax.random.normal(ks[4], (D_KV, D_KV), jnp.float32) * 0.02
        memory_norm = jnp.ones((D_KV, 1), jnp.float32)
        memory_weight = jnp.ones((1,), jnp.float32)
        return dict(x=x, Wq=Wq, Wk=Wk, Wv=Wv, memory=memory, memory_norm=memory_norm, memory_weight=memory_weight)
    _L1_attn_all = _L1_attn_setup()
    _L1_attn_in = {k: v for k, v in _L1_attn_all.items() if k in ('Wq', 'Wk', 'Wv', 'memory', 'memory_norm', 'memory_weight')}
    del _L1_attn_all

    def _L1_xattn_setup():
        import jax, jax.numpy as jnp
        import numpy as np
        B, S, DIM, HD = (4, 128, 256, 128)
        H = DIM // HD
        GN_EPS = 0.001

        def _decay_masks(n_heads, seq_len):
            gam = 1.0 - 2.0 ** (-5.0 - jnp.arange(n_heads, dtype=jnp.float32))
            idx = jnp.arange(seq_len, dtype=jnp.float32)
            expo = idx[None, :] - idx[:, None]
            D = jnp.where(expo[None, :, :] <= 0, gam[:, None, None] ** expo[None, :, :], 0.0)
            return D / jnp.sqrt(D.sum(axis=-1))[:, None, :]
        key = jax.random.key(seed)
        ks = jax.random.split(key, 8)
        x = jax.random.normal(ks[0], (B, S, DIM), dtype=jnp.float32)
        k = jax.random.normal(ks[1], (B, S, DIM), dtype=jnp.float32)
        v = jax.random.normal(ks[2], (B, S, DIM), dtype=jnp.float32)
        Wh = jax.random.normal(ks[3], (H, HD, HD), dtype=jnp.float32) / np.sqrt(HD)
        wg_w = jax.random.normal(ks[4], (DIM, DIM), dtype=jnp.float32) / np.sqrt(DIM)
        wo_w = jax.random.normal(ks[5], (DIM, DIM), dtype=jnp.float32) / np.sqrt(DIM)
        gn_gamma = jnp.ones((DIM,), dtype=jnp.float32)
        gn_beta = jnp.zeros((DIM,), dtype=jnp.float32)
        return {'x': x, 'k': k, 'v': v, 'Wh': Wh, 'wg_w': wg_w, 'wo_w': wo_w, 'gn_gamma': gn_gamma, 'gn_beta': gn_beta}
    _L1_xattn_all = _L1_xattn_setup()
    _L1_xattn_in = {k: v for k, v in _L1_xattn_all.items() if k in ('Wh', 'wg_w', 'wo_w', 'gn_gamma', 'gn_beta')}
    del _L1_xattn_all

    def _L1_ffn_setup():
        import jax, jax.numpy as jnp
        import numpy as np
        B, S, H, I, E, K = (4, 256, 256, 512, 8, 2)
        key = jax.random.key(seed)
        k1, k2, k3, k4 = jax.random.split(key, 4)
        return {'hidden_states': jax.random.normal(k1, (B, S, H), dtype=jnp.float32), 'gate_weight': jax.random.normal(k2, (E, H), dtype=jnp.float32) * 0.02, 'gate_up_proj': jax.random.normal(k3, (E, 2 * I, H), dtype=jnp.float32) * 0.02, 'down_proj': jax.random.normal(k4, (E, H, I), dtype=jnp.float32) * 0.02}
    _L1_ffn_all = _L1_ffn_setup()
    _L1_ffn_in = {k: v for k, v in _L1_ffn_all.items() if k in ('gate_weight', 'gate_up_proj', 'down_proj')}
    del _L1_ffn_all
    return {'x': x, 'ctx_2048': ctx_2048, 'L0_attn_Wq': _L0_attn_in['Wq'], 'L0_attn_bq': _L0_attn_in['bq'], 'L0_attn_Wk': _L0_attn_in['Wk'], 'L0_attn_bk': _L0_attn_in['bk'], 'L0_attn_Wv': _L0_attn_in['Wv'], 'L0_attn_bv': _L0_attn_in['bv'], 'L0_attn_Wo': _L0_attn_in['Wo'], 'L0_attn_bo': _L0_attn_in['bo'], 'L0_attn_sinks': _L0_attn_in['sinks'], 'L0_xattn_q_w': _L0_xattn_in['q_w'], 'L0_xattn_q_b': _L0_xattn_in['q_b'], 'L0_xattn_k_w': _L0_xattn_in['k_w'], 'L0_xattn_k_b': _L0_xattn_in['k_b'], 'L0_xattn_v_w': _L0_xattn_in['v_w'], 'L0_xattn_v_b': _L0_xattn_in['v_b'], 'L0_xattn_k_img_w': _L0_xattn_in['k_img_w'], 'L0_xattn_k_img_b': _L0_xattn_in['k_img_b'], 'L0_xattn_v_img_w': _L0_xattn_in['v_img_w'], 'L0_xattn_v_img_b': _L0_xattn_in['v_img_b'], 'L0_xattn_o_w': _L0_xattn_in['o_w'], 'L0_xattn_o_b': _L0_xattn_in['o_b'], 'L0_xattn_norm_q_w': _L0_xattn_in['norm_q_w'], 'L0_xattn_norm_k_w': _L0_xattn_in['norm_k_w'], 'L0_xattn_norm_k_img_w': _L0_xattn_in['norm_k_img_w'], 'L0_ffn_router_weight': _L0_ffn_in['router_weight'], 'L0_ffn_router_bias': _L0_ffn_in['router_bias'], 'L0_ffn_expert_bias': _L0_ffn_in['expert_bias'], 'L1_attn_Wq': _L1_attn_in['Wq'], 'L1_attn_Wk': _L1_attn_in['Wk'], 'L1_attn_Wv': _L1_attn_in['Wv'], 'L1_attn_memory': _L1_attn_in['memory'], 'L1_attn_memory_norm': _L1_attn_in['memory_norm'], 'L1_attn_memory_weight': _L1_attn_in['memory_weight'], 'L1_xattn_Wh': _L1_xattn_in['Wh'], 'L1_xattn_wg_w': _L1_xattn_in['wg_w'], 'L1_xattn_wo_w': _L1_xattn_in['wo_w'], 'L1_xattn_gn_gamma': _L1_xattn_in['gn_gamma'], 'L1_xattn_gn_beta': _L1_xattn_in['gn_beta'], 'L1_ffn_gate_weight': _L1_ffn_in['gate_weight'], 'L1_ffn_gate_up_proj': _L1_ffn_in['gate_up_proj'], 'L1_ffn_down_proj': _L1_ffn_in['down_proj']}

def reference(x, ctx_2048, L0_attn_Wq, L0_attn_bq, L0_attn_Wk, L0_attn_bk, L0_attn_Wv, L0_attn_bv, L0_attn_Wo, L0_attn_bo, L0_attn_sinks, L0_xattn_q_w, L0_xattn_q_b, L0_xattn_k_w, L0_xattn_k_b, L0_xattn_v_w, L0_xattn_v_b, L0_xattn_k_img_w, L0_xattn_k_img_b, L0_xattn_v_img_w, L0_xattn_v_img_b, L0_xattn_o_w, L0_xattn_o_b, L0_xattn_norm_q_w, L0_xattn_norm_k_w, L0_xattn_norm_k_img_w, L0_ffn_router_weight, L0_ffn_router_bias, L0_ffn_expert_bias, L1_attn_Wq, L1_attn_Wk, L1_attn_Wv, L1_attn_memory, L1_attn_memory_norm, L1_attn_memory_weight, L1_xattn_Wh, L1_xattn_wg_w, L1_xattn_wo_w, L1_xattn_gn_gamma, L1_xattn_gn_beta, L1_ffn_gate_weight, L1_ffn_gate_up_proj, L1_ffn_down_proj):
    import jax
    import jax.numpy as jnp

    def _L0_attn_ref(x, Wq, bq, Wk, bk, Wv, bv, Wo, bo, sinks):
        import jax, jax.numpy as jnp
        import numpy as np
        B, T, HID = (2, 256, 256)
        H, KV, D = (32, 8, 64)
        G = H // KV
        WINDOW = 32
        THETA = 10000.0

        def _rotate_half(u):
            u1, u2 = (u[..., :D // 2], u[..., D // 2:])
            return jnp.concatenate([-u2, u1], axis=-1)
        Bq, Tq, _ = x.shape
        q = (x @ Wq + bq).reshape(Bq, Tq, H, D).transpose(0, 2, 1, 3)
        k = (x @ Wk + bk).reshape(Bq, Tq, KV, D).transpose(0, 2, 1, 3)
        v = (x @ Wv + bv).reshape(Bq, Tq, KV, D).transpose(0, 2, 1, 3)
        inv_freq = 1.0 / THETA ** (jnp.arange(0, D, 2, dtype=jnp.float32) / D)
        t = jnp.arange(Tq, dtype=jnp.float32)
        freqs = t[:, None] * inv_freq[None, :]
        emb = jnp.concatenate([freqs, freqs], axis=-1)
        cos = jnp.cos(emb)[None, None].astype(x.dtype)
        sin = jnp.sin(emb)[None, None].astype(x.dtype)
        q = q * cos + _rotate_half(q) * sin
        k = k * cos + _rotate_half(k) * sin
        k = jnp.repeat(k, G, axis=1)
        v = jnp.repeat(v, G, axis=1)
        scale = D ** (-0.5)
        scores = jnp.einsum('bhqd,bhkd->bhqk', q, k) * scale
        i = jnp.arange(Tq)
        mask = (i[None, :] > i[:, None]) | (i[:, None] - i[None, :] >= WINDOW)
        scores = jnp.where(mask[None, None], -jnp.inf, scores)
        sink_col = jnp.broadcast_to(sinks[None, :, None, None], (Bq, H, Tq, 1))
        combined = jnp.concatenate([scores, sink_col], axis=-1)
        probs = jax.nn.softmax(combined, axis=-1)[..., :-1]
        out = jnp.einsum('bhqk,bhkd->bhqd', probs, v)
        out = out.transpose(0, 2, 1, 3).reshape(Bq, Tq, H * D)
        return out @ Wo + bo

    def _L0_xattn_ref(x, context, q_w, q_b, k_w, k_b, v_w, v_b, k_img_w, k_img_b, v_img_w, v_img_b, o_w, o_b, norm_q_w, norm_k_w, norm_k_img_w):
        import jax, jax.numpy as jnp
        import numpy as np
        DIM = 256
        NH = 16
        HD = DIM // NH
        EPS = 1e-06
        IMG_LEN = 257

        def rms_norm(x, w, eps=EPS):
            xf = x.astype(jnp.float32)
            y = xf * jax.lax.rsqrt(jnp.mean(xf * xf, axis=-1, keepdims=True) + eps)
            return y.astype(x.dtype) * w

        def linear(x, w, b):
            return jnp.einsum('blc,oc->blo', x, w) + b

        def attention(q, k, v):
            scale = 1.0 / jnp.sqrt(jnp.asarray(HD, q.dtype))
            scores = jnp.einsum('bqhd,bkhd->bhqk', q, k) * scale
            probs = jax.nn.softmax(scores, axis=-1)
            return jnp.einsum('bhqk,bkhd->bqhd', probs, v)
        B, L, _ = x.shape
        ctx_img = context[:, :IMG_LEN]
        ctx_txt = context[:, IMG_LEN:]
        q = rms_norm(linear(x, q_w, q_b), norm_q_w).reshape(B, L, NH, HD)
        k = rms_norm(linear(ctx_txt, k_w, k_b), norm_k_w).reshape(B, -1, NH, HD)
        v = linear(ctx_txt, v_w, v_b).reshape(B, -1, NH, HD)
        k_img = rms_norm(linear(ctx_img, k_img_w, k_img_b), norm_k_img_w).reshape(B, -1, NH, HD)
        v_img = linear(ctx_img, v_img_w, v_img_b).reshape(B, -1, NH, HD)
        img_x = attention(q, k_img, v_img)
        txt_x = attention(q, k, v)
        out = (txt_x + img_x).reshape(B, L, DIM)
        return linear(out, o_w, o_b)

    def _L0_ffn_ref(hidden_states, router_weight, router_bias, expert_bias):
        import jax, jax.numpy as jnp
        import numpy as np
        TOP_K = 8
        B, S, H = hidden_states.shape
        flat = hidden_states.reshape(B * S, H)
        logits = jnp.einsum('th,eh->te', flat, router_weight) + router_bias
        scores = jax.nn.softmax(logits, axis=-1)
        topk_w, topk_idx = jax.lax.top_k(scores, TOP_K)
        gathered_bias = expert_bias[topk_idx]
        out = flat * jnp.sum(topk_w, axis=-1, keepdims=True) + jnp.einsum('tk,tkh->th', topk_w, gathered_bias)
        return out.reshape(B, S, H)

    def _L1_attn_ref(x, Wq, Wk, Wv, memory, memory_norm, memory_weight):
        import jax, jax.numpy as jnp
        import numpy as np
        D_MODEL = 256
        N_QUERY = 4
        N_HEAD = 8
        D_HEAD = D_MODEL // (N_QUERY * N_HEAD)
        D_KV = D_HEAD * N_HEAD
        BATCH, SEQ = (2, 256)
        b, s, d = x.shape
        q = x @ Wq.T
        k = x @ Wk.T
        v = x @ Wv.T
        qh = q.reshape(b, s, N_QUERY, N_HEAD, D_HEAD)
        kh = k.reshape(b, s, N_HEAD, D_HEAD)
        vh = v.reshape(b, s, N_HEAD, D_HEAD)
        scale = np.float32(1.0 / np.sqrt(np.float32(D_HEAD)))
        scores = jnp.einsum('bsqhd,bthd->bqhst', qh, kh) * scale
        probs = jax.nn.softmax(scores, axis=-1)
        a_dot = jnp.einsum('bqhst,bthd->bsqhd', probs, vh)
        a_dot = a_dot.reshape(b, s, N_QUERY * N_HEAD, D_HEAD)
        sigma_q = jax.nn.elu(q.reshape(b, s, N_QUERY, D_KV))
        a_mem = sigma_q @ memory / (sigma_q @ memory_norm)
        a_mem = a_mem.reshape(b, s, N_QUERY * N_HEAD, D_HEAD)
        w = jax.nn.sigmoid(memory_weight)
        out = a_dot * (1.0 - w) + a_mem * w
        return out.reshape(b, s, D_MODEL)

    def _L1_xattn_ref(x, k, v, Wh, wg_w, wo_w, gn_gamma, gn_beta):
        import jax, jax.numpy as jnp
        import numpy as np
        B, S, DIM, HD = (4, 128, 256, 128)
        H = DIM // HD
        GN_EPS = 0.001

        def _decay_masks(n_heads, seq_len):
            gam = 1.0 - 2.0 ** (-5.0 - jnp.arange(n_heads, dtype=jnp.float32))
            idx = jnp.arange(seq_len, dtype=jnp.float32)
            expo = idx[None, :] - idx[:, None]
            D = jnp.where(expo[None, :, :] <= 0, gam[:, None, None] ** expo[None, :, :], 0.0)
            return D / jnp.sqrt(D.sum(axis=-1))[:, None, :]
        b, s, dim = x.shape
        h, hd, _ = Wh.shape
        xh = x.reshape(b, s, h, hd)
        kh = k.reshape(b, s, h, hd)
        vh = v.reshape(b, s, h, hd)
        Q = jnp.einsum('bshd,hde->bshe', xh, Wh)
        K = jnp.einsum('bshd,hde->bshe', kh, Wh)
        V = jnp.einsum('bshd,hde->bshe', vh, Wh)
        scores = jnp.einsum('bshe,bthe->bhst', Q, K) / jnp.sqrt(jnp.float32(hd))
        Dn = _decay_masks(h, s)
        masked = scores * Dn[None, :, :, :]
        A = jnp.maximum(jnp.abs(masked.sum(axis=0)), 1.0)
        O = jnp.einsum('hst,bthe->bshe', A, V).reshape(b, s, dim)
        mu = O.mean(axis=-1, keepdims=True)
        var = O.var(axis=-1, keepdims=True)
        Y = (O - mu) / jnp.sqrt(var + GN_EPS) * gn_gamma + gn_beta
        W = jax.nn.relu(x @ wg_w)
        return W * Y @ wo_w

    def _L1_ffn_ref(hidden_states, gate_weight, gate_up_proj, down_proj):
        import jax, jax.numpy as jnp
        import numpy as np
        B, S, H, I, E, K = (4, 256, 256, 512, 8, 2)
        b, s, h = hidden_states.shape
        num_experts, top_k = (gate_weight.shape[0], K)
        x = hidden_states.reshape(-1, h)
        router_logits = x @ gate_weight.T
        probs = jax.nn.softmax(router_logits.astype(jnp.float32), axis=-1)
        top_v, top_i = jax.lax.top_k(probs, top_k)
        top_v = top_v / top_v.sum(axis=-1, keepdims=True)
        combine_w = jnp.einsum('tke,tk->te', jax.nn.one_hot(top_i, num_experts, dtype=top_v.dtype), top_v).astype(x.dtype)

        def expert_step(acc, inp):
            gu, dp, w = inp
            gate, up = jnp.split(x @ gu.T, 2, axis=-1)
            hidden = jax.nn.silu(gate) * up
            y = hidden @ dp.T
            return (acc + w[:, None] * y, None)
        out, _ = jax.lax.scan(expert_step, jnp.zeros_like(x), (gate_up_proj, down_proj, combine_w.T))
        return out.reshape(b, s, h)
    x = x + _L0_attn_ref(_layernorm(x, axis=-1), L0_attn_Wq, L0_attn_bq, L0_attn_Wk, L0_attn_bk, L0_attn_Wv, L0_attn_bv, L0_attn_Wo, L0_attn_bo, L0_attn_sinks)
    x = x + _L0_xattn_ref(_layernorm(x, axis=-1), ctx_2048, L0_xattn_q_w, L0_xattn_q_b, L0_xattn_k_w, L0_xattn_k_b, L0_xattn_v_w, L0_xattn_v_b, L0_xattn_k_img_w, L0_xattn_k_img_b, L0_xattn_v_img_w, L0_xattn_v_img_b, L0_xattn_o_w, L0_xattn_o_b, L0_xattn_norm_q_w, L0_xattn_norm_k_w, L0_xattn_norm_k_img_w)
    x = x + _L0_ffn_ref(_layernorm(x, axis=-1), L0_ffn_router_weight, L0_ffn_router_bias, L0_ffn_expert_bias)
    x = x + _L1_attn_ref(_layernorm(x, axis=-1), L1_attn_Wq, L1_attn_Wk, L1_attn_Wv, L1_attn_memory, L1_attn_memory_norm, L1_attn_memory_weight)
    x = x + _L1_xattn_ref(_layernorm(x, axis=-1), ctx_2048, ctx_2048, L1_xattn_Wh, L1_xattn_wg_w, L1_xattn_wo_w, L1_xattn_gn_gamma, L1_xattn_gn_beta)
    x = x + _L1_ffn_ref(_layernorm(x, axis=-1), L1_ffn_gate_weight, L1_ffn_gate_up_proj, L1_ffn_down_proj)
    return x

_drawn_inputs = setup_inputs


def setup_inputs(seed=0):
    import zlib

    import numpy as np

    out = dict(_drawn_inputs(seed))
    spreads = {'L0_xattn_q_b': (0.0, 0.1),
     'L0_xattn_k_b': (0.0, 0.1),
     'L0_xattn_v_b': (0.0, 0.1),
     'L0_xattn_k_img_b': (0.0, 0.1),
     'L0_xattn_v_img_b': (0.0, 0.1),
     'L0_xattn_o_b': (0.0, 0.1),
     'L0_xattn_norm_q_w': (1.0, 0.2),
     'L0_xattn_norm_k_w': (1.0, 0.2),
     'L0_xattn_norm_k_img_w': (1.0, 0.2),
     'L0_ffn_router_bias': (0.0, 0.1),
     'L1_attn_memory_norm': (1.0, 0.2),
     'L1_xattn_gn_gamma': (1.0, 0.2),
     'L1_xattn_gn_beta': (0.0, 0.1)}
    factors = {'L1_attn_Wk': 3.378,
     'L1_ffn_gate_weight': 8.0,
     'L1_ffn_gate_up_proj': 7.805,
     'L1_ffn_down_proj': 7.823}
    for name, (base, spread) in spreads.items():
        noise = np.random.default_rng([zlib.crc32(name.encode()), seed]).standard_normal(out[name].shape)
        drawn = base * np.exp(spread * noise) if base else spread * noise
        out[name] = jnp.asarray(drawn.astype(out[name].dtype))
    for name, factor in factors.items():
        out[name] = (out[name] * factor).astype(out[name].dtype)
    return out
```

```python
from contextlib import ExitStack

import numpy as np

import concourse.bass as bass
from concourse import mybir

F32 = mybir.dt.float32
BF16 = mybir.dt.bfloat16
U32 = mybir.dt.uint32
ALU = mybir.AluOpType
ACT = mybir.ActivationFunctionType
AX = mybir.AxisListType

NSEQ, T, DM = 16, 128, 256
P = 128
KT_ = DM // P
NH0, NKV, D0, G0, WIN = 32, 8, 64, 4, 32
NBLK = T // WIN
SCALE0 = float(D0) ** -0.5
MASKED = -1.0e30
NHX, DHX = 16, 16
NHM, DHM, NQM = 8, 8, 4
E0, TOP0 = 64, 8
NE, NI = 8, 512
EPS_LN, EPS_RMS, EPS_GN = 1e-5, 1e-6, 1e-3


SOFT = ("0", "1", "3a", "3b")
FAMILIES = {
    "var": [f"var{n}" for n in range(5)], "rstd": [f"rstd{n}" for n in range(5)],
    "ln": [f"ln{n}" for n in range(5)], "tr": [f"tr{n}" for n in range(5)],
    "xT": [f"xT{n}" for n in range(5)],
    "scores": [f"s{n}" for n in SOFT], "shifted": [f"s{n}m" for n in SOFT],
    "probs_high": [f"p{n}h" for n in SOFT], "probs": [f"p{n}" for n in SOFT],
    "probs_turned": [f"pT{n}" for n in SOFT], "turned_high": [f"pt{n}h" for n in SOFT],
    "turned": [f"pt{n}" for n in SOFT], "weighted": [f"pv{n}" for n in SOFT],
    "b_var": [f"b_var{n}" for n in ("", "g", "5")], "b_rstd": [f"b_rstd{n}" for n in ("", "g", "5")],
}
MEMBER = {m: (f, k, len(ms)) for f, ms in FAMILIES.items() for k, m in enumerate(ms)}


def at(name, it, u):
    _, k, uses = MEMBER.get(name, (name, 0, 1))
    return it * (2 * uses) + (2 * k + u + 1)


def program(nc, a, out):
    with ExitStack() as ctx:
        def sb(name, shape, dt=F32):
            return ctx.enter_context(nc.sbuf_tensor(name, shape, dt))

        def sem(name):
            return ctx.enter_context(nc.semaphore(name))

        sigs = {}

        def sig(name):
            name = MEMBER.get(name, (name,))[0]
            if name not in sigs:
                sigs[name] = sem("s_" + name)
            return sigs[name]

        def two(name, shape, dt=F32):
            return [sb(f"{name}{u}", shape, dt) for u in range(2)]

        PS = [ctx.enter_context(nc.psum_tensor(f"ps{u}", [P, 4, 512], F32)) for u in range(2)]

        ident = sb("ident", [P, P])
        identb = sb("identb", [P, P], BF16)
        cosI, sinI = sb("cosI", [P, 512]), sb("sinI", [P, 512])
        mask = sb("mask", [P, NBLK * 64])
        sinkT = sb("sinkT", [P, 32])
        eps = sb("eps", [P, 4])
        decay = sb("decay", [P, 2, T])
        iota8 = sb("iota8", [P, NE])
        bq, bk = sb("bq", [P, 4, P]), sb("bk", [P, 4])
        rows = sb("rows", [P, 9, DM])
        BO, QB, KB, VB, OB, NQ, NK_, GAM, BET = range(9)
        bv = sb("bv", [P, 512])
        rb = sb("rb", [P, E0])
        wq_h, wq_l = sb("wq_h", [P, KT_, 2048], BF16), sb("wq_l", [P, KT_, 2048], BF16)
        wk_h, wk_l = sb("wk_h", [P, KT_, 512], BF16), sb("wk_l", [P, KT_, 512], BF16)
        wv_h, wv_l = sb("wv_h", [P, KT_, 512], BF16), sb("wv_l", [P, KT_, 512], BF16)
        wo_h, wo_l = sb("wo_h", [P, 16, DM], BF16), sb("wo_l", [P, 16, DM], BF16)
        wx = sb("wx", [P, 4, KT_, DM])
        rw = sb("rw", [P, KT_, E0])
        ebias = sb("ebias", [E0, DM])
        wm = sb("wm", [P, KT_, 384])
        mem = sb("mem", [P, 65])
        memw = sb("memw", [P, 4])
        wh = sb("wh", [P, 2, P])
        wgo = sb("wgo", [P, 2, KT_, DM])
        gw = sb("gw", [P, KT_, NE])
        acc = sb("acc", [P, 2, T])
        mixT = sb("mixT", [P, 2, T])
        xall = sb("xall", [P, NSEQ, DM])
        vall = sb("vall", [P, NSEQ, 2, P])

        xin, cin = two("xin", [P, DM]), two("cin", [P, DM])
        xr, xn = two("xr", [P, DM]), two("xn", [P, DM])
        bst, mv, rstd = two("bst", [P, 6]), two("mv", [P, 2]), two("rstd", [P, 2])
        xT_h, xT_l = two("xT_h", [P, KT_, 160], BF16), two("xT_l", [P, KT_, 160], BF16)
        xT, cT = two("xT", [P, KT_, T]), two("cT", [P, KT_, T])
        big = two("big", [P, 2048])
        qhl = two("qhl", [P, 2048])
        q_h = [b[:, 0:1024].bitcast(BF16) for b in qhl]
        q_l = [b[:, 1024:2048].bitcast(BF16) for b in qhl]
        k_h, k_l = two("k_h", [P, 4, 160], BF16), two("k_l", [P, 4, 160], BF16)
        kf = two("kf", [P, 2, 512])
        v_h, v_l = two("v_h", [P, 1024], BF16), two("v_l", [P, 1024], BF16)
        ptf = two("ptf", [P, 2048])
        pt_h = [b[:, 0:1024].bitcast(BF16) for b in ptf]
        pt_l = [b[:, 1024:2048].bitcast(BF16) for b in ptf]
        st32 = two("st32", [P, 4, 32])
        qf = [b[:, 0:DM] for b in big]
        kvf = [b[:, DM:3 * DM].rearrange("p (a d) -> p a d", a=2) for b in big]
        af2 = [b[:, 3 * DM:4 * DM] for b in big]
        qp, kp = v_h, v_l
        vp_h, vp_l = two("vp_h", [P, 272], BF16), two("vp_l", [P, 272], BF16)
        af = two("af", [P, DM])
        aT = two("aT", [P, KT_, T])
        lg, wt = two("lg", [P, 2, E0]), two("wt", [P, T])
        sm = two("sm", [P, 16])

        n_const = 27
        A = a

        def split(c):
            return [slice(c * P, (c + 1) * P)]

        n_consts = 16 + 2 + 9 + 3

        def ps_f(u, b, w=512, o=0):
            return PS[u][:, b, o:o + w]

        def psb(u, b):
            return PS[u][:, b, :].bitcast(BF16)

        ps_all = [PS[u][:, :, :].rearrange("p b n -> p (b n)") for u in range(2)]

        def q_table(t, n):
            return t[:, None, :].to_broadcast([P, n, 512])

        def k_table(t, n):
            v = t[:]
            return bass.AP(v.tensor, v.offset, [v.ap[0], [0, n], [G0 * WIN, NBLK], [1, WIN]])

        def by_block(u):
            return ps_all[u].rearrange("p (i k r) -> p k i r", i=NBLK, r=WIN)

        def by_token(b):
            return b.rearrange("p (k i r) -> p k i r", i=NBLK, r=WIN)

        def place(h, tiles):
            return (h % tiles) * (16 // tiles) + (h % 16) // tiles

        def head_at(j, tiles):
            return tiles * (j % (16 // tiles)) + j // (16 // tiles)

        def apart(eng):
            eng.sem_inc(sig("apart"), 1)

        class Own:

            def __init__(self, eng, name, per_turn=None):
                self.eng, self.sem, self.n = eng, sig(name), 0
                self.per_turn, self.it, self.base = per_turn, None, 0

            def value(self):
                return self.base + self.n if self.it is None else self.it * self.per_turn + (self.base + self.n)

            def mark(self, ins):
                ins.then_inc(self.sem, 1)
                self.n += 1

            def wait(self):
                self.eng.wait_ge(self.sem, self.value())

            def link(self, ins):
                self.mark(ins)
                self.wait()

            def enter(self, it):
                self.base, self.n, self.it = self.base + self.n, 0, it

            def leave(self, turns):
                assert self.n == self.per_turn, (self.sem, self.n, self.per_turn)
                self.base, self.n, self.it = self.base + turns * self.per_turn, 0, None

        PER = {"act": 26, "dve": 164, "act_b": 6, "dve_b": 40, "dve_c": 26}

        xa_h, xa_l = wq_h, wq_l
        cw = sb("cw", [P, NSEQ, NE])
        ecw = two("ecw", [P, NSEQ])
        idx = two("idx", [P, 8], U32)
        gu_f = [b[:] for b in big]
        dn_f = [b[:, 0:1024] for b in qhl]
        v32 = vall[:].rearrange("p b h e -> p (b h e)")
        eh = [wo_h[:].rearrange("p k n -> p (k n)"), v32[:, 0:1536].bitcast(BF16)]
        el = [wo_l[:].rearrange("p k n -> p (k n)"), v32[:, 1536:3072].bitcast(BF16)]
        NBLKC, TB = 4, 512
        sil = [kf[s][:, 0, :] for s in range(2)]
        prod = [kf[s][:, 1, :] for s in range(2)]

        def order_c(hidden, down):
            for n in range(2 * NBLKC + 1):
                if n < 2 * NBLKC:
                    hidden(n)
                if n >= 1:
                    down(n - 1)

        def tensor_b(pe, mm, mm3):
            with pe.Fori(0, NSEQ // 2) as it:
                def W(name, u):
                    pe.wait_ge(sig(name), at(name, it, u))

                def tr(u, name, ready, bank, src):
                    W(ready, u)
                    for k in range(KT_):
                        m = pe.transpose(ps_f(u, bank, P, k * P), src[u][:, k * P:(k + 1) * P], ident[:])
                    m.then_inc(sig(name), 1)

                def b1(u):
                    W("b_xT", u)
                    pe.wait_ge(sig("mixT"), 1)
                    for h in range(2):
                        mm(ps_f(u, 0, P, h * P), mixT[:, h, :], big[u][:, h * P:(h + 1) * P], True, True)
                    for k in range(KT_):
                        m = mm(ps_f(u, 0, DM, DM), xT[u][:, k, :], wgo[:, 0, k, :], k == 0, k == KT_ - 1)
                    m.then_inc(sig("b_mix"), 1)

                def b2(u):
                    W("b_aT", u)
                    for k in range(KT_):
                        m = mm(ps_f(u, 2, DM), aT[u][:, k, :], wgo[:, 1, k, :], k == 0, k == KT_ - 1)
                    m.then_inc(sig("b_wo"), 1)

                def b3(u):
                    W("b_xT5", u)
                    for k in range(KT_):
                        m = mm(ps_f(u, 0, NE), xT[u][:, k, :], gw[:, k, :], k == 0, k == KT_ - 1)
                    m.then_inc(sig("b_gate"), 1)

                for s in (lambda u: tr(u, "b_tr", "b_ln", 1, xn), b1, lambda u: tr(u, "b_atr", "b_a", 1, af), b2,
                          lambda u: tr(u, "b_tr5", "b_ln5", 3, xn), b3):
                    for u in range(2):
                        s(u)

            pe.wait_ge(sig("w0_lo"), 1)
            pe.wait_ge(sig("xa_lo"), NSEQ)
            with pe.Fori(0, NE // 2) as it:
                def hidden(n):
                    p, j = n // NBLKC, n % NBLKC
                    if j == 0:
                        pe.wait_ge(sig(f"w{p}_lo"), it + 1)
                    gh, gl = [w[p][:, 0:2048].rearrange("p (k n) -> p k n", k=KT_) for w in (eh, el)]
                    tok = slice(j * TB, (j + 1) * TB)
                    for i in range(4):
                        q = n * 4 + i
                        pe.wait_ge(sig("c_prod"), it * 32 + max(q - 1, 0))
                        for g in range(2):
                            c = slice(g * NI + i * P, g * NI + (i + 1) * P)
                            for k in range(KT_):
                                m = mm3(ps_f(0, 2 * (q % 2) + g), gh[:, k, c], gl[:, k, c],
                                        xa_h[:, k, tok], xa_l[:, k, tok], k == 0, k == KT_ - 1)
                        m.then_inc(sig("c_hid"), 1)

                def down(n):
                    p, m_ = n // NBLKC, n % 2
                    dh, dl = [w[p][:, 2048:3072].rearrange("p (k n) -> p k n", k=4) for w in (eh, el)]
                    pe.wait_ge(sig("c_hl"), it * 32 + 4 * n + 4)
                    pe.wait_ge(sig("c_acc"), it * 8 + max(n - 1, 0))
                    for t in range(4):
                        o = ps_f(1, 2 * m_ + t // 2, DM, (t % 2) * DM)
                        for i in range(4):
                            c = slice(i * TB + t * P, i * TB + (t + 1) * P)
                            m = mm3(o, pt_h[m_][:, c], pt_l[m_][:, c], dh[:, i, :], dl[:, i, :], i == 0, i == 3)
                    m.then_inc(sig("c_down"), 1)

                order_c(hidden, down)

        def scalar_b(act, own, f):
            own_b = Own(act, "act_own_b", PER["act_b"])
            with act.Fori(0, NSEQ // 2) as it:
                own_b.enter(it)

                def W(name, u):
                    act.wait_ge(sig(name), at(name, it, u))

                def rs(u, n, e=0):
                    W(f"b_var{n}", u)
                    own_b.link(f(rstd[u][:, 0:1], mv[u][:, 1:2], ACT.Ln, bias=eps[:, e:e + 1]))
                    f(rstd[u][:, 0:1], rstd[u][:, 0:1], ACT.Exp, scale=-0.5).then_inc(sig(f"b_rstd{n}"), 1)

                def hi(u):
                    W("b_tr5", u)
                    f(xa_h[:].rearrange("p k (i u t) -> p k i u t", i=NSEQ // 2, u=2)[:, :, bass.ds(it, 1), u, :]
                      .rearrange("p k o t -> p k (o t)"),
                      ps_f(u, 3, DM).rearrange("p (k t) -> p k t", k=2), ACT.Copy).then_inc(sig("xa_hi"), 1)

                def gate(u):
                    W("b_dif", u)
                    f(sm[u][:, 10:11], sm[u][:, 9:10], ACT.Exp).then_inc(sig("b_edif"), 1)

                for s in (lambda u: rs(u, ""), lambda u: rs(u, "g", 2), lambda u: rs(u, "5"), hi, gate):
                    for u in range(2):
                        s(u)
                own_b.leave(NSEQ // 2)

            def w_high(p, count):
                act.wait_ge(sig(f"w{p}_in"), count * 32)
                f(eh[p][:, 0:2048], gu_f[p], ACT.Copy)
                f(eh[p][:, 2048:3072], dn_f[p], ACT.Copy).then_inc(sig(f"w{p}_hi"), 1)
            w_high(0, 1)
            with act.Fori(0, NE // 2) as it:
                def hidden(n):
                    for i in range(4):
                        q = n * 4 + i
                        act.wait_ge(sig("c_hid"), it * 32 + q + 1)
                        f(sil[q % 2], ps_f(0, 2 * (q % 2)), ACT.Silu).then_inc(sig("c_silu"), 1)
                        act.wait_ge(sig("c_prod"), it * 32 + q + 1)
                        if i == 0:
                            act.wait_ge(sig("c_down"), it * 8 + max(n - 1, 0))
                        f(pt_h[n % 2][:, i * TB:(i + 1) * TB], prod[q % 2], ACT.Copy).then_inc(sig("c_hh"), 1)
                    if n == 0:
                        act.wait_ge(sig("c_down"), it * 8)
                        w_high(1, it + 1)
                    if n == 5:
                        act.wait_ge(sig("c_down"), it * 8 + 4)
                        w_high(0, it + 2)

                order_c(hidden, lambda n: None)

        def vector_b(dve, own):
            tt, ts, cp, red = dve.tensor_tensor, dve.tensor_scalar, dve.tensor_copy, dve.tensor_reduce
            stt = dve.scalar_tensor_tensor
            accf = acc[:].rearrange("p h t -> p (h t)")
            own.link(tt(accf, accf, decay[:].rearrange("p h t -> p (h t)"), ALU.mult))
            mixf = mixT[:].rearrange("p h t -> p (h t)")
            own.link(stt(mixf, accf, -1.0, accf, ALU.mult, ALU.max))
            ts(mixf, mixf, 1.0, None, ALU.max).then_inc(sig("mixT"), 1)
            own_b = Own(dve, "dve_own_b", PER["dve_b"])
            link, mark = own_b.link, own_b.mark
            xs = xall[:].rearrange("p (i u) d -> p i u d", u=2)
            vs = vall[:].rearrange("p (i u) h e -> p i u (h e)", u=2)
            cws = cw[:].rearrange("p (i u) e -> p i u e", u=2)
            with dve.Fori(0, NSEQ // 2) as it:
                own_b.enter(it)
                own = own_b

                def W(name, u):
                    dve.wait_ge(sig(name), at(name, it, u))

                def S(ins, name):
                    ins.then_inc(sig(name), 1)

                def norm(u, n, x, e="b_ln"):
                    link(dve.bn_stats(bst[u][:], x))
                    apart(dve)
                    S(dve.bn_aggr(mv[u][:], bst[u][:]), f"b_var{n}")
                    W(f"b_rstd{n}", u)
                    return ts(xn[u][:], x, mv[u][:, 0:1], rstd[u][:, 0:1], ALU.subtract, ALU.mult)

                def b0(u):
                    apart(dve)
                    link(cp(xr[u][:, None, :], xs[:, bass.ds(it, 1), u, :]))
                    S(norm(u, "", xr[u][:]), "b_ln")

                def b1(u):
                    W("b_tr", u)
                    apart(dve)
                    mark(cp(big[u][:, None, 0:DM], vs[:, bass.ds(it, 1), u, :]))
                    S(cp(xT[u][:].rearrange("p k t -> p (k t)"), ps_f(u, 1, DM)), "b_xT")

                def b2(u):
                    W("b_mix", u)
                    link(norm(u, "g", ps_f(u, 0, DM)))
                    link(tt(xn[u][:], xn[u][:], rows[:, GAM, :], ALU.mult))
                    link(tt(xn[u][:], xn[u][:], rows[:, BET, :], ALU.add))
                    S(stt(af[u][:], ps_f(u, 0, DM, DM), 0.0, xn[u][:], ALU.max, ALU.mult), "b_a")

                def b3(u):
                    W("b_atr", u)
                    S(cp(aT[u][:].rearrange("p k t -> p (k t)"), ps_f(u, 1, DM)), "b_aT")

                def b4(u):
                    W("b_wo", u)
                    link(tt(xr[u][:], ps_f(u, 2, DM), xr[u][:], ALU.add))
                    apart(dve)
                    mark(cp(xs[:, bass.ds(it, 1), u, :], xr[u][:, None, :]))
                    S(norm(u, "5", xr[u][:]), "b_ln5")

                def b5(u):
                    W("xa_hi", u)
                    S(cp(xT[u][:].rearrange("p k t -> p (k t)"), ps_f(u, 3, DM)), "b_xT5")
                    v = [b[:].rearrange("p k (i u t) -> p k i u t", i=NSEQ // 2, u=2)[:, :, bass.ds(it, 1), u, :]
                         .rearrange("p k o t -> p k (o t)") for b in (xa_l, xa_h)]
                    S(tt(v[0], ps_f(u, 3, DM).rearrange("p (k t) -> p k t", k=2), v[1], ALU.subtract), "xa_lo")

                def b6(u):
                    W("b_gate", u)
                    link(cp(lg[u][:, 0, 0:NE], ps_f(u, 0, NE)))
                    apart(dve)
                    link(dve.max(sm[u][:, 0:8], lg[u][:, 0, 0:NE]))
                    apart(dve)
                    mark(dve.max_index(idx[u][:], sm[u][:, 0:8], lg[u][:, 0, 0:NE]))
                    S(tt(sm[u][:, 9:10], sm[u][:, 1:2], sm[u][:, 0:1], ALU.subtract), "b_dif")
                    own.wait()
                    link(cp(st32[u][:, 0, 0:8], idx[u][:]))
                    W("b_edif", u)
                    link(ts(sm[u][:, 11:12], sm[u][:, 10:11], 1.0, None, ALU.add))
                    link(dve.reciprocal(sm[u][:, 12:13], sm[u][:, 11:12]))
                    link(tt(sm[u][:, 13:14], sm[u][:, 12:13], sm[u][:, 10:11], ALU.mult))
                    mark(ts(st32[u][:, 1, 0:8], iota8[:], st32[u][:, 0, 0:1], sm[u][:, 12:13],
                            ALU.is_equal, ALU.mult))
                    link(ts(st32[u][:, 2, 0:8], iota8[:], st32[u][:, 0, 1:2], sm[u][:, 13:14],
                            ALU.is_equal, ALU.mult))
                    link(tt(cws[:, bass.ds(it, 1), u, :], st32[u][:, 1:2, 0:8], st32[u][:, 2:3, 0:8], ALU.add))

                for s in (b0, b1, b2, b3, b4, b5, b6):
                    for u in range(2):
                        s(u)
                print("dve_b per turn", own_b.n)
                own_b.leave(NSEQ // 2)

            def w_low(p, count):
                dve.wait_ge(sig(f"w{p}_hi"), count)
                tt(el[p][:, 0:2048], gu_f[p], eh[p][:, 0:2048], ALU.subtract)
                tt(el[p][:, 2048:3072], dn_f[p], eh[p][:, 2048:3072], ALU.subtract).then_inc(sig(f"w{p}_lo"), 1)
            w_low(0, 1)
            own_c = Own(dve, "dve_own_c", PER["dve_c"])
            cwe = cw[:].rearrange("p b (i g) -> p b i g", g=2)
            with dve.Fori(0, NE // 2) as it:
                own_c.enter(it)
                dve.wait_ge(sig("c_acc"), it * 8)
                apart(dve)
                for g in range(2):
                    own_c.mark(cp(ecw[g][:, :, None], cwe[:, :, bass.ds(it, 1), g]))
                own_c.wait()

                def hidden(n):
                    for i in range(4):
                        q = n * 4 + i
                        dve.wait_ge(sig("c_silu"), it * 32 + q + 1)
                        dve.wait_ge(sig("c_hl"), it * 32 + max(q - 1, 0))
                        tt(prod[q % 2], sil[q % 2], ps_f(0, 2 * (q % 2) + 1), ALU.mult).then_inc(sig("c_prod"), 1)
                    if n == 0:
                        w_low(1, it + 1)
                    if n == 5:
                        w_low(0, it + 2)

                def down(n):
                    p, j = n // NBLKC, n % NBLKC
                    dve.wait_ge(sig("c_down"), it * 8 + n + 1)
                    for t in range(4):
                        b = 4 * j + t
                        if n > 0 or t > 0:
                            pass
                        last = stt(xall[:, b, :], ps_f(1, 2 * (n % 2) + t // 2, DM, (t % 2) * DM),
                                   ecw[p][:, b:b + 1], xall[:, b, :], ALU.mult, ALU.add)
                        if t < 3:
                            own_c.mark(last)
                        else:
                            last.then_inc(sig("c_acc"), 1)

                order_c(hidden, down)
                print("dve_c per turn", own_c.n)
                own_c.leave(NE // 2)

        def pool_b(pool):
            with pool.Fori(0, NE // 2) as it:
                def hidden(n):
                    for i in range(4):
                        q = n * 4 + i
                        pool.wait_ge(sig("c_hh"), it * 32 + q + 1)
                        c = slice(i * TB, (i + 1) * TB)
                        pool.tensor_tensor(pt_l[n % 2][:, c], prod[q % 2], pt_h[n % 2][:, c],
                                           ALU.subtract).then_inc(sig("c_hl"), 1)
                order_c(hidden, lambda n: None)

        def sync_b(sp):
            def load(p, e):
                sp.dma_start(gu_f[p], A["gu"][e]).then_inc(sig(f"w{p}_in"), 16)
                sp.dma_start(dn_f[p], A["dn"][e]).then_inc(sig(f"w{p}_in"), 16)
            sp.wait_ge(sig("b_mix"), NSEQ)
            load(0, 0)
            load(1, 1)
            for it in range(NE // 2):
                if it == 0:
                    sp.wait_ge(sig("w0_lo"), 1)
                    load(0, 2)
                if it + 1 < NE // 2:
                    sp.wait_ge(sig("w1_lo"), it + 1)
                    load(1, 2 * it + 3)
                    sp.wait_ge(sig("w0_lo"), it + 2)
                    load(0, (2 * it + 4) % NE)
            sp.wait_ge(sig("c_acc"), 8 * NE // 2)
            sp.dma_start(out.rearrange("b t d -> t b d"), xall[:]).then_inc(sig("stored"), 16)
            sp.wait_ge(sig("stored"), 16)

        block = ctx.enter_context(nc.Block())

        @block.sync
        def _(sp):
            def load(dst, src, name="consts"):
                sp.dma_start(dst, src).then_inc(sig(name), 16)
            for u in range(2):
                sp.dma_start(xin[u][:], A["x"][u]).then_inc(sig(f"x_in{u}"), 16)
                sp.dma_start(cin[u][:], A["ctx"][u]).then_inc(sig(f"x_in{u}"), 16)
            load(big[0][:], A["wq"][:, 0, :], "w_in")
            load(big[1][:], A["wq"][:, 1, :], "w_in")
            load(kf[0][:], A["wk"], "w_in")
            load(kf[1][:], A["wv"], "w_in")
            load(ptf[0][:], A["wo"][:, 0:8, :].rearrange("p k n -> p (k n)"), "w_in")
            load(ptf[1][:], A["wo"][:, 8:16, :].rearrange("p k n -> p (k n)"), "w_in")
            consts = [(ident, "ident"), (cosI, "cosI"), (sinI, "sinI"), (mask, "mask"), (sinkT, "sinkT"),
                      (decay, "decay"), (iota8, "iota8"), (bq, "bq"), (bk, "bk"), (wx, "wx"), (rw, "rw"),
                      (ebias, "ebias"), (wm, "wm"), (wh, "wh"), (wgo, "wgo"), (gw, "gw")]
            for t, n in consts:
                load(t[:], A[n])
            load(mem[0:64, :], A["mem"])
            load(mem[64:128, :], A["mem"])
            for i in range(9):
                load(rows[:, i, :], A["rows"][i:i + 1, :].to_broadcast([P, DM]))
            load(bv[:], A["bv"].to_broadcast([P, 512]))
            load(rb[:], A["rb"].to_broadcast([P, E0]))
            load(memw[:, 0:1], A["memw"].to_broadcast([P, 1]))
            assert len(consts) + 2 + 9 + 3 == n_consts
            xs = A["x"].rearrange("(i u) p d -> i u p d", u=2)
            cs = A["ctx"].rearrange("(i u) p d -> i u p d", u=2)
            with sp.Fori(0, NSEQ // 2 - 1) as it:
                for u in range(2):
                    sp.wait_ge(sig("ln0"), at("ln0", it, u))
                    sp.wait_ge(sig("tr0"), at("tr0", it, u))
                    nx = bass.ds(it + 1, 1)
                    sp.dma_start(xin[u][:], xs[nx, u].rearrange("o p d -> (o p) d")).then_inc(sig(f"x_in{u}"), 16)
                    sp.dma_start(cin[u][:], cs[nx, u].rearrange("o p d -> (o p) d")).then_inc(sig(f"x_in{u}"), 16)
            sync_b(sp)

        @block.tensor
        def _(pe):
            def mm(o, l, r, start, stop):
                return pe.matmul(o, l, r, start=start, stop=stop)

            def mm3(o, lh, ll, rh, rl, start=True, stop=True):
                mm(o, lh, rh, start, False)
                mm(o, ll, rh, False, False)
                return mm(o, lh, rl, False, stop)

            pe.wait_ge(sig("consts"), 16 * n_consts)
            pe.wait_ge(sig("w_ready"), 3)
            with pe.Fori(0, NSEQ // 2) as it:
                def W(name, u):
                    pe.wait_ge(sig(name), at(name, it, u))

                def transposes_x(u, name, bank, src, ready):
                    W(ready, u)
                    for k in range(KT_):
                        m = pe.transpose(ps_f(u, bank, P, k * P), src[u][:, k * P:(k + 1) * P], ident[:])
                    m.then_inc(sig(name), 1)

                def a0(u):
                    W("ln0", u)
                    pe.wait_ge(sig(f"x_in{u}"), it * 32 + 32)
                    for k in range(KT_):
                        pe.transpose(ps_f(u, 0, P, k * P), xn[u][:, k * P:(k + 1) * P], ident[:])
                        m = pe.transpose(ps_f(u, 0, P, 256 + k * P), cin[u][:, k * P:(k + 1) * P], ident[:])
                    m.then_inc(sig("tr0"), 1)

                def a1(u):
                    W("xT0", u)
                    for t in range(4):
                        o = ps_f(u, 1, P, t * P)
                        for k in range(KT_):
                            c = slice(t * P, (t + 1) * P)
                            mm3(o, wk_h[:, k, c], wk_l[:, k, c], xT_h[u][:, k, 32:160], xT_l[u][:, k, 32:160],
                                k == 0, k == KT_ - 1)
                    for p in range(2):
                        for k in range(KT_):
                            c = slice(k * 256 + p * P, k * 256 + (p + 1) * P)
                            m = mm3(ps_f(u, 2 + p), q_h[u][:, c], q_l[u][:, c], wv_h[:, k, :], wv_l[:, k, :],
                                    k == 0, k == KT_ - 1)
                    m.then_inc(sig("kv0"), 1)

                def a2(u):
                    W("kv0_out", u)
                    for t in range(16):
                        o = ps_f(u, t // 4).rearrange("p (i g r) -> p g i r", i=NBLK, g=G0)[:, t % 4]
                        for k in range(KT_):
                            c = slice(t * P, (t + 1) * P)
                            m = mm3(o, wq_h[:, k, c], wq_l[:, k, c], xT_h[u][:, k, 32:160], xT_l[u][:, k, 32:160],
                                    k == 0, k == KT_ - 1)
                    m.then_inc(sig("q0"), 1)

                def a3(u):
                    W("q0_out", u)
                    qv = [b[u].rearrange("p (a h i m) -> p a h i m", a=2, h=2, i=NBLK) for b in (q_h, q_l)]
                    for hf in range(2):
                        for i in range(NBLK):
                            for kvl in range(4):
                                r = slice(32 * kvl, 32 * kvl + 32)
                                o = ps_f(u, kvl, 64, hf * 256 + i * 64)
                                for ab in range(2):
                                    q1, q2 = [v[r, ab, hf, i, :] for v in qv]
                                    k1, k2 = [b[u][r, ab * 2 + hf, 32 * i:32 * i + 64] for b in (k_h, k_l)]
                                    m = mm3(o, q1, q2, k1, k2, ab == 0, ab == 1)
                    m.then_inc(sig("s0"), 1)

                def p_transposes(u, name, ready):
                    W(ready, u)
                    for part, b in enumerate((q_h, q_l)):
                        for j in range(16):
                            m = pe.transpose(psb(u, part * 2 + j // 8)[:, (j % 8) * P:(j % 8 + 1) * P],
                                             b[u][:, j * P:(j + 1) * P], identb[:])
                    m.then_inc(sig(name), 1)

                def a5(u):
                    W("pt0", u)
                    W("v0", u)
                    apart(pe)
                    for kvl in range(4):
                        for hf in range(2):
                            kvp, par = hf * 2 + kvl // 2, kvl % 2
                            kv = hf * 4 + kvl
                            for i in range(NBLK):
                                ip, i2 = i // 2, i % 2
                                blk = (kvl * 2 + hf) * 2 + ip
                                r = slice(64 * i2, 64 * i2 + 64)
                                o = PS[u][64 * par:64 * par + 64, i, kvp * P:(kvp + 1) * P]
                                c = slice(ip * 512 + kv * 64, ip * 512 + kv * 64 + 64)
                                m = mm3(o, v_h[u][r, c], v_l[u][r, c], pt_h[u][r, blk * P:(blk + 1) * P],
                                        pt_l[u][r, blk * P:(blk + 1) * P])
                    m.then_inc(sig("pv0"), 1)

                def a6(u):
                    W("o0", u)
                    for t in range(16):
                        c = slice(t * P, (t + 1) * P)
                        m = mm3(ps_f(u, 0, DM), q_h[u][:, c], q_l[u][:, c], wo_h[:, t, :], wo_l[:, t, :],
                                t == 0, t == 15)
                    m.then_inc(sig("wo0"), 1)

                def a7(u):
                    W("xT1", u)
                    for i, src in enumerate((xT, cT, cT)):
                        o = ps_f(u, i // 2, DM, (i % 2) * DM)
                        for k in range(KT_):
                            m = mm(o, src[u][:, k, :], wx[:, i, k, :], k == 0, k == KT_ - 1)
                    m.then_inc(sig("qkv1"), 1)

                def pack_transposes(u, name, ready, nk):
                    W(ready, u)
                    for j in range(8):
                        pe.transpose(psb(u, 0)[:, j * P:(j + 1) * P], qp[u][:, j * P:(j + 1) * P], identb[:])
                    for j in range(nk):
                        m = pe.transpose(psb(u, 1)[:, j * P:(j + 1) * P], kp[u][:, j * P:(j + 1) * P], identb[:])
                    return m

                def a9(u):
                    W("qkT1", u)
                    for h in range(NHX):
                        r = slice(64 * (h % 2), 64 * (h % 2) + 64)
                        c = slice((h // 2) * P, (h // 2 + 1) * P)
                        j = place(h, 2)
                        m = mm(ps_f(u, j // 4, P, (j % 4) * P), pt_h[u][r, c], pt_l[u][r, c], True, True)
                    m.then_inc(sig("s1"), 1)

                def pv(u, name, ready, tiles, nkh, dv):
                    W(ready, u)
                    for j in range(16):
                        c = slice(j * P, (j + 1) * P)
                        h = head_at(j, tiles)
                        w = slice((h % nkh) * dv, (h % nkh + 1) * dv)
                        m = mm3(ps_f(u, 0, dv, h * 32), pt_h[u][:, c], pt_l[u][:, c], vp_h[u][:, w], vp_l[u][:, w])
                    m.then_inc(sig(name), 1)

                def proj_x(u):
                    W("aT1", u)
                    for k in range(KT_):
                        m = mm(ps_f(u, 0, DM), aT[u][:, k, :], wx[:, 3, k, :], k == 0, k == KT_ - 1)
                    m.then_inc(sig("wo1"), 1)

                def a15(u):
                    W("xT2", u)
                    for k in range(KT_):
                        m = mm(ps_f(u, 0, E0), xT[u][:, k, :], rw[:, k, :], k == 0, k == KT_ - 1)
                    m.then_inc(sig("rl"), 1)

                def a16(u):
                    W("rw", u)
                    apart(pe)
                    pe.transpose(PS[u][0:E0, 1, 0:P], lg[u][:, 0, :], ident[:]).then_inc(sig("rwT"), 1)

                def a17(u):
                    W("rwT_out", u)
                    mm(ps_f(u, 0, DM), wt[u][0:E0, :], ebias[:], True, True).then_inc(sig("eb"), 1)

                def a19(u):
                    W("xT3", u)
                    for k in range(KT_):
                        m = mm(ps_f(u, 0, 384), xT[u][:, k, :], wm[:, k, :], k == 0, k == KT_ - 1)
                    m.then_inc(sig("qkv3"), 1)

                def a20(u):
                    pack_transposes(u, "", "pk3", 2)
                    for k in range(2):
                        m = pe.transpose(ps_f(u, 2, P, k * P), af[u][:, k * P:(k + 1) * P], ident[:])
                    m.then_inc(sig("tr3b"), 1)

                def a20m(u):
                    W("qkT3", u)
                    for qi in range(NQM):
                        r = slice(64 * (qi % 2), 64 * (qi % 2) + 64)
                        m = mm(ps_f(u, 2 + qi % 2, 65, (qi // 2) * P), aT[u][r, qi // 2, :], mem[r, :], True, True)
                    m.then_inc(sig("mem"), 1)

                def a21(u, half):
                    W("mem_out" if half == 0 else "pv3a_out", u)
                    for hh in range(half * 16, half * 16 + 16):
                        j = place(hh, 4)
                        h = hh % NHM
                        r = slice(32 * (hh % 4), 32 * (hh % 4) + 32)
                        m = mm(ps_f(u, j // 4, P, (j % 4) * P), qp[u][r, (hh // 4) * P:(hh // 4 + 1) * P],
                               kp[u][r, (h // 4) * P:(h // 4 + 1) * P], True, True)
                    m.then_inc(sig("s3" + "ab"[half]), 1)

                def a31(u):
                    W("xT4", u)
                    for h in range(2):
                        mm(ps_f(u, 0, P, h * P), wh[:, h, :], xT[u][:, h, :], True, True)
                        mm(ps_f(u, 0, P, 256 + h * P), wh[:, h, :], cT[u][:, h, :], True, True)
                        m = mm(ps_f(u, 1, P, 256 + h * P), cT[u][:, h, :], wh[:, h, :], True, True)
                    m.then_inc(sig("mixqkv"), 1)

                def a32(u):
                    W("mixqkv_out", u)
                    for h in range(2):
                        m = mm(ps_f(u, 2, P, h * P), big[u][:, 256 + h * P:256 + (h + 1) * P],
                               big[u][:, h * P:(h + 1) * P], True, True)
                    m.then_inc(sig("mixs"), 1)

                stages = [a0, a1, a2, a3, lambda u: p_transposes(u, "pT0", "p0"), a5, a6,
                          lambda u: transposes_x(u, "tr1", 1, xn, "ln1"), a7,
                          lambda u: pack_transposes(u, "", "pk1", 8).then_inc(sig("qkT1p"), 1), a9,
                          lambda u: p_transposes(u, "pT1", "p1"),
                          lambda u: pv(u, "pv1", "pt1", 2, NHX, DHX + 1),
                          lambda u: transposes_x(u, "atr1", 1, af, "a1"), proj_x,
                          lambda u: transposes_x(u, "tr2", 1, xn, "ln2"), a15, a16, a17,
                          lambda u: transposes_x(u, "tr3", 1, xn, "ln3"), a19, a20, a20m,
                          lambda u: a21(u, 0), lambda u: p_transposes(u, "pT3a", "p3a"),
                          lambda u: pv(u, "pv3a", "pt3a", 4, NHM, DHM + 1),
                          lambda u: a21(u, 1), lambda u: p_transposes(u, "pT3b", "p3b"),
                          lambda u: pv(u, "pv3b", "pt3b", 4, NHM, DHM + 1),
                          lambda u: transposes_x(u, "tr4", 1, xn, "ln4"), a31, a32]
                for s in stages:
                    for u in range(2):
                        s(u)
            tensor_b(pe, mm, mm3)

        @block.scalar
        def _(act):
            own = Own(act, "act_own", PER["act"])
            f = act.activation
            act.wait_ge(sig("w_in"), 6 * 16)
            for n in range(2):
                f(wq_h[:, n, :], big[n][:], ACT.Copy)
                f(wo_h[:, 8 * n:8 * n + 8, :].rearrange("p k n -> p (k n)"), ptf[n][:], ACT.Copy)
            f(wk_h[:], kf[0][:], ACT.Copy)
            f(wv_h[:], kf[1][:], ACT.Copy).then_inc(sig("w_high"), 1)
            act.wait_ge(sig("consts"), 16 * n_consts)
            act.wait_ge(sig("w_ready"), 2)
            f(identb[:], ident[:], ACT.Copy).then_inc(sig("w_ready"), 1)
            f(memw[:, 1:2], memw[:, 0:1], ACT.Exp, scale=-1.0).then_inc(sig("memw"), 1)
            with act.Fori(0, NSEQ // 2) as it:
                own.enter(it)

                def W(name, u):
                    act.wait_ge(sig(name), at(name, it, u))

                def rs(u, n, e=0, scale=1.0, src=None):
                    W(f"var{n}", u)
                    own.link(f(rstd[u][:, 0:1], mv[u][:, 1:2] if src is None else src, ACT.Ln,
                               bias=eps[:, e:e + 1], scale=scale))
                    f(rstd[u][:, 0:1], rstd[u][:, 0:1], ACT.Exp, scale=-0.5).then_inc(sig(f"rstd{n}"), 1)

                def a0(u):
                    W("tr0", u)
                    f(xT_h[u][:, :, 32:160], ps_f(u, 0, 256).rearrange("p (k t) -> p k t", k=2), ACT.Copy)\
                        .then_inc(sig("xT0h"), 1)
                    f(cT[u][:].rearrange("p k t -> p (k t)"), ps_f(u, 0, 256, 256), ACT.Copy)\
                        .then_inc(sig("cT0"), 1)

                def a1(u):
                    W("k0r", u)
                    f(k_h[u][:, :, 32:160], kf[u][:, 0, :].rearrange("p (a t) -> p a t", a=4), ACT.Copy)\
                        .then_inc(sig("k0h"), 1)
                    W("v0f", u)
                    f(v_h[u][:], big[u][:, 0:1024], ACT.Copy).then_inc(sig("v0h"), 1)

                def a2(u):
                    W("q0r", u)
                    f(q_h[u], big[u][:], ACT.Copy).then_inc(sig("q0h"), 1)

                def a3(u):
                    W("s0m", u)
                    own.link(f(big[u][:], big[u][:], ACT.Exp))
                    f(st32[u][:, 1, :], st32[u][:, 1, :], ACT.Exp).then_inc(sig("e0"), 1)
                    W("p0n", u)
                    f(q_h[u], big[u][:], ACT.Copy).then_inc(sig("p0h"), 1)

                def pt(u, tr, nm):
                    W(tr, u)
                    f(pt_h[u][:, 0:1024], psb(u, 0), ACT.Copy)
                    f(pt_h[u][:, 1024:2048], psb(u, 1), ACT.Copy).then_inc(sig(nm), 1)

                def a5(u):
                    W("pv0", u)
                    f(by_token(q_h[u]), by_block(u), ACT.Copy).then_inc(sig("o0h"), 1)

                def rms(u, n, src, e):
                    W(f"{n}f", u)
                    own.link(f(af2[u], src, ACT.Square, accum_out=rstd[u][:, 1:2]))
                    own.link(f(rstd[u][:, 0:1], rstd[u][:, 1:2], ACT.Ln, bias=eps[:, e:e + 1], scale=1.0 / DM))
                    f(rstd[u][:, 0:1], rstd[u][:, 0:1], ACT.Exp, scale=-0.5).then_inc(sig(f"{n}rstd"), 1)

                def a7(u):
                    rms(u, "q1", qf[u], 1)
                    W("q1n", u)
                    rms(u, "k1", kvf[u][:, 0, :], 1)

                def qkT(u, tr, nm, nk):
                    W(tr, u)
                    f((pt_h if nk == 8 else qp)[u][:, 0:1024], psb(u, 0), ACT.Copy).then_inc(sig(nm), 1)

                def soft(u, n, scale):
                    W(f"s{n}m", u)
                    own.link(f(big[u][:], big[u][:], ACT.Exp, scale=scale))
                    f(q_h[u], big[u][:], ACT.Copy).then_inc(sig(f"p{n}h"), 1)

                def a15(u):
                    W("rlm", u)
                    f(lg[u][:, 0, :], lg[u][:, 0, :], ACT.Exp, accum_out=sm[u][:, 8:9]).then_inc(sig("rle"), 1)

                def a19(u):
                    W("sgm", u)
                    f(af2[u], af2[u], ACT.Exp).then_inc(sig("sge"), 1)

                def a31(u):
                    W("mixqkv", u)
                    f(big[u][:, 0:512], ps_f(u, 0), ACT.Copy).then_inc(sig("mixqkv_out"), 1)

                stages = [lambda u: rs(u, 0), a0, a1, a2, a3, lambda u: pt(u, "pT0", "pt0h"), a5,
                          lambda u: rs(u, 1), a7, lambda u: qkT(u, "qkT1p", "qT1", 8),
                          lambda u: soft(u, "1", float(DHX) ** -0.5), lambda u: pt(u, "pT1", "pt1h"),
                          lambda u: rs(u, 2), a15, lambda u: rs(u, 3), a19,
                          lambda u: qkT(u, "tr3b", "qT3", 2),
                          lambda u: soft(u, "3a", float(DHM) ** -0.5), lambda u: pt(u, "pT3a", "pt3ah"),
                          lambda u: soft(u, "3b", float(DHM) ** -0.5), lambda u: pt(u, "pT3b", "pt3bh"),
                          lambda u: rs(u, 4), a31]
                for s in stages:
                    for u in range(2):
                        s(u)
                own.leave(NSEQ // 2)
            scalar_b(act, own, f)

        @block.gpsimd
        def _(pool):
            for n in range(2):
                for b in (xT_h, xT_l, k_h, k_l):
                    pool.memset(b[n][:], 0.0).then_inc(sig("zeros"), 1)
            with pool.Fori(0, NSEQ // 2) as it:
                def rope(u, nm, srcb, dst, shape, sin):
                    pool.wait_ge(sig(nm + "b"), at(nm + "b", it, u))
                    w = srcb.shape[1] // 2
                    A_, B_, dA, dB = [shape(b) for b in (srcb[:, 0:w], srcb[:, w:2 * w], dst[:, 0:w], dst[:, w:2 * w])]
                    pool.tensor_tensor(dA, B_, sin, ALU.mult)
                    pool.tensor_tensor(dB, A_, sin, ALU.mult).then_inc(sig(nm + "sin"), 1)
                pool.wait_ge(sig("consts"), 16 * n_consts)
                for u in range(2):
                    rope(u, "k0", kf[u][:, 0, :], kf[u][:, 1, :],
                         lambda b: b.rearrange("p (h i r) -> p h i r", h=2, i=NBLK),
                         k_table(sinI, 2))
                for u in range(2):
                    rope(u, "q0", big[u][:], ptf[u][:],
                         lambda b: b.rearrange("p (h m) -> p h m", h=2), q_table(sinI, 2))
            pool_b(pool)

        @block.vector
        def _(dve):
            own = Own(dve, "dve_own", PER["dve"])
            link, mark = own.link, own.mark
            tt, ts, cp, red = dve.tensor_tensor, dve.tensor_scalar, dve.tensor_copy, dve.tensor_reduce
            stt = dve.scalar_tensor_tensor
            for i, e in enumerate((EPS_LN, EPS_RMS, EPS_GN, 0.0)):
                mark(dve.memset(eps[:, i:i + 1], e))
            mark(dve.memset(acc[:], 0.0))
            for u in range(2):
                mark(dve.memset(vp_l[u][:], 0.0))
                mark(dve.memset(vp_h[u][:], 1.0))
            dve.wait_ge(sig("w_high"), 1)
            for n in range(2):
                mark(tt(wq_l[:, n, :], big[n][:], wq_h[:, n, :], ALU.subtract))
                c = slice(8 * n, 8 * n + 8)
                mark(tt(wo_l[:, c, :].rearrange("p k n -> p (k n)"), ptf[n][:],
                        wo_h[:, c, :].rearrange("p k n -> p (k n)"), ALU.subtract))
            mark(tt(wk_l[:], kf[0][:], wk_h[:], ALU.subtract))
            link(tt(wv_l[:], kf[1][:], wv_h[:], ALU.subtract))
            dve.wait_ge(sig("zeros"), 8)
            dve.memset(sm[0][:], 0.0).then_inc(sig("w_ready"), 1)
            dve.wait_ge(sig("consts"), 16 * n_consts)
            dve.memset(sm[1][:], 0.0).then_inc(sig("w_ready"), 1)
            dve.wait_ge(sig("w_ready"), 3)
            dve.wait_ge(sig("memw"), 1)
            link(ts(memw[:, 2:3], memw[:, 1:2], 1.0, None, ALU.add))
            link(dve.reciprocal(memw[:, 2:3], memw[:, 2:3]))
            link(ts(memw[:, 3:4], memw[:, 2:3], -1.0, 1.0, ALU.mult, ALU.add))

            with dve.Fori(0, NSEQ // 2) as it:
                own.enter(it)

                def W(name, u):
                    dve.wait_ge(sig(name), at(name, it, u))

                def S(ins, name):
                    ins.then_inc(sig(name), 1)

                def norm(u, n, x):
                    link(dve.bn_stats(bst[u][:], x))
                    apart(dve)
                    S(dve.bn_aggr(mv[u][:], bst[u][:]), f"var{n}")
                    W(f"rstd{n}", u)
                    S(ts(xn[u][:], x, mv[u][:, 0:1], rstd[u][:, 0:1], ALU.subtract, ALU.mult), f"ln{n}")

                def l0(u):
                    dve.wait_ge(sig(f"x_in{u}"), it * 32 + 32)
                    link(tt(xr[u][:], xin[u][:], rows[:, BO, :], ALU.add))
                    norm(u, 0, xin[u][:])

                def a0(u):
                    W("tr0", u)
                    W("xT0h", u)
                    W("cT0", u)
                    link(tt(xT_l[u][:, :, 32:160], ps_f(u, 0, 256).rearrange("p (k t) -> p k t", k=2),
                            xT_h[u][:, :, 32:160], ALU.subtract))
                    for d, b in ((q_h, xT_h), (q_l, xT_l)):
                        v = b[u][:]
                        last = cp(d[u][:, 0:512].rearrange("p (k i c) -> p k i c", k=KT_, i=NBLK),
                                  bass.AP(v.tensor, v.offset, [v.ap[0], [160, KT_], [WIN, NBLK], [1, 2 * WIN]]))
                        if b is xT_h:
                            mark(last)
                    S(last, "xT0")

                def a1(u):
                    W("kv0", u)
                    kps = ps_f(u, 1).rearrange("p (a t) -> p a t", a=4)
                    kb = kf[u][:, 0, :]
                    kb4 = kb.rearrange("p (a t) -> p a t", a=4)
                    S(tt(kb4, kps, bk[:, :, None].to_broadcast([P, 4, P]), ALU.add), "k0b")
                    mark(tt(big[u][:, 0:512], ps_f(u, 2), bv[:], ALU.add))
                    S(tt(big[u][:, 512:1024], ps_f(u, 3), bv[:], ALU.add), "v0f")
                    W("k0b", u)
                    W("k0sin", u)
                    kb5 = kb.rearrange("p (a i r) -> p a i r", a=4, i=NBLK)
                    link(tt(kb5, kb5, k_table(cosI, 4), ALU.mult))
                    mark(tt(kb[:, 0:256], kb[:, 0:256], kf[u][:, 1, 0:256], ALU.subtract))
                    S(tt(kb[:, 256:512], kb[:, 256:512], kf[u][:, 1, 256:512], ALU.add), "k0r")
                    W("v0h", u)
                    S(tt(v_l[u][:], big[u][:, 0:1024], v_h[u][:], ALU.subtract), "v0")
                    W("k0h", u)
                    S(tt(k_l[u][:, :, 32:160], kf[u][:, 0, :].rearrange("p (a t) -> p a t", a=4),
                         k_h[u][:, :, 32:160], ALU.subtract), "kv0_out")

                def a2(u):
                    W("q0", u)
                    W("v0", u)
                    for ab in range(4):
                        last = tt(big[u][:, ab * 512:(ab + 1) * 512].rearrange("p (i m) -> p i m", i=NBLK),
                                  ps_f(u, ab).rearrange("p (i m) -> p i m", i=NBLK),
                                  bq[:, ab:ab + 1, :].to_broadcast([P, NBLK, P]), ALU.add)
                        if ab < 3:
                            mark(last)
                    S(last, "q0b")
                    W("q0b", u)
                    W("q0sin", u)
                    b4 = big[u][:].rearrange("p (a m) -> p a m", a=4)
                    link(tt(b4, b4, q_table(cosI, 4), ALU.mult))
                    mark(tt(big[u][:, 0:1024], big[u][:, 0:1024], ptf[u][:, 0:1024], ALU.subtract))
                    S(tt(big[u][:, 1024:2048], big[u][:, 1024:2048], ptf[u][:, 1024:2048], ALU.add), "q0r")
                    W("q0h", u)
                    S(tt(q_l[u], big[u][:], q_h[u], ALU.subtract), "q0_out")

                def a3(u):
                    W("s0", u)
                    b8 = big[u][:].rearrange("p (a t) -> p a t", a=8)
                    link(stt(b8, ps_all[u].rearrange("p (a t) -> p a t", a=8), SCALE0,
                             mask[:, None, :].to_broadcast([P, 8, 256]), ALU.mult, ALU.add))
                    b32 = big[u][:].rearrange("p (a t) -> p a t", a=32)
                    link(red(st32[u][:, 0, :], b32, AX.X, ALU.max))
                    link(tt(st32[u][:, 0, :], st32[u][:, 0, :], sinkT[:], ALU.max))
                    link(tt(st32[u][:, 1, :], sinkT[:], st32[u][:, 0, :], ALU.subtract))
                    S(tt(b32, b32, st32[u][:, 0, :, None].to_broadcast([P, 32, 64]), ALU.subtract), "s0m")
                    W("e0", u)
                    link(red(st32[u][:, 2, :], b32, AX.X, ALU.add))
                    link(tt(st32[u][:, 2, :], st32[u][:, 2, :], st32[u][:, 1, :], ALU.add))
                    link(dve.reciprocal(st32[u][:, 2, :], st32[u][:, 2, :]))
                    S(tt(b32, b32, st32[u][:, 2, :, None].to_broadcast([P, 32, 64]), ALU.mult), "p0n")
                    W("p0h", u)
                    S(tt(q_l[u], big[u][:], q_h[u], ALU.subtract), "p0")

                def pt(u, tr, nm):
                    W(tr, u)
                    mark(cp(pt_l[u][:, 0:1024], psb(u, 2)))
                    W(nm + "h", u)
                    S(cp(pt_l[u][:, 1024:2048], psb(u, 3)), nm)

                def a5(u):
                    W("o0h", u)
                    S(tt(by_token(q_l[u]), by_block(u), by_token(q_h[u]), ALU.subtract), "o0")

                def a6(u):
                    W("wo0", u)
                    link(tt(xr[u][:], ps_f(u, 0, DM), xr[u][:], ALU.add))
                    norm(u, 1, xr[u][:])

                def xTn(u, n):
                    W(f"tr{n}", u)
                    S(cp(xT[u][:].rearrange("p k t -> p (k t)"), ps_f(u, 1, DM)), f"xT{n}")

                def pack(u, dst, srcf, nh, dh, hi2, done=None):
                    d = dst.rearrange("p (h c d) -> p h c d", c=4, d=dh)
                    s = srcf.rearrange("p (h d) -> p h d", d=dh)
                    for a_ in range(2):
                        ch = 2 * a_ if hi2 == 2 else a_
                        mark(cp(d[:, :, ch, :], s))
                    own.wait()
                    for a_ in range(2):
                        cl = 2 * a_ + 1 if hi2 == 2 else 2 + a_
                        last = tt(d[:, :, cl, :], s, d[:, :, 0, :], ALU.subtract)
                        if a_ == 0 or done is None:
                            mark(last)
                        else:
                            S(last, done)

                def packv(u, srcf, nh, dh):
                    w = nh * (dh + 1)
                    vh = vp_h[u][:, 0:w].rearrange("p (h d) -> p h d", d=dh + 1)
                    vl = vp_l[u][:, 0:w].rearrange("p (h d) -> p h d", d=dh + 1)
                    s = srcf.rearrange("p (h d) -> p h d", d=dh)
                    mark(dve.memset(vh[:, :, dh:dh + 1], 1.0))
                    mark(dve.memset(vl[:, :, dh:dh + 1], 0.0))
                    link(cp(vh[:, :, 0:dh], s))
                    link(tt(vl[:, :, 0:dh], s, vh[:, :, 0:dh], ALU.subtract))

                def a7(u):
                    W("qkv1", u)
                    link(tt(xr[u][:], xr[u][:], rows[:, OB, :], ALU.add))
                    S(tt(qf[u], ps_f(u, 0, DM), rows[:, QB, :], ALU.add), "q1f")
                    mark(tt(kvf[u][:, 1, :], ps_f(u, 1, DM), rows[:, VB, :], ALU.add))
                    own.wait()
                    packv(u, kvf[u][:, 1, :], NHX, DHX)
                    W("q1rstd", u)
                    S(stt(qf[u], qf[u], rstd[u][:, 0:1], rows[:, NQ, :], ALU.mult, ALU.mult), "q1n")
                    S(tt(kvf[u][:, 0, :], ps_f(u, 0, DM, DM), rows[:, KB, :], ALU.add), "k1f")
                    W("q1n", u)
                    pack(u, qp[u][:], qf[u], NHX, DHX, 2)
                    W("k1rstd", u)
                    link(stt(kvf[u][:, 0, :], kvf[u][:, 0, :], rstd[u][:, 0:1], rows[:, NK_, :], ALU.mult, ALU.mult))
                    pack(u, kp[u][:], kvf[u][:, 0, :], NHX, DHX, 1, "pk1")

                def a8(u):
                    W("qkT1p", u)
                    W("qT1", u)
                    S(cp(pt_l[u][:, 0:1024], psb(u, 1)), "qkT1")

                def soft(u, n):
                    W(f"s{n}", u)
                    p16 = ps_all[u].rearrange("p (a t) -> p a t", a=16)
                    b16 = big[u][:].rearrange("p (a t) -> p a t", a=16)
                    link(red(st32[u][:, 0, 0:16], p16, AX.X, ALU.max))
                    S(tt(b16, p16, st32[u][:, 0, 0:16, None].to_broadcast([P, 16, P]), ALU.subtract), f"s{n}m")
                    W(f"p{n}h", u)
                    S(tt(q_l[u], big[u][:], q_h[u], ALU.subtract), f"p{n}")

                def heads_out(u, n, dst, dh):
                    W(f"pv{n}", u)
                    o = ps_f(u, 0).rearrange("p (h d) -> p h d", d=32)
                    r = st32[u][:, 1, 0:16]
                    link(dve.reciprocal(r[:, :, None], o[:, :, dh:dh + 1]))
                    return tt(dst.rearrange("p (h d) -> p h d", d=dh), o[:, :, 0:dh],
                              r[:, :, None].to_broadcast([P, 16, dh]), ALU.mult)

                def a11(u):
                    S(heads_out(u, "1", af[u][:], DHX), "a1")

                def a12(u):
                    W("atr1", u)
                    S(cp(aT[u][:].rearrange("p k t -> p (k t)"), ps_f(u, 1, DM)), "aT1")

                def a13(u):
                    W("wo1", u)
                    link(tt(xr[u][:], ps_f(u, 0, DM), xr[u][:], ALU.add))
                    norm(u, 2, xr[u][:])

                def a15(u):
                    W("rl", u)
                    l0_, l1_ = lg[u][:, 0, :], lg[u][:, 1, :]
                    link(tt(l0_, ps_f(u, 0, E0), rb[:], ALU.add))
                    link(red(sm[u][:, 9:10], l0_, AX.X, ALU.max))
                    S(ts(l0_, l0_, sm[u][:, 9:10], None, ALU.subtract), "rlm")
                    W("rle", u)
                    link(dve.reciprocal(sm[u][:, 8:9], sm[u][:, 8:9]))
                    link(ts(l0_, l0_, sm[u][:, 8:9], None, ALU.mult))
                    apart(dve)
                    link(dve.max(sm[u][:, 0:8], l0_))
                    apart(dve)
                    link(dve.match_replace(l1_, sm[u][:, 0:8], l0_, 0.0))
                    link(red(sm[u][:, 9:10], sm[u][:, 0:8], AX.X, ALU.add))
                    S(tt(l0_, l0_, l1_, ALU.subtract), "rw")

                def a16(u):
                    W("rwT", u)
                    S(cp(wt[u][0:E0, :], PS[u][0:E0, 1, 0:P]), "rwT_out")

                def a17(u):
                    W("eb", u)
                    link(tt(xr[u][:], ps_f(u, 0, DM), xr[u][:], ALU.add))
                    link(stt(xr[u][:], xn[u][:], sm[u][:, 9:10], xr[u][:], ALU.mult, ALU.add))
                    norm(u, 3, xr[u][:])

                def a19(u):
                    W("qkv3", u)
                    mark(cp(qf[u], ps_f(u, 0, DM)))
                    mark(cp(kvf[u][:, :, 0:64], ps_f(u, 0, 128, DM).rearrange("p (a d) -> p a d", a=2)))
                    own.wait()
                    S(ts(af2[u], qf[u], 0.0, None, ALU.min), "sgm")
                    packv(u, kvf[u][:, 1, 0:64], NHM, DHM)
                    pack(u, qp[u][:], qf[u], 32, DHM, 2)
                    pack(u, kp[u][:, 0:256], kvf[u][:, 0, 0:64], NHM, DHM, 1)
                    link(ts(af[u][:], qf[u], 0.0, -1.0, ALU.max, ALU.add))
                    W("sge", u)
                    own.wait()
                    S(tt(af[u][:], af[u][:], af2[u], ALU.add), "pk3")

                def a20(u):
                    W("tr3b", u)
                    mark(cp(kp[u][:, 0:256], psb(u, 1)[:, 0:256]))
                    W("qT3", u)
                    S(cp(aT[u][:].rearrange("p k t -> p (k t)"), ps_f(u, 2, DM)), "qkT3")

                def a20m(u):
                    W("mem", u)
                    m4 = PS[u][:, 2:4, 0:256].rearrange("p b (s d) -> p s b d", s=2)
                    den = sm[u][:, 8:12].rearrange("p (s b) -> p s b", s=2)[:, :, :, None]
                    link(dve.reciprocal(den, m4[:, :, :, 64:65]))
                    link(ts(sm[u][:, 8:12], sm[u][:, 8:12], memw[:, 2:3], None, ALU.mult))
                    link(tt(af2[u].rearrange("p (s b d) -> p s b d", s=2, b=2), m4[:, :, :, 0:64],
                            den.to_broadcast([P, 2, 2, 64]), ALU.mult))
                    S(tt(xr[u][:], xr[u][:], af2[u], ALU.add), "mem_out")

                def a22(u, half):
                    n = "3" + "ab"[half]
                    last = heads_out(u, n, af[u][:, half * P:(half + 1) * P], DHM)
                    if half == 0:
                        S(last, "pv3a_out")
                        return
                    link(last)
                    link(stt(xr[u][:], af[u][:], memw[:, 3:4], xr[u][:], ALU.mult, ALU.add))
                    apart(dve)
                    link(cp(xall[:].rearrange("p (i u) d -> p i u d", u=2)[:, bass.ds(it, 1), u, :], xr[u][:, None, :]))
                    norm(u, 4, xr[u][:])

                def a31(u):
                    W("mixqkv", u)
                    apart(dve)
                    mark(cp(vall[:].rearrange("p (i u) h d -> p i u (h d)", u=2)[:, bass.ds(it, 1), u, :],
                            ps_f(u, 1, DM, DM)[:, None, :]))

                def a32(u):
                    W("mixs", u)
                    link(tt(acc[:].rearrange("p h t -> p (h t)"), ps_f(u, 2, DM), acc[:].rearrange("p h t -> p (h t)"),
                            ALU.add))

                stages = [l0, a0, a1, a2, a3, lambda u: pt(u, "pT0", "pt0"), a5, a6, lambda u: xTn(u, 1), a7, a8,
                          lambda u: soft(u, "1"), lambda u: pt(u, "pT1", "pt1"), a11, a12, a13,
                          lambda u: xTn(u, 2), a15, a16, a17, lambda u: xTn(u, 3), a19, a20, a20m,
                          lambda u: soft(u, "3a"), lambda u: pt(u, "pT3a", "pt3a"), lambda u: a22(u, 0),
                          lambda u: soft(u, "3b"), lambda u: pt(u, "pT3b", "pt3b"), lambda u: a22(u, 1),
                          lambda u: xTn(u, 4), a31, a32]
                for s in stages:
                    for u in range(2):
                        s(u)
                print("dve per turn", own.n)
                own.leave(NSEQ // 2)
            vector_b(dve, own)


def shape_constants():
    f = np.float32
    inv = (f(1.0) / (f(10000.0) ** (np.arange(0, D0, 2, dtype=f) / f(D0)))).astype(f)
    ang = (np.arange(T, dtype=f)[None, :] * np.tile(inv, 4)[:, None]).astype(f).astype(np.float64)

    def cols(m):
        return np.broadcast_to(m.reshape(P, NBLK, 1, WIN), (P, NBLK, G0, WIN)).reshape(P, 512).astype(f)
    r, c = np.arange(P)[:, None] % WIN, np.arange(64)[None, :]
    seen = (c > r) & (c <= r + WIN)
    masks = np.stack([seen & (c >= WIN)] + [seen] * (NBLK - 1), 1)
    gam = 1.0 - 2.0 ** (-5.0 - np.arange(2))
    expo = np.arange(T)[None, :] - np.arange(T)[:, None]
    d = np.where(expo[None] <= 0, gam[:, None, None] ** expo[None], 0.0)
    dn = d / np.sqrt(d.sum(-1))[:, None, :] / np.sqrt(float(P))
    return {
        "ident": np.eye(P, dtype=f), "cosI": cols(np.cos(ang)), "sinI": cols(np.sin(ang)),
        "mask": np.where(masks, f(0), f(MASKED)).reshape(P, NBLK * 64).astype(f),
        "decay": np.ascontiguousarray(dn.transpose(2, 0, 1)).astype(f),
        "iota8": np.broadcast_to(np.arange(NE, dtype=f), (P, NE)).copy(),
    }


def layout(x, ctx_2048, **w):
    def tiles(m):
        return m.reshape(-1, P, m.shape[1]).transpose(1, 0, 2)
    L0, X0, M = "L0_attn_", "L0_xattn_", "L1_attn_"
    wq = w[L0 + "Wq"].reshape(DM, 2, 4, G0, 2, 32).transpose(0, 4, 1, 3, 2, 5).reshape(DM, 2048)
    wk = w[L0 + "Wk"].reshape(DM, 2, 4, 2, 32).transpose(0, 3, 1, 2, 4).reshape(DM, 512)
    bq = w[L0 + "bq"].reshape(2, 4, G0, 2, 32).transpose(1, 4, 3, 0, 2).reshape(P, 4, G0, 1)
    bq = np.broadcast_to(bq, (P, 4, G0, WIN)).reshape(P, 4, P)
    bk = w[L0 + "bk"].reshape(2, 4, 2, 32).transpose(2, 0, 1, 3).reshape(4, P).T
    wo = w[L0 + "Wo"].reshape(4, 2, G0, D0, DM).transpose(1, 3, 0, 2, 4).reshape(P, 16, DM)
    sinks = w[L0 + "sinks"].reshape(2, 4, G0).transpose(2, 1, 0)
    sinks = np.broadcast_to(sinks[:, None, :, :, None], (G0, WIN, 4, 2, NBLK)).reshape(P, 32)
    mem = np.concatenate([w[M + "memory"], w[M + "memory_norm"]], 1)
    d = {
        "x": x, "ctx": ctx_2048, "wq": tiles(wq), "wk": tiles(wk), "wv": tiles(w[L0 + "Wv"]), "wo": wo,
        "bq": bq, "bk": bk, "bv": w[L0 + "bv"][None], "sinkT": sinks,
        "wx": np.stack([tiles(w[X0 + n].T) for n in ("q_w", "k_img_w", "v_img_w", "o_w")], 1),
        "rows": np.stack([w[L0 + "bo"], w[X0 + "q_b"], w[X0 + "k_img_b"], w[X0 + "v_img_b"], w[X0 + "o_b"],
                          w[X0 + "norm_q_w"], w[X0 + "norm_k_img_w"], w["L1_xattn_gn_gamma"],
                          w["L1_xattn_gn_beta"]]),
        "rw": tiles(w["L0_ffn_router_weight"].T), "rb": w["L0_ffn_router_bias"][None],
        "ebias": w["L0_ffn_expert_bias"],
        "wm": tiles(np.concatenate([w[M + "Wq"].T, w[M + "Wk"].T, w[M + "Wv"].T], 1)),
        "mem": mem, "memw": w[M + "memory_weight"][None],
        "wh": w["L1_xattn_Wh"].transpose(1, 0, 2),
        "wgo": np.stack([tiles(w["L1_xattn_wg_w"]), tiles(w["L1_xattn_wo_w"])], 1),
        "gw": tiles(w["L1_ffn_gate_weight"].T),
        "gu": w["L1_ffn_gate_up_proj"].transpose(0, 2, 1).reshape(NE, KT_, P, 2 * NI).transpose(0, 2, 1, 3)
        .reshape(NE, P, KT_ * 2 * NI),
        "dn": w["L1_ffn_down_proj"].transpose(0, 2, 1).reshape(NE, 4, P, DM).transpose(0, 2, 1, 3)
        .reshape(NE, P, 4 * DM),
    }
    d.update(shape_constants())
    return {k: np.ascontiguousarray(v) for k, v in d.items()}


def kernel(**inputs):
    import concourse.bacc as _bacc
    from concourse.bass_utils import run_bass_kernel_spmd as _run

    nc = _bacc.Bacc("TRN2", target_bir_lowering=False, num_devices=1)
    data = layout(**{k: np.asarray(v) for k, v in inputs.items()})
    arrays, args = {}, {}
    for name, v in data.items():
        arrays[f"in_{name}"] = v
        args[name] = nc.dram_tensor(f"in_{name}", v.shape, mybir.dt.from_np(v.dtype), kind="ExternalInput").ap()
    out = nc.dram_tensor("out_0", (NSEQ, T, DM), F32, kind="ExternalOutput").ap()
    program(nc, args, out)
    return _run(nc, [arrays], core_ids=[0]).results[0]["out_0"]
```

```python
from contextlib import ExitStack

import numpy as np

import concourse.bass as bass
from concourse import mybir

F32 = mybir.dt.float32
H16 = mybir.dt.float16
BF16 = mybir.dt.bfloat16
U32 = mybir.dt.uint32
ALU = mybir.AluOpType
ACT = mybir.ActivationFunctionType
AX = mybir.AxisListType

NSEQ, T, DM = 16, 128, 256
P = 128
KT_ = DM // P
NH0, NKV, D0, G0, WIN = 32, 8, 64, 4, 32
NBLK = T // WIN
SCALE0 = float(D0) ** -0.5
MASKED = -1.0e30
NHX, DHX = 16, 16
NHM, DHM, NQM = 8, 8, 4
E0, TOP0 = 64, 8
NE, NI = 8, 512
EPS_LN, EPS_RMS, EPS_GN = 1e-5, 1e-6, 1e-3


SOFT = ("0", "1", "3a", "3b")
FAMILIES = {
    "var": [f"var{n}" for n in range(5)], "rstd": [f"rstd{n}" for n in range(5)],
    "ln": [f"ln{n}" for n in range(5)], "tr": [f"tr{n}" for n in range(5)],
    "xT": [f"xT{n}" for n in range(5)],
    "scores": [f"s{n}" for n in SOFT], "shifted": [f"s{n}m{h}" for n in SOFT for h in (0, 1)],
    "exps": [f"e{n}{h}" for n in SOFT for h in (0, 1)], "normed0": ["n00", "n01"],
    "probs_turned": [f"pT{n}{h}" for n in SOFT for h in (0, 1)],
    "turned_high": [f"pt{n}h{h}" for n in SOFT for h in (0, 1)],
    "turned": [f"pt{n}" for n in SOFT], "weighted": [f"pv{n}" for n in SOFT],
    "b_var": [f"b_var{n}" for n in ("", "g", "5")], "b_rstd": [f"b_rstd{n}" for n in ("", "g", "5")],
}
MEMBER = {m: (f, k, len(ms)) for f, ms in FAMILIES.items() for k, m in enumerate(ms)}


def at(name, it, u):
    _, k, uses = MEMBER.get(name, (name, 0, 1))
    return it * (2 * uses) + (2 * k + u + 1)


def program(nc, a, out):
    with ExitStack() as ctx:
        def sb(name, shape, dt=F32):
            return ctx.enter_context(nc.sbuf_tensor(name, shape, dt))

        def sem(name):
            return ctx.enter_context(nc.semaphore(name))

        sigs = {}

        def sig(name):
            name = MEMBER.get(name, (name,))[0]
            if name not in sigs:
                sigs[name] = sem("s_" + name)
            return sigs[name]

        def two(name, shape, dt=F32):
            return [sb(f"{name}{u}", shape, dt) for u in range(2)]

        PS = [ctx.enter_context(nc.psum_tensor(f"ps{u}", [P, 4, 512], F32)) for u in range(2)]

        ident = sb("ident", [P, P])
        identb, identm = sb("identb", [P, P], H16), sb("identm", [P, P], BF16)
        cosI, sinI = sb("cosI", [P, 512]), sb("sinI", [P, 512])
        mask = sb("mask", [P, NBLK * 64], BF16)
        sinkT = sb("sinkT", [P, 32])
        eps = sb("eps", [P, 4])
        decay = sb("decay", [P, 2, T])
        iota8 = sb("iota8", [P, NE])
        bq, bk = sb("bq", [P, 4, P]), sb("bk", [P, 4])
        rows = sb("rows", [P, 9, DM])
        BO, QB, KB, VB, OB, NQ, NK_, GAM, BET = range(9)
        bv = sb("bv", [P, 512])
        rb = sb("rb", [P, E0])
        wq_h, wq_l = sb("wq_h", [P, KT_, 2048], H16), sb("wq_l", [P, KT_, 2048], H16)
        wk_h, wk_l = sb("wk_h", [P, KT_, 512], H16), sb("wk_l", [P, KT_, 512], H16)
        wv_h, wv_l = sb("wv_h", [P, KT_, 512], H16), sb("wv_l", [P, KT_, 512], H16)
        wo_h, wo_l = sb("wo_h", [P, 16, DM], H16), sb("wo_l", [P, 16, DM], H16)
        wx = sb("wx", [P, 4, KT_, DM])
        rw = sb("rw", [P, KT_, E0])
        ebias = sb("ebias", [E0, DM])
        wm = sb("wm", [P, KT_, 384])
        mem = sb("mem", [P, 65])
        memw = sb("memw", [P, 4])
        wh = sb("wh", [P, 2, P])
        wgo = sb("wgo", [P, 2, KT_, DM])
        gw = sb("gw", [P, KT_, NE])
        acc = sb("acc", [P, 2, T])
        mixT = sb("mixT", [P, 2, T])
        xall = sb("xall", [P, NSEQ, DM])
        vall = sb("vall", [P, NSEQ, 2, P])

        xin, cin = two("xin", [P, DM]), two("cin", [P, DM])
        xr, xn = two("xr", [P, DM]), two("xn", [P, DM])
        bst, mv, rstd = two("bst", [P, 6]), two("mv", [P, 2]), two("rstd", [P, 3])
        xT_h, xT_l = two("xT_h", [P, KT_, 160], H16), two("xT_l", [P, KT_, 160], H16)
        xT, cT = two("xT", [P, KT_, T]), two("cT", [P, KT_, T])
        big = two("big", [P, 2048])
        qhl = two("qhl", [P, 2048])
        q_h = [b[:, 0:1024].bitcast(H16) for b in qhl]
        q_l = [b[:, 1024:2048].bitcast(H16) for b in qhl]
        k_h, k_l = two("k_h", [P, 4, 160], H16), two("k_l", [P, 4, 160], H16)
        kf = two("kf", [P, 2, 512])
        v_h, v_l = two("v_h", [P, 1024], H16), two("v_l", [P, 1024], H16)
        ptf = two("ptf", [P, 2048])
        pt_h = [b[:, 0:1024].bitcast(H16) for b in ptf]
        pt_l = [b[:, 1024:2048].bitcast(H16) for b in ptf]
        st32 = two("st32", [P, 4, 32])
        qf = [b[:, 0:DM] for b in big]
        kvf = [b[:, DM:3 * DM].rearrange("p (a d) -> p a d", a=2) for b in big]
        af2 = [b[:, 3 * DM:4 * DM] for b in big]
        qp, kp = v_h, v_l
        vp_h, vp_l = two("vp_h", [P, 272], H16), two("vp_l", [P, 272], H16)
        af = two("af", [P, DM])
        aT = two("aT", [P, KT_, T])
        lg, wt = two("lg", [P, 2, E0]), two("wt", [P, T])
        sm = two("sm", [P, 16])

        n_const = 27
        A = a

        def split(c):
            return [slice(c * P, (c + 1) * P)]

        n_consts = 15 + 2 + 9 + 4

        def ps_f(u, b, w=512, o=0):
            return PS[u][:, b, o:o + w]

        def psb(u, b):
            return PS[u][:, b, :].bitcast(H16)

        ps_all = [PS[u][:, :, :].rearrange("p b n -> p (b n)") for u in range(2)]

        def q_table(t, n):
            return t[:, None, :].to_broadcast([P, n, 512])

        def k_table(t, n):
            v = t[:]
            return bass.AP(v.tensor, v.offset, [v.ap[0], [0, n], [G0 * WIN, NBLK], [1, WIN]])

        def by_block(u):
            return ps_all[u].rearrange("p (i k r) -> p k i r", i=NBLK, r=WIN)

        def by_token(b):
            return b.rearrange("p (k i r) -> p k i r", i=NBLK, r=WIN)

        def place(h, tiles):
            return (h % tiles) * (16 // tiles) + (h % 16) // tiles

        def head_at(j, tiles):
            return tiles * (j % (16 // tiles)) + j // (16 // tiles)

        def apart(eng):
            eng.sem_inc(sig("apart"), 1)

        class Own:

            def __init__(self, eng, name, per_turn=None):
                self.eng, self.sem, self.n = eng, sig(name), 0
                self.per_turn, self.it, self.base = per_turn, None, 0

            def value(self):
                return self.base + self.n if self.it is None else self.it * self.per_turn + (self.base + self.n)

            def mark(self, ins):
                ins.then_inc(self.sem, 1)
                self.n += 1

            def wait(self):
                self.eng.wait_ge(self.sem, self.value())

            def link(self, ins):
                self.mark(ins)
                self.wait()

            def enter(self, it):
                self.base, self.n, self.it = self.base + self.n, 0, it

            def leave(self, turns):
                assert self.n == self.per_turn, (self.sem, self.n, self.per_turn)
                self.base, self.n, self.it = self.base + turns * self.per_turn, 0, None

        PER = {"act": 18, "dve": 254, "act_b": 6, "dve_b": 64, "dve_c": 26}

        xa_h, xa_l = wq_h, wq_l
        cw = sb("cw", [P, NSEQ, NE])
        ecw = two("ecw", [P, NSEQ])
        idx = two("idx", [P, 8], U32)
        gu_f = [b[:] for b in big]
        dn_f = [b[:, 0:1024] for b in qhl]
        v32 = vall[:].rearrange("p b h e -> p (b h e)")
        eh = [wo_h[:].rearrange("p k n -> p (k n)"), v32[:, 0:1536].bitcast(H16)]
        el = [wo_l[:].rearrange("p k n -> p (k n)"), v32[:, 1536:3072].bitcast(H16)]
        NBLKC, TB = 4, 512
        sil = [kf[s][:, 0, :] for s in range(2)]
        prod = [kf[s][:, 1, :] for s in range(2)]

        def order_c(hidden, down):
            for n in range(2 * NBLKC + 1):
                if n < 2 * NBLKC:
                    hidden(n)
                if n >= 1:
                    down(n - 1)

        def tensor_b(pe, mm, mm3):
            with pe.Fori(0, NSEQ // 2) as it:
                def W(name, u):
                    pe.wait_ge(sig(name), at(name, it, u))

                def tr(u, name, ready, bank, src):
                    W(ready, u)
                    for k in range(KT_):
                        m = pe.transpose(ps_f(u, bank, P, k * P), src[u][:, k * P:(k + 1) * P], ident[:])
                    m.then_inc(sig(name), 1)

                def b1(u):
                    W("b_xT", u)
                    pe.wait_ge(sig("mixT"), 1)
                    for h in range(2):
                        mm(ps_f(u, 0, P, h * P), mixT[:, h, :], big[u][:, h * P:(h + 1) * P], True, True)
                    for k in range(KT_):
                        m = mm(ps_f(u, 0, DM, DM), xT[u][:, k, :], wgo[:, 0, k, :], k == 0, k == KT_ - 1)
                    m.then_inc(sig("b_mix"), 1)

                def b2(u):
                    W("b_aT", u)
                    for k in range(KT_):
                        m = mm(ps_f(u, 2, DM), aT[u][:, k, :], wgo[:, 1, k, :], k == 0, k == KT_ - 1)
                    m.then_inc(sig("b_wo"), 1)

                def b3(u):
                    W("b_xT5", u)
                    for k in range(KT_):
                        m = mm(ps_f(u, 0, NE), xT[u][:, k, :], gw[:, k, :], k == 0, k == KT_ - 1)
                    m.then_inc(sig("b_gate"), 1)

                for s in (lambda u: tr(u, "b_tr", "b_ln", 1, xn), b1, lambda u: tr(u, "b_atr", "b_a", 1, af), b2,
                          lambda u: tr(u, "b_tr5", "b_ln5", 3, xn), b3):
                    for u in range(2):
                        s(u)

            pe.wait_ge(sig("w0_lo"), 1)
            pe.wait_ge(sig("xa_lo"), NSEQ)
            pe.sem_inc(sig("c_down"), 1)
            with pe.Fori(0, NE // 2) as it:
                def hidden(n):
                    p, j = n // NBLKC, n % NBLKC
                    if j == 0:
                        pe.wait_ge(sig(f"w{p}_lo"), it + 1)
                    gh, gl = [w[p][:, 0:2048].rearrange("p (k n) -> p k n", k=KT_) for w in (eh, el)]
                    tok = slice(j * TB, (j + 1) * TB)
                    for i in range(4):
                        q = n * 4 + i
                        pe.wait_ge(sig("c_prod"), it * 32 + max(q - 1, 0) + 1)
                        for g in range(2):
                            c = slice(g * NI + i * P, g * NI + (i + 1) * P)
                            for k in range(KT_):
                                m = mm3(ps_f(0, 2 * (q % 2) + g), gh[:, k, c], gl[:, k, c],
                                        xa_h[:, k, tok], xa_l[:, k, tok], k == 0, k == KT_ - 1)
                        m.then_inc(sig("c_hid"), 1)

                def down(n):
                    p, m_ = n // NBLKC, n % 2
                    dh, dl = [w[p][:, 2048:3072].rearrange("p (k n) -> p k n", k=4) for w in (eh, el)]
                    pe.wait_ge(sig("c_hl"), it * 32 + 4 * n + 5)
                    pe.wait_ge(sig("c_acc"), it * 8 + max(n - 1, 0) + 1)
                    for t in range(4):
                        o = ps_f(1, 2 * m_ + t // 2, DM, (t % 2) * DM)
                        for i in range(4):
                            c = slice(i * TB + t * P, i * TB + (t + 1) * P)
                            m = mm3(o, pt_h[m_][:, c], pt_l[m_][:, c], dh[:, i, :], dl[:, i, :], i == 0, i == 3)
                    m.then_inc(sig("c_down"), 1)

                order_c(hidden, down)

        def scalar_b(act, own, f):
            own_b = Own(act, "act_own_b", PER["act_b"])
            with act.Fori(0, NSEQ // 2) as it:
                own_b.enter(it)

                def W(name, u):
                    act.wait_ge(sig(name), at(name, it, u))

                def rs(u, n, e=0):
                    W(f"b_var{n}", u)
                    own_b.link(f(rstd[u][:, 0:1], mv[u][:, 1:2], ACT.Ln, bias=eps[:, e:e + 1]))
                    f(rstd[u][:, 0:1], rstd[u][:, 0:1], ACT.Exp, scale=-0.5).then_inc(sig(f"b_rstd{n}"), 1)

                def hi(u):
                    W("b_tr5", u)
                    f(xa_h[:].rearrange("p k (i u t) -> p k i u t", i=NSEQ // 2, u=2)[:, :, bass.ds(it, 1), u, :]
                      .rearrange("p k o t -> p k (o t)"),
                      ps_f(u, 3, DM).rearrange("p (k t) -> p k t", k=2), ACT.Copy).then_inc(sig("xa_hi"), 1)

                def gate(u):
                    W("b_dif", u)
                    f(sm[u][:, 10:11], sm[u][:, 9:10], ACT.Exp).then_inc(sig("b_edif"), 1)

                for s in (lambda u: rs(u, ""), lambda u: rs(u, "g", 2), lambda u: rs(u, "5"), hi, gate):
                    for u in range(2):
                        s(u)
                own_b.leave(NSEQ // 2)

            def w_high(p, count):
                act.wait_ge(sig(f"w{p}_in"), count * 32)
                f(eh[p][:, 0:2048], gu_f[p], ACT.Copy)
                f(eh[p][:, 2048:3072], dn_f[p], ACT.Copy).then_inc(sig(f"w{p}_hi"), 1)
            w_high(0, 1)
            with act.Fori(0, NE // 2) as it:
                def hidden(n):
                    for i in range(4):
                        q = n * 4 + i
                        act.wait_ge(sig("c_hid"), it * 32 + q + 1)
                        f(sil[q % 2], ps_f(0, 2 * (q % 2)), ACT.Silu).then_inc(sig("c_silu"), 1)
                        act.wait_ge(sig("c_prod"), it * 32 + q + 2)
                        if i == 0:
                            act.wait_ge(sig("c_down"), it * 8 + max(n - 1, 0) + 1)
                        f(pt_h[n % 2][:, i * TB:(i + 1) * TB], prod[q % 2], ACT.Copy).then_inc(sig("c_hh"), 1)
                    if n == 0:
                        act.wait_ge(sig("c_down"), it * 8 + 1)
                        w_high(1, it + 1)
                    if n == 5:
                        act.wait_ge(sig("c_down"), it * 8 + 4 + 1)
                        w_high(0, it + 2)

                order_c(hidden, lambda n: None)

        def vector_b(dve, own, refine):
            tt, ts, cp, red = dve.tensor_tensor, dve.tensor_scalar, dve.tensor_copy, dve.tensor_reduce
            stt = dve.scalar_tensor_tensor
            accf = acc[:].rearrange("p h t -> p (h t)")
            own.link(tt(accf, accf, decay[:].rearrange("p h t -> p (h t)"), ALU.mult))
            mixf = mixT[:].rearrange("p h t -> p (h t)")
            own.link(stt(mixf, accf, -1.0, accf, ALU.mult, ALU.max))
            ts(mixf, mixf, 1.0, None, ALU.max).then_inc(sig("mixT"), 1)
            own_b = Own(dve, "dve_own_b", PER["dve_b"])
            link, mark = own_b.link, own_b.mark
            xs = xall[:].rearrange("p (i u) d -> p i u d", u=2)
            vs = vall[:].rearrange("p (i u) h e -> p i u (h e)", u=2)
            cws = cw[:].rearrange("p (i u) e -> p i u e", u=2)
            with dve.Fori(0, NSEQ // 2) as it:
                own_b.enter(it)
                own = own_b

                def W(name, u):
                    dve.wait_ge(sig(name), at(name, it, u))

                def S(ins, name):
                    ins.then_inc(sig(name), 1)

                def norm(u, n, x, e="b_ln"):
                    link(dve.bn_stats(bst[u][:], x))
                    apart(dve)
                    S(dve.bn_aggr(mv[u][:], bst[u][:]), f"b_var{n}")
                    W(f"b_rstd{n}", u)
                    refine(link, rstd[u], mv[u][:, 1:2], 1.0, EPS_GN if n == "g" else EPS_LN)
                    return ts(xn[u][:], x, mv[u][:, 0:1], rstd[u][:, 0:1], ALU.subtract, ALU.mult)

                def b0(u):
                    apart(dve)
                    link(cp(xr[u][:, None, :], xs[:, bass.ds(it, 1), u, :]))
                    S(norm(u, "", xr[u][:]), "b_ln")

                def b1(u):
                    W("b_tr", u)
                    apart(dve)
                    mark(cp(big[u][:, None, 0:DM], vs[:, bass.ds(it, 1), u, :]))
                    S(cp(xT[u][:].rearrange("p k t -> p (k t)"), ps_f(u, 1, DM)), "b_xT")

                def b2(u):
                    W("b_mix", u)
                    link(norm(u, "g", ps_f(u, 0, DM)))
                    link(tt(xn[u][:], xn[u][:], rows[:, GAM, :], ALU.mult))
                    link(tt(xn[u][:], xn[u][:], rows[:, BET, :], ALU.add))
                    S(stt(af[u][:], ps_f(u, 0, DM, DM), 0.0, xn[u][:], ALU.max, ALU.mult), "b_a")

                def b3(u):
                    W("b_atr", u)
                    S(cp(aT[u][:].rearrange("p k t -> p (k t)"), ps_f(u, 1, DM)), "b_aT")

                def b4(u):
                    W("b_wo", u)
                    link(tt(xr[u][:], ps_f(u, 2, DM), xr[u][:], ALU.add))
                    apart(dve)
                    mark(cp(xs[:, bass.ds(it, 1), u, :], xr[u][:, None, :]))
                    S(norm(u, "5", xr[u][:]), "b_ln5")

                def b5(u):
                    W("xa_hi", u)
                    S(cp(xT[u][:].rearrange("p k t -> p (k t)"), ps_f(u, 3, DM)), "b_xT5")
                    v = [b[:].rearrange("p k (i u t) -> p k i u t", i=NSEQ // 2, u=2)[:, :, bass.ds(it, 1), u, :]
                         .rearrange("p k o t -> p k (o t)") for b in (xa_l, xa_h)]
                    S(tt(v[0], ps_f(u, 3, DM).rearrange("p (k t) -> p k t", k=2), v[1], ALU.subtract), "xa_lo")

                def b6(u):
                    W("b_gate", u)
                    link(cp(lg[u][:, 0, 0:NE], ps_f(u, 0, NE)))
                    apart(dve)
                    link(dve.max(sm[u][:, 0:8], lg[u][:, 0, 0:NE]))
                    apart(dve)
                    mark(dve.max_index(idx[u][:], sm[u][:, 0:8], lg[u][:, 0, 0:NE]))
                    S(tt(sm[u][:, 9:10], sm[u][:, 1:2], sm[u][:, 0:1], ALU.subtract), "b_dif")
                    own.wait()
                    link(cp(st32[u][:, 0, 0:8], idx[u][:]))
                    W("b_edif", u)
                    link(ts(sm[u][:, 11:12], sm[u][:, 10:11], 1.0, None, ALU.add))
                    link(dve.reciprocal(sm[u][:, 12:13], sm[u][:, 11:12]))
                    link(tt(sm[u][:, 13:14], sm[u][:, 12:13], sm[u][:, 10:11], ALU.mult))
                    mark(ts(st32[u][:, 1, 0:8], iota8[:], st32[u][:, 0, 0:1], sm[u][:, 12:13],
                            ALU.is_equal, ALU.mult))
                    link(ts(st32[u][:, 2, 0:8], iota8[:], st32[u][:, 0, 1:2], sm[u][:, 13:14],
                            ALU.is_equal, ALU.mult))
                    link(tt(cws[:, bass.ds(it, 1), u, :], st32[u][:, 1:2, 0:8], st32[u][:, 2:3, 0:8], ALU.add))

                for s in (b0, b1, b2, b3, b4, b5, b6):
                    for u in range(2):
                        s(u)
                print("dve_b per turn", own_b.n)
                own_b.leave(NSEQ // 2)

            def w_low(p, count):
                dve.wait_ge(sig(f"w{p}_hi"), count)
                tt(el[p][:, 0:2048], gu_f[p], eh[p][:, 0:2048], ALU.subtract)
                tt(el[p][:, 2048:3072], dn_f[p], eh[p][:, 2048:3072], ALU.subtract).then_inc(sig(f"w{p}_lo"), 1)
            w_low(0, 1)
            own_c = Own(dve, "dve_own_c", PER["dve_c"])
            cwe = cw[:].rearrange("p b (i g) -> p b i g", g=2)
            for name in ("c_prod", "c_acc"):
                dve.sem_inc(sig(name), 1)
            with dve.Fori(0, NE // 2) as it:
                own_c.enter(it)
                dve.wait_ge(sig("c_acc"), it * 8 + 1)
                apart(dve)
                for g in range(2):
                    own_c.mark(cp(ecw[g][:, :, None], cwe[:, :, bass.ds(it, 1), g]))
                own_c.wait()

                def hidden(n):
                    for i in range(4):
                        q = n * 4 + i
                        dve.wait_ge(sig("c_silu"), it * 32 + q + 1)
                        dve.wait_ge(sig("c_hl"), it * 32 + max(q - 1, 0) + 1)
                        tt(prod[q % 2], sil[q % 2], ps_f(0, 2 * (q % 2) + 1), ALU.mult).then_inc(sig("c_prod"), 1)
                    if n == 0:
                        w_low(1, it + 1)
                    if n == 5:
                        w_low(0, it + 2)

                def down(n):
                    p, j = n // NBLKC, n % NBLKC
                    dve.wait_ge(sig("c_down"), it * 8 + n + 2)
                    for t in range(4):
                        b = 4 * j + t
                        if n > 0 or t > 0:
                            pass
                        last = stt(xall[:, b, :], ps_f(1, 2 * (n % 2) + t // 2, DM, (t % 2) * DM),
                                   ecw[p][:, b:b + 1], xall[:, b, :], ALU.mult, ALU.add)
                        if t < 3:
                            own_c.mark(last)
                        else:
                            last.then_inc(sig("c_acc"), 1)

                order_c(hidden, down)
                print("dve_c per turn", own_c.n)
                own_c.leave(NE // 2)

        def pool_b(pool):
            pool.sem_inc(sig("c_hl"), 1)
            with pool.Fori(0, NE // 2) as it:
                def hidden(n):
                    for i in range(4):
                        q = n * 4 + i
                        pool.wait_ge(sig("c_hh"), it * 32 + q + 1)
                        c = slice(i * TB, (i + 1) * TB)
                        pool.tensor_tensor(pt_l[n % 2][:, c], prod[q % 2], pt_h[n % 2][:, c],
                                           ALU.subtract).then_inc(sig("c_hl"), 1)
                order_c(hidden, lambda n: None)

        def sync_b(sp):
            def load(p, e):
                sp.dma_start(gu_f[p], A["gu"][e]).then_inc(sig(f"w{p}_in"), 16)
                sp.dma_start(dn_f[p], A["dn"][e]).then_inc(sig(f"w{p}_in"), 16)
            sp.wait_ge(sig("b_mix"), NSEQ)
            load(0, 0)
            load(1, 1)
            for it in range(NE // 2):
                if it == 0:
                    sp.wait_ge(sig("w0_lo"), 1)
                    load(0, 2)
                if it + 1 < NE // 2:
                    sp.wait_ge(sig("w1_lo"), it + 1)
                    load(1, 2 * it + 3)
                    sp.wait_ge(sig("w0_lo"), it + 2)
                    load(0, (2 * it + 4) % NE)
            sp.wait_ge(sig("c_acc"), 8 * NE // 2 + 1)
            sp.dma_start(out.rearrange("b t d -> t b d"), xall[:]).then_inc(sig("stored"), 16)
            sp.wait_ge(sig("stored"), 16)

        block = ctx.enter_context(nc.Block())

        @block.sync
        def _(sp):
            def load(dst, src, name="consts"):
                sp.dma_start(dst, src).then_inc(sig(name), 16)
            for u in range(2):
                sp.dma_start(xin[u][:], A["x"][u]).then_inc(sig(f"x_in{u}"), 16)
                sp.dma_start(cin[u][:], A["ctx"][u]).then_inc(sig(f"x_in{u}"), 16)
            load(big[0][:], A["wq"][:, 0, :], "w_in")
            load(big[1][:], A["wq"][:, 1, :], "w_in")
            load(kf[0][:], A["wk"], "w_in")
            load(kf[1][:], A["wv"], "w_in")
            load(ptf[0][:], A["wo"][:, 0:8, :].rearrange("p k n -> p (k n)"), "w_in")
            load(ptf[1][:], A["wo"][:, 8:16, :].rearrange("p k n -> p (k n)"), "w_in")
            consts = [(ident, "ident"), (cosI, "cosI"), (sinI, "sinI"), (sinkT, "sinkT"),
                      (decay, "decay"), (iota8, "iota8"), (bq, "bq"), (bk, "bk"), (wx, "wx"), (rw, "rw"),
                      (ebias, "ebias"), (wm, "wm"), (wh, "wh"), (wgo, "wgo"), (gw, "gw")]
            for t, n in consts:
                load(t[:], A[n])
            load(mem[0:64, :], A["mem"])
            load(mem[64:128, :], A["mem"])
            for i in range(9):
                load(rows[:, i, :], A["rows"][i:i + 1, :].to_broadcast([P, DM]))
            load(bv[:], A["bv"].to_broadcast([P, 512]))
            load(xn[0][:], A["mask"])
            load(rb[:], A["rb"].to_broadcast([P, E0]))
            load(memw[:, 0:1], A["memw"].to_broadcast([P, 1]))
            assert len(consts) + 2 + 9 + 4 == n_consts
            xs = A["x"].rearrange("(i u) p d -> i u p d", u=2)
            cs = A["ctx"].rearrange("(i u) p d -> i u p d", u=2)
            with sp.Fori(0, NSEQ // 2 - 1) as it:
                for u in range(2):
                    sp.wait_ge(sig("ln0"), at("ln0", it, u))
                    sp.wait_ge(sig("tr0"), at("tr0", it, u))
                    nx = bass.ds(it + 1, 1)
                    sp.dma_start(xin[u][:], xs[nx, u].rearrange("o p d -> (o p) d")).then_inc(sig(f"x_in{u}"), 16)
                    sp.dma_start(cin[u][:], cs[nx, u].rearrange("o p d -> (o p) d")).then_inc(sig(f"x_in{u}"), 16)
            sync_b(sp)

        @block.tensor
        def _(pe):
            def mm(o, l, r, start, stop):
                return pe.matmul(o, l, r, start=start, stop=stop)

            def mm3(o, lh, ll, rh, rl, start=True, stop=True):
                mm(o, lh, rh, start, False)
                mm(o, ll, rh, False, False)
                return mm(o, lh, rl, False, stop)

            pe.wait_ge(sig("consts"), 16 * n_consts)
            pe.wait_ge(sig("w_ready"), 3)
            with pe.Fori(0, NSEQ // 2) as it:
                def W(name, u):
                    pe.wait_ge(sig(name), at(name, it, u))

                def transposes_x(u, name, bank, src, ready):
                    W(ready, u)
                    for k in range(KT_):
                        m = pe.transpose(ps_f(u, bank, P, k * P), src[u][:, k * P:(k + 1) * P], ident[:])
                    m.then_inc(sig(name), 1)

                def a0(u):
                    W("ln0", u)
                    pe.wait_ge(sig(f"x_in{u}"), it * 32 + 32)
                    for k in range(KT_):
                        pe.transpose(ps_f(u, 0, P, k * P), xn[u][:, k * P:(k + 1) * P], ident[:])
                        m = pe.transpose(ps_f(u, 0, P, 256 + k * P), cin[u][:, k * P:(k + 1) * P], ident[:])
                    m.then_inc(sig("tr0"), 1)

                def a1(u):
                    W("xT0", u)
                    for t in range(4):
                        o = ps_f(u, 1, P, t * P)
                        for k in range(KT_):
                            c = slice(t * P, (t + 1) * P)
                            mm3(o, wk_h[:, k, c], wk_l[:, k, c], xT_h[u][:, k, 32:160], xT_l[u][:, k, 32:160],
                                k == 0, k == KT_ - 1)
                    for p in range(2):
                        for k in range(KT_):
                            c = slice(k * 256 + p * P, k * 256 + (p + 1) * P)
                            m = mm3(ps_f(u, 2 + p), q_h[u][:, c], q_l[u][:, c], wv_h[:, k, :], wv_l[:, k, :],
                                    k == 0, k == KT_ - 1)
                    m.then_inc(sig("kv0"), 1)

                def a2(u):
                    W("kv0_out", u)
                    for t in range(16):
                        o = ps_f(u, t // 4).rearrange("p (i g r) -> p g i r", i=NBLK, g=G0)[:, t % 4]
                        for k in range(KT_):
                            c = slice(t * P, (t + 1) * P)
                            m = mm3(o, wq_h[:, k, c], wq_l[:, k, c], xT_h[u][:, k, 32:160], xT_l[u][:, k, 32:160],
                                    k == 0, k == KT_ - 1)
                    m.then_inc(sig("q0"), 1)

                def a3(u):
                    W("q0_out", u)
                    qv = [b[u].rearrange("p (a h i m) -> p a h i m", a=2, h=2, i=NBLK) for b in (q_h, q_l)]
                    for b in range(4):
                        for hf in range(2):
                            pe.matmul(ps_f(u, b, 256, hf * 256), identm[:], mask[:], start=hf == 0, stop=False,
                                      skip_group_check=True)
                    for hf in range(2):
                        for i in range(NBLK):
                            for kvl in range(4):
                                r = slice(32 * kvl, 32 * kvl + 32)
                                o = ps_f(u, kvl, 64, hf * 256 + i * 64)
                                for ab in range(2):
                                    q1, q2 = [v[r, ab, hf, i, :] for v in qv]
                                    k1, k2 = [b[u][r, ab * 2 + hf, 32 * i:32 * i + 64] for b in (k_h, k_l)]
                                    for l_, r_ in ((q1, k1), (q2, k1), (q1, k2)):
                                        m = pe.matmul(o, l_, r_, start=False, stop=False, skip_group_check=True)
                    m.then_inc(sig("s0"), 1)

                def p_transposes(u, n):
                    for h in range(2):
                        W(f"n0{h}" if n == "0" else f"e{n}{h}", u)
                        for j in range(8 * h, 8 * h + 8):
                            m = pe.transpose(ps_f(u, j // 4, P, (j % 4) * P), big[u][:, j * P:(j + 1) * P], ident[:])
                        m.then_inc(sig(f"pT{n}{h}"), 1)

                def a5(u):
                    W("pt0", u)
                    W("v0", u)
                    apart(pe)
                    for kvl in range(4):
                        for hf in range(2):
                            kvp, par = hf * 2 + kvl // 2, kvl % 2
                            kv = hf * 4 + kvl
                            for i in range(NBLK):
                                ip, i2 = i // 2, i % 2
                                blk = (kvl * 2 + hf) * 2 + ip
                                r = slice(64 * i2, 64 * i2 + 64)
                                o = PS[u][64 * par:64 * par + 64, i, kvp * P:(kvp + 1) * P]
                                c = slice(ip * 512 + kv * 64, ip * 512 + kv * 64 + 64)
                                m = mm3(o, v_h[u][r, c], v_l[u][r, c], pt_h[u][r, blk * P:(blk + 1) * P],
                                        pt_l[u][r, blk * P:(blk + 1) * P])
                    m.then_inc(sig("pv0"), 1)

                def a6(u):
                    W("o0", u)
                    for t in range(16):
                        c = slice(t * P, (t + 1) * P)
                        m = mm3(ps_f(u, 0, DM), q_h[u][:, c], q_l[u][:, c], wo_h[:, t, :], wo_l[:, t, :],
                                t == 0, t == 15)
                    m.then_inc(sig("wo0"), 1)

                def a7(u):
                    W("xT1", u)
                    for i, src in enumerate((xT, cT, cT)):
                        o = ps_f(u, i // 2, DM, (i % 2) * DM)
                        for k in range(KT_):
                            m = mm(o, src[u][:, k, :], wx[:, i, k, :], k == 0, k == KT_ - 1)
                    m.then_inc(sig("qkv1"), 1)

                def pack_transposes(u, name, ready, nk):
                    W(ready, u)
                    for j in range(8):
                        pe.transpose(psb(u, 0)[:, j * P:(j + 1) * P], qp[u][:, j * P:(j + 1) * P], identb[:])
                    for j in range(nk):
                        m = pe.transpose(psb(u, 1)[:, j * P:(j + 1) * P], kp[u][:, j * P:(j + 1) * P], identb[:])
                    return m

                def a9(u):
                    W("qkT1", u)
                    for h in range(NHX):
                        r = slice(64 * (h % 2), 64 * (h % 2) + 64)
                        c = slice((h // 2) * P, (h // 2 + 1) * P)
                        j = place(h, 2)
                        m = mm(ps_f(u, j // 4, P, (j % 4) * P), pt_h[u][r, c], pt_l[u][r, c], True, True)
                    m.then_inc(sig("s1"), 1)

                def pv(u, name, ready, tiles, nkh, dv):
                    W(ready, u)
                    for j in range(16):
                        c = slice(j * P, (j + 1) * P)
                        h = head_at(j, tiles)
                        w = slice((h % nkh) * dv, (h % nkh + 1) * dv)
                        m = mm3(ps_f(u, 0, dv, h * 32), pt_h[u][:, c], pt_l[u][:, c], vp_h[u][:, w], vp_l[u][:, w])
                    m.then_inc(sig(name), 1)

                def proj_x(u):
                    W("aT1", u)
                    for k in range(KT_):
                        m = mm(ps_f(u, 0, DM), aT[u][:, k, :], wx[:, 3, k, :], k == 0, k == KT_ - 1)
                    m.then_inc(sig("wo1"), 1)

                def a15(u):
                    W("xT2", u)
                    for k in range(KT_):
                        m = mm(ps_f(u, 0, E0), xT[u][:, k, :], rw[:, k, :], k == 0, k == KT_ - 1)
                    m.then_inc(sig("rl"), 1)

                def a16(u):
                    W("rw", u)
                    apart(pe)
                    pe.transpose(PS[u][0:E0, 1, 0:P], lg[u][:, 0, :], ident[:]).then_inc(sig("rwT"), 1)

                def a17(u):
                    W("rwT_out", u)
                    mm(ps_f(u, 0, DM), wt[u][0:E0, :], ebias[:], True, True).then_inc(sig("eb"), 1)

                def a19(u):
                    W("xT3", u)
                    for k in range(KT_):
                        m = mm(ps_f(u, 0, 384), xT[u][:, k, :], wm[:, k, :], k == 0, k == KT_ - 1)
                    m.then_inc(sig("qkv3"), 1)

                def a20(u):
                    pack_transposes(u, "", "pk3", 2)
                    for k in range(2):
                        m = pe.transpose(ps_f(u, 2, P, k * P), af[u][:, k * P:(k + 1) * P], ident[:])
                    m.then_inc(sig("tr3b"), 1)

                def a20m(u):
                    W("qkT3", u)
                    for qi in range(NQM):
                        r = slice(64 * (qi % 2), 64 * (qi % 2) + 64)
                        m = mm(ps_f(u, 2 + qi % 2, 65, (qi // 2) * P), aT[u][r, qi // 2, :], mem[r, :], True, True)
                    m.then_inc(sig("mem"), 1)

                def a21(u, half):
                    W("mem_out" if half == 0 else "pv3a_out", u)
                    for hh in range(half * 16, half * 16 + 16):
                        j = place(hh, 4)
                        h = hh % NHM
                        r = slice(32 * (hh % 4), 32 * (hh % 4) + 32)
                        m = mm(ps_f(u, j // 4, P, (j % 4) * P), qp[u][r, (hh // 4) * P:(hh // 4 + 1) * P],
                               kp[u][r, (h // 4) * P:(h // 4 + 1) * P], True, True)
                    m.then_inc(sig("s3" + "ab"[half]), 1)

                def a31(u):
                    W("xT4", u)
                    for h in range(2):
                        mm(ps_f(u, 0, P, h * P), wh[:, h, :], xT[u][:, h, :], True, True)
                        mm(ps_f(u, 0, P, 256 + h * P), wh[:, h, :], cT[u][:, h, :], True, True)
                        m = mm(ps_f(u, 1, P, 256 + h * P), cT[u][:, h, :], wh[:, h, :], True, True)
                    m.then_inc(sig("mixqkv"), 1)

                def a32(u):
                    W("mixqkv_out", u)
                    for h in range(2):
                        m = mm(ps_f(u, 2, P, h * P), big[u][:, 256 + h * P:256 + (h + 1) * P],
                               big[u][:, h * P:(h + 1) * P], True, True)
                    m.then_inc(sig("mixs"), 1)

                stages = [a0, a1, a2, a3, lambda u: p_transposes(u, "0"), a5, a6,
                          lambda u: transposes_x(u, "tr1", 1, xn, "ln1"), a7,
                          lambda u: pack_transposes(u, "", "pk1", 8).then_inc(sig("qkT1p"), 1), a9,
                          lambda u: p_transposes(u, "1"),
                          lambda u: pv(u, "pv1", "pt1", 2, NHX, DHX + 1),
                          lambda u: transposes_x(u, "atr1", 1, af, "a1"), proj_x,
                          lambda u: transposes_x(u, "tr2", 1, xn, "ln2"), a15, a16, a17,
                          lambda u: transposes_x(u, "tr3", 1, xn, "ln3"), a19, a20, a20m,
                          lambda u: a21(u, 0), lambda u: p_transposes(u, "3a"),
                          lambda u: pv(u, "pv3a", "pt3a", 4, NHM, DHM + 1),
                          lambda u: a21(u, 1), lambda u: p_transposes(u, "3b"),
                          lambda u: pv(u, "pv3b", "pt3b", 4, NHM, DHM + 1),
                          lambda u: transposes_x(u, "tr4", 1, xn, "ln4"), a31, a32]
                for s in stages:
                    for u in range(2):
                        s(u)
            tensor_b(pe, mm, mm3)

        @block.scalar
        def _(act):
            own = Own(act, "act_own", PER["act"])
            f = act.activation
            act.wait_ge(sig("w_in"), 6 * 16)
            for n in range(2):
                f(wq_h[:, n, :], big[n][:], ACT.Copy)
                f(wo_h[:, 8 * n:8 * n + 8, :].rearrange("p k n -> p (k n)"), ptf[n][:], ACT.Copy)
            f(wk_h[:], kf[0][:], ACT.Copy)
            f(wv_h[:], kf[1][:], ACT.Copy).then_inc(sig("w_high"), 1)
            act.wait_ge(sig("consts"), 16 * n_consts)
            act.wait_ge(sig("w_ready"), 2)
            f(identm[:], ident[:], ACT.Copy)
            f(mask[:], xn[0][:], ACT.Copy)
            f(identb[:], ident[:], ACT.Copy).then_inc(sig("w_ready"), 1)
            f(memw[:, 1:2], memw[:, 0:1], ACT.Exp, scale=-1.0).then_inc(sig("memw"), 1)
            act.preload_act_table_set("natural_log_exp_and_others")
            with act.Fori(0, NSEQ // 2) as it:
                own.enter(it)

                def W(name, u):
                    act.wait_ge(sig(name), at(name, it, u))

                def rs(u, n, e=0, scale=1.0, src=None):
                    W(f"var{n}", u)
                    own.link(f(rstd[u][:, 0:1], mv[u][:, 1:2] if src is None else src, ACT.Ln,
                               bias=eps[:, e:e + 1], scale=scale))
                    f(rstd[u][:, 0:1], rstd[u][:, 0:1], ACT.Exp, scale=-0.5).then_inc(sig(f"rstd{n}"), 1)

                def a0(u):
                    W("tr0", u)
                    f(xT_h[u][:, :, 32:160], ps_f(u, 0, 256).rearrange("p (k t) -> p k t", k=2), ACT.Copy)\
                        .then_inc(sig("xT0h"), 1)
                    f(cT[u][:].rearrange("p k t -> p (k t)"), ps_f(u, 0, 256, 256), ACT.Copy)\
                        .then_inc(sig("cT0"), 1)

                def a1(u):
                    W("k0r", u)
                    f(k_h[u][:, :, 32:160], kf[u][:, 0, :].rearrange("p (a t) -> p a t", a=4), ACT.Copy)\
                        .then_inc(sig("k0h"), 1)
                    W("v0f", u)
                    f(v_h[u][:], big[u][:, 0:1024], ACT.Copy).then_inc(sig("v0h"), 1)

                def a2(u):
                    W("q0r", u)
                    f(q_h[u], big[u][:], ACT.Copy).then_inc(sig("q0h"), 1)

                def soft(u, n, scale):
                    for h in range(2):
                        W(f"s{n}m{h}", u)
                        c = slice(1024 * h, 1024 * h + 1024)
                        if n == "0":
                            k = slice(16 * h, 16 * h + 16)
                            f(st32[u][:, 1, k], st32[u][:, 1, k], ACT.Exp, scale=scale)
                        f(big[u][:, c], big[u][:, c], ACT.Exp, scale=scale).then_inc(sig(f"e{n}{h}"), 1)

                def pt(u, n):
                    for h in range(2):
                        W(f"pT{n}{h}", u)
                        c = slice(1024 * h, 1024 * h + 1024)
                        f(pt_h[u][:, c], ps_all[u][:, c], ACT.Copy).then_inc(sig(f"pt{n}h{h}"), 1)

                def a5(u):
                    W("pv0", u)
                    f(by_token(q_h[u]), by_block(u), ACT.Copy).then_inc(sig("o0h"), 1)

                def rms(u, n, src, e):
                    W(f"{n}f", u)
                    own.link(f(af2[u], src, ACT.Square, accum_out=rstd[u][:, 1:2]))
                    own.link(f(rstd[u][:, 0:1], rstd[u][:, 1:2], ACT.Ln, bias=eps[:, e:e + 1], scale=1.0 / DM))
                    f(rstd[u][:, 0:1], rstd[u][:, 0:1], ACT.Exp, scale=-0.5).then_inc(sig(f"{n}rstd"), 1)

                def a7(u):
                    rms(u, "q1", qf[u], 1)
                    W("q1n", u)
                    rms(u, "k1", kvf[u][:, 0, :], 1)

                def qkT(u, tr, nm, nk):
                    W(tr, u)
                    f((pt_h if nk == 8 else qp)[u][:, 0:1024], psb(u, 0), ACT.Copy).then_inc(sig(nm), 1)

                def a15(u):
                    W("rlm", u)
                    f(lg[u][:, 0, :], lg[u][:, 0, :], ACT.Exp, accum_out=sm[u][:, 8:9]).then_inc(sig("rle"), 1)

                def a19(u):
                    if u == 0:
                        act.preload_act_table_set("exp_and_others")
                    W("sgm", u)
                    f(af2[u], af2[u], ACT.Tanh, scale=0.5).then_inc(sig("sge"), 1)
                    if u == 1:
                        act.preload_act_table_set("natural_log_exp_and_others")

                def a31(u):
                    W("mixqkv", u)
                    f(big[u][:, 0:512], ps_f(u, 0), ACT.Copy).then_inc(sig("mixqkv_out"), 1)

                stages = [lambda u: rs(u, 0), a0, a1, a2, lambda u: soft(u, "0", SCALE0), lambda u: pt(u, "0"), a5,
                          lambda u: rs(u, 1), a7, lambda u: qkT(u, "qkT1p", "qT1", 8),
                          lambda u: soft(u, "1", float(DHX) ** -0.5), lambda u: pt(u, "1"),
                          lambda u: rs(u, 2), a15, lambda u: rs(u, 3), a19,
                          lambda u: qkT(u, "tr3b", "qT3", 2),
                          lambda u: soft(u, "3a", float(DHM) ** -0.5), lambda u: pt(u, "3a"),
                          lambda u: soft(u, "3b", float(DHM) ** -0.5), lambda u: pt(u, "3b"),
                          lambda u: rs(u, 4), a31]
                for s in stages:
                    for u in range(2):
                        s(u)
                own.leave(NSEQ // 2)
            scalar_b(act, own, f)

        @block.gpsimd
        def _(pool):
            for n in range(2):
                for b in (xT_h, xT_l, k_h, k_l):
                    pool.memset(b[n][:], 0.0).then_inc(sig("zeros"), 1)
            pool_b(pool)

        @block.vector
        def _(dve):
            own = Own(dve, "dve_own", PER["dve"])
            link, mark = own.link, own.mark
            tt, ts, cp, red = dve.tensor_tensor, dve.tensor_scalar, dve.tensor_copy, dve.tensor_reduce
            stt = dve.scalar_tensor_tensor

            def refine(link, y, var, scale, eps_):
                link(ts(y[:, 2:3], var, scale, eps_, ALU.mult, ALU.add))
                link(stt(y[:, 2:3], y[:, 0:1], y[:, 0:1], y[:, 2:3], ALU.mult, ALU.mult))
                link(ts(y[:, 2:3], y[:, 2:3], -0.5, 1.5, ALU.mult, ALU.add))
                link(tt(y[:, 0:1], y[:, 0:1], y[:, 2:3], ALU.mult))

            for i, e in enumerate((EPS_LN, EPS_RMS, EPS_GN, 0.0)):
                mark(dve.memset(eps[:, i:i + 1], e))
            mark(dve.memset(acc[:], 0.0))
            for u in range(2):
                mark(dve.memset(vp_l[u][:], 0.0))
                mark(dve.memset(vp_h[u][:], 1.0))
            dve.wait_ge(sig("w_high"), 1)
            for n in range(2):
                mark(tt(wq_l[:, n, :], big[n][:], wq_h[:, n, :], ALU.subtract))
                c = slice(8 * n, 8 * n + 8)
                mark(tt(wo_l[:, c, :].rearrange("p k n -> p (k n)"), ptf[n][:],
                        wo_h[:, c, :].rearrange("p k n -> p (k n)"), ALU.subtract))
            mark(tt(wk_l[:], kf[0][:], wk_h[:], ALU.subtract))
            link(tt(wv_l[:], kf[1][:], wv_h[:], ALU.subtract))
            dve.wait_ge(sig("zeros"), 8)
            dve.memset(sm[0][:], 0.0).then_inc(sig("w_ready"), 1)
            dve.wait_ge(sig("consts"), 16 * n_consts)
            dve.memset(sm[1][:], 0.0).then_inc(sig("w_ready"), 1)
            dve.wait_ge(sig("w_ready"), 3)
            dve.wait_ge(sig("memw"), 1)
            link(ts(sinkT[:], sinkT[:], 1.0 / SCALE0, None, ALU.mult))
            link(ts(memw[:, 2:3], memw[:, 1:2], 1.0, None, ALU.add))
            link(dve.reciprocal(memw[:, 2:3], memw[:, 2:3]))
            link(ts(memw[:, 3:4], memw[:, 2:3], -1.0, 1.0, ALU.mult, ALU.add))

            with dve.Fori(0, NSEQ // 2) as it:
                own.enter(it)

                def W(name, u):
                    dve.wait_ge(sig(name), at(name, it, u))

                def S(ins, name):
                    ins.then_inc(sig(name), 1)

                def norm(u, n, x):
                    link(dve.bn_stats(bst[u][:], x))
                    apart(dve)
                    S(dve.bn_aggr(mv[u][:], bst[u][:]), f"var{n}")
                    W(f"rstd{n}", u)
                    refine(link, rstd[u], mv[u][:, 1:2], 1.0, EPS_LN)
                    S(ts(xn[u][:], x, mv[u][:, 0:1], rstd[u][:, 0:1], ALU.subtract, ALU.mult), f"ln{n}")

                def l0(u):
                    dve.wait_ge(sig(f"x_in{u}"), it * 32 + 32)
                    link(tt(xr[u][:], xin[u][:], rows[:, BO, :], ALU.add))
                    norm(u, 0, xin[u][:])

                def a0(u):
                    W("tr0", u)
                    W("xT0h", u)
                    W("cT0", u)
                    link(tt(xT_l[u][:, :, 32:160], ps_f(u, 0, 256).rearrange("p (k t) -> p k t", k=2),
                            xT_h[u][:, :, 32:160], ALU.subtract))
                    for d, b in ((q_h, xT_h), (q_l, xT_l)):
                        v = b[u][:]
                        last = cp(d[u][:, 0:512].rearrange("p (k i c) -> p k i c", k=KT_, i=NBLK),
                                  bass.AP(v.tensor, v.offset, [v.ap[0], [160, KT_], [WIN, NBLK], [1, 2 * WIN]]))
                        if b is xT_h:
                            mark(last)
                    S(last, "xT0")

                def rope_sin(srcb, dst, shape, sin):
                    w = srcb.shape[1] // 2
                    A_, B_, dA, dB = [shape(b) for b in (srcb[:, 0:w], srcb[:, w:2 * w], dst[:, 0:w], dst[:, w:2 * w])]
                    mark(tt(dA, B_, sin, ALU.mult))
                    link(tt(dB, A_, sin, ALU.mult))

                def a1(u):
                    W("kv0", u)
                    kps = ps_f(u, 1).rearrange("p (a t) -> p a t", a=4)
                    kb = kf[u][:, 0, :]
                    kb4 = kb.rearrange("p (a t) -> p a t", a=4)
                    mark(tt(kb4, kps, bk[:, :, None].to_broadcast([P, 4, P]), ALU.add))
                    mark(tt(big[u][:, 0:512], ps_f(u, 2), bv[:], ALU.add))
                    S(tt(big[u][:, 512:1024], ps_f(u, 3), bv[:], ALU.add), "v0f")
                    own.wait()
                    rope_sin(kb, kf[u][:, 1, :], lambda b: b.rearrange("p (h i r) -> p h i r", h=2, i=NBLK),
                             k_table(sinI, 2))
                    kb5 = kb.rearrange("p (a i r) -> p a i r", a=4, i=NBLK)
                    link(tt(kb5, kb5, k_table(cosI, 4), ALU.mult))
                    mark(tt(kb[:, 0:256], kb[:, 0:256], kf[u][:, 1, 0:256], ALU.subtract))
                    S(tt(kb[:, 256:512], kb[:, 256:512], kf[u][:, 1, 256:512], ALU.add), "k0r")
                    W("v0h", u)
                    S(tt(v_l[u][:], big[u][:, 0:1024], v_h[u][:], ALU.subtract), "v0")
                    W("k0h", u)
                    S(tt(k_l[u][:, :, 32:160], kf[u][:, 0, :].rearrange("p (a t) -> p a t", a=4),
                         k_h[u][:, :, 32:160], ALU.subtract), "kv0_out")

                def a2(u):
                    W("q0", u)
                    W("v0", u)
                    for ab in range(4):
                        last = tt(big[u][:, ab * 512:(ab + 1) * 512].rearrange("p (i m) -> p i m", i=NBLK),
                                  ps_f(u, ab).rearrange("p (i m) -> p i m", i=NBLK),
                                  bq[:, ab:ab + 1, :].to_broadcast([P, NBLK, P]), ALU.add)
                        mark(last)
                    own.wait()
                    rope_sin(big[u][:], ptf[u][:], lambda b: b.rearrange("p (h m) -> p h m", h=2), q_table(sinI, 2))
                    b4 = big[u][:].rearrange("p (a m) -> p a m", a=4)
                    link(tt(b4, b4, q_table(cosI, 4), ALU.mult))
                    mark(tt(big[u][:, 0:1024], big[u][:, 0:1024], ptf[u][:, 0:1024], ALU.subtract))
                    S(tt(big[u][:, 1024:2048], big[u][:, 1024:2048], ptf[u][:, 1024:2048], ALU.add), "q0r")
                    W("q0h", u)
                    S(tt(q_l[u], big[u][:], q_h[u], ALU.subtract), "q0_out")

                def a3(u):
                    W("s0", u)
                    for h in range(2):
                        k = slice(16 * h, 16 * h + 16)
                        c = slice(1024 * h, 1024 * h + 1024)
                        p16 = ps_all[u][:, c].rearrange("p (a t) -> p a t", a=16)
                        b16 = big[u][:, c].rearrange("p (a t) -> p a t", a=16)
                        m_ = st32[u][:, 0, k]
                        link(red(m_, p16, AX.X, ALU.max))
                        link(tt(m_, m_, sinkT[:, k], ALU.max))
                        mark(tt(st32[u][:, 1, k], sinkT[:, k], m_, ALU.subtract))
                        S(tt(b16, p16, m_[:, :, None].to_broadcast([P, 16, 64]), ALU.subtract), f"s0m{h}")

                def a3n(u):
                    for h in range(2):
                        k = slice(16 * h, 16 * h + 16)
                        b16 = big[u][:, 1024 * h:1024 * h + 1024].rearrange("p (a t) -> p a t", a=16)
                        l_ = st32[u][:, 2, k]
                        W(f"e0{h}", u)
                        link(red(l_, b16, AX.X, ALU.add))
                        link(tt(l_, l_, st32[u][:, 1, k], ALU.add))
                        link(dve.reciprocal(l_, l_))
                        S(tt(b16, b16, l_[:, :, None].to_broadcast([P, 16, 64]), ALU.mult), f"n0{h}")

                def pt(u, n):
                    for h in range(2):
                        W(f"pt{n}h{h}", u)
                        c = slice(1024 * h, 1024 * h + 1024)
                        last = tt(pt_l[u][:, c], ps_all[u][:, c], pt_h[u][:, c], ALU.subtract)
                        if h == 0:
                            mark(last)
                        else:
                            S(last, f"pt{n}")

                def a5(u):
                    W("o0h", u)
                    S(tt(by_token(q_l[u]), by_block(u), by_token(q_h[u]), ALU.subtract), "o0")

                def a6(u):
                    W("wo0", u)
                    link(tt(xr[u][:], ps_f(u, 0, DM), xr[u][:], ALU.add))
                    norm(u, 1, xr[u][:])

                def xTn(u, n):
                    W(f"tr{n}", u)
                    S(cp(xT[u][:].rearrange("p k t -> p (k t)"), ps_f(u, 1, DM)), f"xT{n}")

                def pack(u, dst, srcf, nh, dh, hi2, done=None):
                    d = dst.rearrange("p (h c d) -> p h c d", c=4, d=dh)
                    s = srcf.rearrange("p (h d) -> p h d", d=dh)
                    for a_ in range(2):
                        ch = 2 * a_ if hi2 == 2 else a_
                        mark(cp(d[:, :, ch, :], s))
                    own.wait()
                    for a_ in range(2):
                        cl = 2 * a_ + 1 if hi2 == 2 else 2 + a_
                        last = tt(d[:, :, cl, :], s, d[:, :, 0, :], ALU.subtract)
                        if a_ == 0 or done is None:
                            mark(last)
                        else:
                            S(last, done)

                def packv(u, srcf, nh, dh):
                    w = nh * (dh + 1)
                    vh = vp_h[u][:, 0:w].rearrange("p (h d) -> p h d", d=dh + 1)
                    vl = vp_l[u][:, 0:w].rearrange("p (h d) -> p h d", d=dh + 1)
                    s = srcf.rearrange("p (h d) -> p h d", d=dh)
                    mark(dve.memset(vh[:, :, dh:dh + 1], 1.0))
                    mark(dve.memset(vl[:, :, dh:dh + 1], 0.0))
                    link(cp(vh[:, :, 0:dh], s))
                    link(tt(vl[:, :, 0:dh], s, vh[:, :, 0:dh], ALU.subtract))

                def a7(u):
                    W("qkv1", u)
                    link(tt(xr[u][:], xr[u][:], rows[:, OB, :], ALU.add))
                    S(tt(qf[u], ps_f(u, 0, DM), rows[:, QB, :], ALU.add), "q1f")
                    mark(tt(kvf[u][:, 1, :], ps_f(u, 1, DM), rows[:, VB, :], ALU.add))
                    own.wait()
                    packv(u, kvf[u][:, 1, :], NHX, DHX)
                    W("q1rstd", u)
                    refine(link, rstd[u], rstd[u][:, 1:2], 1.0 / DM, EPS_RMS)
                    S(stt(qf[u], qf[u], rstd[u][:, 0:1], rows[:, NQ, :], ALU.mult, ALU.mult), "q1n")
                    S(tt(kvf[u][:, 0, :], ps_f(u, 0, DM, DM), rows[:, KB, :], ALU.add), "k1f")
                    W("q1n", u)
                    pack(u, qp[u][:], qf[u], NHX, DHX, 2)
                    W("k1rstd", u)
                    refine(link, rstd[u], rstd[u][:, 1:2], 1.0 / DM, EPS_RMS)
                    link(stt(kvf[u][:, 0, :], kvf[u][:, 0, :], rstd[u][:, 0:1], rows[:, NK_, :], ALU.mult, ALU.mult))
                    pack(u, kp[u][:], kvf[u][:, 0, :], NHX, DHX, 1, "pk1")

                def a8(u):
                    W("qkT1p", u)
                    W("qT1", u)
                    S(cp(pt_l[u][:, 0:1024], psb(u, 1)), "qkT1")

                def soft(u, n):
                    W(f"s{n}", u)
                    for h in range(2):
                        c = slice(1024 * h, 1024 * h + 1024)
                        p8 = ps_all[u][:, c].rearrange("p (a t) -> p a t", a=8)
                        b8 = big[u][:, c].rearrange("p (a t) -> p a t", a=8)
                        m_ = st32[u][:, 0, 8 * h:8 * h + 8]
                        link(red(m_, p8, AX.X, ALU.max))
                        S(tt(b8, p8, m_[:, :, None].to_broadcast([P, 8, P]), ALU.subtract), f"s{n}m{h}")

                def heads_out(u, n, dst, dh):
                    W(f"pv{n}", u)
                    o = ps_f(u, 0).rearrange("p (h d) -> p h d", d=32)
                    r = st32[u][:, 1, 0:16]
                    link(dve.reciprocal(r[:, :, None], o[:, :, dh:dh + 1]))
                    return tt(dst.rearrange("p (h d) -> p h d", d=dh), o[:, :, 0:dh],
                              r[:, :, None].to_broadcast([P, 16, dh]), ALU.mult)

                def a11(u):
                    S(heads_out(u, "1", af[u][:], DHX), "a1")

                def a12(u):
                    W("atr1", u)
                    S(cp(aT[u][:].rearrange("p k t -> p (k t)"), ps_f(u, 1, DM)), "aT1")

                def a13(u):
                    W("wo1", u)
                    link(tt(xr[u][:], ps_f(u, 0, DM), xr[u][:], ALU.add))
                    norm(u, 2, xr[u][:])

                def a15(u):
                    W("rl", u)
                    l0_, l1_ = lg[u][:, 0, :], lg[u][:, 1, :]
                    link(tt(l0_, ps_f(u, 0, E0), rb[:], ALU.add))
                    link(red(sm[u][:, 9:10], l0_, AX.X, ALU.max))
                    S(ts(l0_, l0_, sm[u][:, 9:10], None, ALU.subtract), "rlm")
                    W("rle", u)
                    link(dve.reciprocal(sm[u][:, 8:9], sm[u][:, 8:9]))
                    link(ts(l0_, l0_, sm[u][:, 8:9], None, ALU.mult))
                    apart(dve)
                    link(dve.max(sm[u][:, 0:8], l0_))
                    apart(dve)
                    link(dve.match_replace(l1_, sm[u][:, 0:8], l0_, 0.0))
                    link(red(sm[u][:, 9:10], sm[u][:, 0:8], AX.X, ALU.add))
                    S(tt(l0_, l0_, l1_, ALU.subtract), "rw")

                def a16(u):
                    W("rwT", u)
                    S(cp(wt[u][0:E0, :], PS[u][0:E0, 1, 0:P]), "rwT_out")

                def a17(u):
                    W("eb", u)
                    link(tt(xr[u][:], ps_f(u, 0, DM), xr[u][:], ALU.add))
                    link(stt(xr[u][:], xn[u][:], sm[u][:, 9:10], xr[u][:], ALU.mult, ALU.add))
                    norm(u, 3, xr[u][:])

                def a19(u):
                    W("qkv3", u)
                    mark(cp(qf[u], ps_f(u, 0, DM)))
                    mark(cp(kvf[u][:, :, 0:64], ps_f(u, 0, 128, DM).rearrange("p (a d) -> p a d", a=2)))
                    own.wait()
                    S(ts(af2[u], qf[u], 0.0, None, ALU.min), "sgm")
                    packv(u, kvf[u][:, 1, 0:64], NHM, DHM)
                    pack(u, qp[u][:], qf[u], 32, DHM, 2)
                    pack(u, kp[u][:, 0:256], kvf[u][:, 0, 0:64], NHM, DHM, 1)
                    tmp = big[u][:, 4 * DM:5 * DM]
                    W("sge", u)
                    link(ts(tmp, af2[u], -0.5, 0.5, ALU.mult, ALU.add))
                    link(dve.reciprocal(tmp, tmp))
                    mark(ts(af[u][:], qf[u], 0.0, None, ALU.max))
                    link(tt(tmp, tmp, af2[u], ALU.mult))
                    S(tt(af[u][:], af[u][:], tmp, ALU.add), "pk3")

                def a20(u):
                    W("tr3b", u)
                    mark(cp(kp[u][:, 0:256], psb(u, 1)[:, 0:256]))
                    W("qT3", u)
                    S(cp(aT[u][:].rearrange("p k t -> p (k t)"), ps_f(u, 2, DM)), "qkT3")

                def a20m(u):
                    W("mem", u)
                    m4 = PS[u][:, 2:4, 0:256].rearrange("p b (s d) -> p s b d", s=2)
                    den = sm[u][:, 8:12].rearrange("p (s b) -> p s b", s=2)[:, :, :, None]
                    link(dve.reciprocal(den, m4[:, :, :, 64:65]))
                    link(ts(sm[u][:, 8:12], sm[u][:, 8:12], memw[:, 2:3], None, ALU.mult))
                    link(tt(af2[u].rearrange("p (s b d) -> p s b d", s=2, b=2), m4[:, :, :, 0:64],
                            den.to_broadcast([P, 2, 2, 64]), ALU.mult))
                    S(tt(xr[u][:], xr[u][:], af2[u], ALU.add), "mem_out")

                def a22(u, half):
                    n = "3" + "ab"[half]
                    last = heads_out(u, n, af[u][:, half * P:(half + 1) * P], DHM)
                    if half == 0:
                        S(last, "pv3a_out")
                        return
                    link(last)
                    link(stt(xr[u][:], af[u][:], memw[:, 3:4], xr[u][:], ALU.mult, ALU.add))
                    apart(dve)
                    link(cp(xall[:].rearrange("p (i u) d -> p i u d", u=2)[:, bass.ds(it, 1), u, :], xr[u][:, None, :]))
                    norm(u, 4, xr[u][:])

                def a31(u):
                    W("mixqkv", u)
                    apart(dve)
                    mark(cp(vall[:].rearrange("p (i u) h d -> p i u (h d)", u=2)[:, bass.ds(it, 1), u, :],
                            ps_f(u, 1, DM, DM)[:, None, :]))

                def a32(u):
                    W("mixs", u)
                    link(tt(acc[:].rearrange("p h t -> p (h t)"), ps_f(u, 2, DM), acc[:].rearrange("p h t -> p (h t)"),
                            ALU.add))

                stages = [l0, a0, a1, a2, a3, a3n, lambda u: pt(u, "0"), a5, a6, lambda u: xTn(u, 1), a7, a8,
                          lambda u: soft(u, "1"), lambda u: pt(u, "1"), a11, a12, a13,
                          lambda u: xTn(u, 2), a15, a16, a17, lambda u: xTn(u, 3), a19, a20, a20m,
                          lambda u: soft(u, "3a"), lambda u: pt(u, "3a"), lambda u: a22(u, 0),
                          lambda u: soft(u, "3b"), lambda u: pt(u, "3b"), lambda u: a22(u, 1),
                          lambda u: xTn(u, 4), a31, a32]
                for s in stages:
                    for u in range(2):
                        s(u)
                print("dve per turn", own.n)
                own.leave(NSEQ // 2)
            vector_b(dve, own, refine)


def shape_constants():
    f = np.float32
    inv = (f(1.0) / (f(10000.0) ** (np.arange(0, D0, 2, dtype=f) / f(D0)))).astype(f)
    ang = (np.arange(T, dtype=f)[None, :] * np.tile(inv, 4)[:, None]).astype(f).astype(np.float64)

    def cols(m):
        return np.broadcast_to(m.reshape(P, NBLK, 1, WIN), (P, NBLK, G0, WIN)).reshape(P, 512).astype(f)
    r, c = np.arange(P)[:, None] % WIN, np.arange(64)[None, :]
    seen = (c > r) & (c <= r + WIN)
    masks = np.stack([seen & (c >= WIN)] + [seen] * (NBLK - 1), 1)
    gam = 1.0 - 2.0 ** (-5.0 - np.arange(2))
    expo = np.arange(T)[None, :] - np.arange(T)[:, None]
    d = np.where(expo[None] <= 0, gam[:, None, None] ** expo[None], 0.0)
    dn = d / np.sqrt(d.sum(-1))[:, None, :] / np.sqrt(float(P))
    return {
        "ident": np.eye(P, dtype=f), "cosI": cols(np.cos(ang)), "sinI": cols(np.sin(ang)),
        "mask": np.where(masks, f(0), f(MASKED)).reshape(P, NBLK * 64).astype(f),
        "decay": np.ascontiguousarray(dn.transpose(2, 0, 1)).astype(f),
        "iota8": np.broadcast_to(np.arange(NE, dtype=f), (P, NE)).copy(),
    }


def layout(x, ctx_2048, **w):
    def tiles(m):
        return m.reshape(-1, P, m.shape[1]).transpose(1, 0, 2)
    L0, X0, M = "L0_attn_", "L0_xattn_", "L1_attn_"
    wq = w[L0 + "Wq"].reshape(DM, 2, 4, G0, 2, 32).transpose(0, 4, 1, 3, 2, 5).reshape(DM, 2048)
    wk = w[L0 + "Wk"].reshape(DM, 2, 4, 2, 32).transpose(0, 3, 1, 2, 4).reshape(DM, 512)
    bq = w[L0 + "bq"].reshape(2, 4, G0, 2, 32).transpose(1, 4, 3, 0, 2).reshape(P, 4, G0, 1)
    bq = np.broadcast_to(bq, (P, 4, G0, WIN)).reshape(P, 4, P)
    bk = w[L0 + "bk"].reshape(2, 4, 2, 32).transpose(2, 0, 1, 3).reshape(4, P).T
    wo = w[L0 + "Wo"].reshape(4, 2, G0, D0, DM).transpose(1, 3, 0, 2, 4).reshape(P, 16, DM)
    sinks = w[L0 + "sinks"].reshape(2, 4, G0).transpose(2, 1, 0)
    sinks = np.broadcast_to(sinks[:, None, :, :, None], (G0, WIN, 4, 2, NBLK)).reshape(P, 32)
    mem = np.concatenate([w[M + "memory"], w[M + "memory_norm"]], 1)
    d = {
        "x": x, "ctx": ctx_2048, "wq": tiles(wq), "wk": tiles(wk), "wv": tiles(w[L0 + "Wv"]), "wo": wo,
        "bq": bq, "bk": bk, "bv": w[L0 + "bv"][None], "sinkT": sinks,
        "wx": np.stack([tiles(w[X0 + n].T) for n in ("q_w", "k_img_w", "v_img_w", "o_w")], 1),
        "rows": np.stack([w[L0 + "bo"], w[X0 + "q_b"], w[X0 + "k_img_b"], w[X0 + "v_img_b"], w[X0 + "o_b"],
                          w[X0 + "norm_q_w"], w[X0 + "norm_k_img_w"], w["L1_xattn_gn_gamma"],
                          w["L1_xattn_gn_beta"]]),
        "rw": tiles(w["L0_ffn_router_weight"].T), "rb": w["L0_ffn_router_bias"][None],
        "ebias": w["L0_ffn_expert_bias"],
        "wm": tiles(np.concatenate([w[M + "Wq"].T, w[M + "Wk"].T, w[M + "Wv"].T], 1)),
        "mem": mem, "memw": w[M + "memory_weight"][None],
        "wh": w["L1_xattn_Wh"].transpose(1, 0, 2),
        "wgo": np.stack([tiles(w["L1_xattn_wg_w"]), tiles(w["L1_xattn_wo_w"])], 1),
        "gw": tiles(w["L1_ffn_gate_weight"].T),
        "gu": w["L1_ffn_gate_up_proj"].transpose(0, 2, 1).reshape(NE, KT_, P, 2 * NI).transpose(0, 2, 1, 3)
        .reshape(NE, P, KT_ * 2 * NI),
        "dn": w["L1_ffn_down_proj"].transpose(0, 2, 1).reshape(NE, 4, P, DM).transpose(0, 2, 1, 3)
        .reshape(NE, P, 4 * DM),
    }
    d.update(shape_constants())
    return {k: np.ascontiguousarray(v) for k, v in d.items()}


def kernel(**inputs):
    import concourse.bacc as _bacc
    from concourse.bass_utils import run_bass_kernel_spmd as _run

    nc = _bacc.Bacc("TRN2", target_bir_lowering=False, num_devices=1)
    data = layout(**{k: np.asarray(v) for k, v in inputs.items()})
    arrays, args = {}, {}
    for name, v in data.items():
        arrays[f"in_{name}"] = v
        args[name] = nc.dram_tensor(f"in_{name}", v.shape, mybir.dt.from_np(v.dtype), kind="ExternalInput").ap()
    out = nc.dram_tensor("out_0", (NSEQ, T, DM), F32, kind="ExternalOutput").ap()
    program(nc, args, out)
    return _run(nc, [arrays], core_ids=[0]).results[0]["out_0"]
```

```python
from contextlib import ExitStack

import numpy as np

import concourse.bass as bass
from concourse import mybir

F32 = mybir.dt.float32
H16 = mybir.dt.float16
BF16 = mybir.dt.bfloat16
ALU = mybir.AluOpType
ACT = mybir.ActivationFunctionType
AX = mybir.AxisListType

NSEQ, T, DM = 16, 128, 256
P = 128
KT_ = DM // P
NH0, NKV, D0, G0, WIN = 32, 8, 64, 4, 32
NBLK = T // WIN
SCALE0 = float(D0) ** -0.5
MASKED = -1.0e30
NHX, DHX = 16, 16
NHM, DHM, NQM = 8, 8, 4
E0, TOP0 = 64, 8
NE, NI = 8, 512
EPS_LN, EPS_RMS, EPS_GN = 1e-5, 1e-6, 1e-3


SOFT = ("0", "1", "3a", "3b")
FAMILIES = {
    "product": ["keys0", "kv0", "q0a", "q0b", "s0p0", "s0p1", "pv0", "wo0", "qkv1", "s1p0", "s1p1", "pv1",
                "wo1", "rl", "rwT", "eb", "qkv3", "mem", "s3ap0", "s3ap1", "pv3a", "s3bp0", "s3bp1", "pv3b",
                "mixqkv", "mixs"],
    "turned": ["tr0", "tr1", "qkT1p", "atr1", "tr2", "tr3", "tr3b", "tr4"],
    "probs_turned": [f"pT{n}{h}" for n in SOFT for h in (0, 1)],
    "b_product": ["b_mix", "b_wo", "b_gate"], "b_turned": ["b_tr", "b_atr", "b_tr5"],
    "rstd": [f"rstd{n}" for n in range(5)], "b_rstd": [f"b_rstd{n}" for n in ("", "g", "5")],
    "high": ["xT0h", "v0h", "k0h", "q0h0", "q0h1"], "exps": [f"e{n}{h}" for n in SOFT for h in (0, 1)],
    "turned_out": [f"pt{n}h{h}" for n in SOFT for h in (0, 1)], "packed_out": ["qT1", "qT3"],
    "var": [f"var{n}" for n in range(5)], "ln": [f"ln{n}" for n in range(5)],
    "xT": [f"xT{n}" for n in range(1, 5)], "b_var": [f"b_var{n}" for n in ("", "g", "5")],
    "rotated": ["k0r", "q0r0", "q0r1"], "split": ["xT0", "v0", "kv0_out", "q0_out0", "q0_out1"],
    "maxima": [f"s{n}m{h}" for n in SOFT for h in (0, 1)], "normed0": ["n00", "n01"],
    "probs_low": [f"pt{n}" for n in SOFT], "packed": ["pk1", "pk3"], "packed_turned": ["qkT1", "qkT3"],
    "attended": ["a1", "aT1"], "head_sums": ["mem_out", "pv3a_out"],
    "b_rows": ["b_ln", "b_a", "b_ln5"], "b_columns": ["b_xT", "b_aT", "b_xT5"],
}
MEMBER = {m: (f, k, len(ms)) for f, ms in FAMILIES.items() for k, m in enumerate(ms)}


def at(name, it, u):
    _, k, uses = MEMBER.get(name, (name, 0, 1))
    return it * uses + (k + 1)


TURNS = NSEQ // 2
TENSOR_TURN = """
1:a31 0:a0 1:a32 1:a33 0:a1a 0:a1b 0:a1c 0:a20 1:T00 1:T01 0:a21 0:a22 0:a23 1:a50 1:a51 1:a52 0:a3m 0:a30
0:a31 0:a32 1:a53 0:a33 1:a60 1:a61 0:T00 0:T01 1:tr1 1:a7 0:a50 0:a51 0:a52 0:a53 1:pk1 0:a60 1:c10 1:c11
0:a61 1:T10 1:T11 0:tr1 0:a7 1:pv1 1:atr 1:prj 0:pk1 0:c10 0:c11 1:tr2 1:a15 0:T10 0:T11 1:a16 1:a17 0:pv1
0:atr 1:tr3 0:prj 1:a19 0:tr2 0:a15 1:pk3 0:a16 0:a17 1:memp 1:c3a0 1:c3a1 0:tr3 0:a19 1:T3a0 1:T3a1 1:pv3a
1:c3b0 1:c3b1 0:pk3 0:memp 1:T3b0 0:c3a0 1:T3b1 0:c3a1 1:pv3b 0:T3a0 0:T3a1 1:tr4 1:mx1 0:pv3a 1:mx2 0:c3b0
0:c3b1 0:T3b0 1+a0 0:T3b1 1+a1a 1+a1b 0:pv3b 1+a1c 1+a20 1+a21 1+a22 0:tr4 1+a23 0:mx1 0:mx2 1+a3m 1+a30
"""
SCALAR_TURN = """
0:rs0 0:a0s 1:e00 1:e01 0:v0h 0:k0h 1:h00 1:h01 0:qh0 0:qh1 1:o0a 0:e00 0:e01 1:rs1 0:h00 0:h01 1:rq 1:rk
0:o0a 1:qT1 1:e10 1:e11 0:rs1 1:h10 1:h11 0:rq 0:rk 0:qT1 1:rs2 0:e10 0:e11 1:a15s 0:h10 0:h11 1:rs3 0:rs2
1:a19s 0:a15s 1:qT3 0:rs3 1:e3a0 1:e3a1 1:h3a0 1:h3a1 0:a19s 0:qT3 1:e3b0 1:e3b1 1:h3b0 1:h3b1 0:e3a0 0:e3a1
1:rs4 0:h3a0 0:h3a1 1:a31s 0:e3b0 1+rs0 0:e3b1 1+a0s 0:h3b0 0:h3b1 1+v0h 1+k0h 0:rs4 0:a31s 1+qh0 1+qh1
"""
VECTOR_TURN = """
0:l0 0:n0 1:s00 0:a0v 1:s01 1:n00 1:n01 0:k0 0:v0 0:k0l 1:l00 1:l01 0:q1 0:q2 0:q3 0:q4 0:ql0 0:ql1 0:s00
1:o0b 0:s01 0:n00 0:n01 1:a6v 1:n1 0:l00 1:xT1 0:l01 1:a7v 1:a7q 1:a7k 0:o0b 1:a8 1:s10 1:s11 0:a6v 0:n1
1:l10 0:xT1 1:l11 0:a7v 1:a11 1:a12 0:a7q 0:a7k 1:a13 0:a8 1:n2 0:s10 0:s11 1:xT2 1:a15v 1:a15t 0:l10 1:a16v
0:l11 1:a17v 0:a11 1:n3 0:a12 1:xT3 0:a13 1:a19v 0:n2 0:xT2 0:a15v 1:a19e 0:a15t 0:a16v 1:pk3v 0:a17v 1:mv
0:n3 1:s3a0 0:xT3 1:s3a1 0:a19v 1:l3a0 1:l3a1 1:a22a 0:a19e 1:s3b0 1:s3b1 0:pk3v 0:mv 0:s3a0 1:l3b0 1:l3b1
0:s3a1 1:a22b 1:n4 0:l3a0 1:xT4 0:l3a1 0:a22a 1:a31v 1:a32v 0:s3b0 1+l0 0:s3b1 1+n0 1+a0v 0:l3b0 0:l3b1 1+k0
0:a22b 1+v0 0:n4 1+k0l 1+q1 0:xT4 1+q2 1+q3 1+q4 1+ql0 1+ql1 0:a31v 0:a32v
"""


def all_turns(eng, own, order, stages, turn):
    order = [(int(item[0]), item[1] == "+", item[2:]) for item in order.split()]
    assert sorted((u, name) for u, _, name in order) == sorted((u, n) for u in (0, 1) for n in stages)
    turn[1] = 0
    for u, ahead, name in order:
        if ahead:
            stages[name](u)
    with eng.Fori(0, TURNS - 1) as it:
        own.enter(it)
        for u, ahead, name in order:
            turn[u] = it + 1 if ahead else it
            stages[name](u)
        own.leave(TURNS - 1)
    for u, ahead, name in order:
        if not ahead:
            turn[u] = TURNS - 1
            stages[name](u)


def program(nc, a, out):
    with ExitStack() as ctx:
        def sb(name, shape, dt=F32):
            return ctx.enter_context(nc.sbuf_tensor(name, shape, dt))

        def sem(name):
            return ctx.enter_context(nc.semaphore(name))

        sigs = {}

        def sig(name, u=""):
            name = f"{MEMBER.get(name, (name,))[0]}{u}"
            if name not in sigs:
                sigs[name] = sem("s_" + name)
            return sigs[name]

        def two(name, shape, dt=F32):
            return [sb(f"{name}{u}", shape, dt) for u in range(2)]

        PS = [ctx.enter_context(nc.psum_tensor(f"ps{u}", [P, 4, 512], F32)) for u in range(2)]

        ident = sb("ident", [P, P])
        identb, identm = sb("identb", [P, P], H16), sb("identm", [P, P], BF16)
        cosI, sinI = sb("cosI", [P, 512]), sb("sinI", [P, 512])
        mask = sb("mask", [P, NBLK * 64], BF16)
        sinkT = sb("sinkT", [P, 32])
        eps = sb("eps", [P, 4])
        decay = sb("decay", [P, 2, T])
        iota8 = sb("iota8", [P, NE])
        b0, spread = sb("b0", [64, 1152], H16), sb("spread", [64, 1152], H16)
        rows = sb("rows", [P, 9, DM])
        BO, QB, KB, VB, OB, NQ, NK_, GAM, BET = range(9)
        rb = sb("rb", [P, E0])
        wq_h, wq_l = sb("wq_h", [P, KT_, 2048], H16), sb("wq_l", [P, KT_, 2048], H16)
        wk_h, wk_l = sb("wk_h", [P, KT_, 512], H16), sb("wk_l", [P, KT_, 512], H16)
        wv_h, wv_l = sb("wv_h", [P, KT_, 512], H16), sb("wv_l", [P, KT_, 512], H16)
        wo = sb("wo", [P, 16, DM])
        wx = sb("wx", [P, 4, KT_, DM])
        rw = sb("rw", [P, KT_, E0])
        ebias = sb("ebias", [E0, DM])
        wm = sb("wm", [P, KT_, 384])
        mem = sb("mem", [P, 65])
        memw = sb("memw", [P, 4])
        wh = sb("wh", [P, 2, P])
        wgo = sb("wgo", [P, 2, KT_, DM])
        gw = sb("gw", [P, KT_, NE])
        acc = sb("acc", [P, 2, T])
        mixT = sb("mixT", [P, 2, T])
        xall = sb("xall", [P, NSEQ, DM])
        vall = sb("vall", [P, NSEQ, 2, P])

        xin, cin = two("xin", [P, DM]), two("cin", [P, DM])
        xr, xn = two("xr", [P, DM]), two("xn", [P, DM])
        bst, mv, rstd = two("bst", [P, 6]), two("mv", [P, 2]), two("rstd", [P, 6])
        xT_h, xT_l = two("xT_h", [P, KT_, 160], H16), two("xT_l", [P, KT_, 160], H16)
        xT, cT = two("xT", [P, KT_, T]), two("cT", [P, KT_, T])
        big = two("big", [P, 2048])
        qhl = two("qhl", [P, 2048])
        q_h = [b[:, 0:1024].bitcast(H16) for b in qhl]
        q_l = [b[:, 1024:2048].bitcast(H16) for b in qhl]
        k_h, k_l = two("k_h", [P, 4, 160], H16), two("k_l", [P, 4, 160], H16)
        kf = two("kf", [P, 2, 512])
        v_h, v_l = two("v_h", [P, 1024], H16), two("v_l", [P, 1024], H16)
        ptf = two("ptf", [P, 2048])
        pt_h = [b[:, 0:1024].bitcast(H16) for b in ptf]
        pt_l = [b[:, 1024:2048].bitcast(H16) for b in ptf]
        st32 = two("st32", [P, 4, 32])
        qf = [b[:, 0:DM] for b in big]
        kvf = [b[:, DM:3 * DM].rearrange("p (a d) -> p a d", a=2) for b in big]
        af2 = [b[:, 3 * DM:4 * DM] for b in big]
        qp, kp = v_h, v_l
        vp1 = [two(f"vp1{p}", [P, NHX, DHX + 1], H16) for p in "hl"]
        vp3 = [two(f"vp3{p}", [P, NHM, DHM + 1], H16) for p in "hl"]
        af = two("af", [P, DM])
        aT = two("aT", [P, KT_, T])
        lg, wt = two("lg", [P, 2, E0]), two("wt", [P, T])
        sm = two("sm", [P, 16])

        A = a

        n_consts = 14 + 2 + 9 + 3

        def ps_f(u, b, w=512, o=0):
            return PS[u][:, b, o:o + w]

        def psb(u, b):
            return PS[u][:, b, :].bitcast(H16)

        ps_all = [PS[u][:, :, :].rearrange("p b n -> p (b n)") for u in range(2)]

        def q_table(t, n):
            return t[:, None, :].to_broadcast([P, n, 512])

        def k_table(t, n):
            v = t[:]
            return bass.AP(v.tensor, v.offset, [v.ap[0], [0, n], [G0 * WIN, NBLK], [1, WIN]])

        def by_block(u):
            return ps_all[u].rearrange("p (i k r) -> p k i r", i=NBLK, r=WIN)

        def by_token(b):
            return b.rearrange("p (k i r) -> p k i r", i=NBLK, r=WIN)

        def head_at(j, tiles):
            return tiles * (j % (16 // tiles)) + j // (16 // tiles)

        def apart(eng):
            eng.sem_inc(sig("apart"), 1)

        class Own:

            def __init__(self, eng, name, per_turn=None):
                self.eng, self.sem, self.n = eng, sig(name), 0
                self.per_turn, self.it, self.base = per_turn, None, 0

            def value(self):
                return self.base + self.n if self.it is None else self.it * self.per_turn + (self.base + self.n)

            def mark(self, ins):
                ins.then_inc(self.sem, 1)
                self.n += 1

            def wait(self):
                self.eng.wait_ge(self.sem, self.value())

            def link(self, ins):
                self.mark(ins)
                self.wait()

            def enter(self, it):
                self.base, self.n, self.it = self.base + self.n, 0, it

            def leave(self, turns):
                assert self.n == self.per_turn, (self.sem, self.n, self.per_turn)
                self.base, self.n, self.it = self.base + turns * self.per_turn, 0, None

        PER = {"act": 18, "dve": 212, "act_b": 12, "dve_b": 80, "dve_c": 26}

        xa_h, xa_l = wq_h, wq_l
        cw = sb("cw", [P, NSEQ, NE])
        gate_w = sb("gate_w", [P, 2, NSEQ])
        ecw = two("ecw", [P, NSEQ])
        logits = sb("logits", [P, NSEQ, NE])
        gu_f = [b[:] for b in big]
        dn_f = [b[:, 0:1024] for b in qhl]
        v32 = vall[:].rearrange("p b h e -> p (b h e)")
        wo32 = wo[:].rearrange("p k n -> p (k n)")
        eh = [wo32[:, 0:1536].bitcast(H16), v32[:, 0:1536].bitcast(H16)]
        el = [wo32[:, 1536:3072].bitcast(H16), v32[:, 1536:3072].bitcast(H16)]
        NBLKC, TB = 4, 512
        sil = [kf[s][:, 0, :] for s in range(2)]
        prod = [kf[s][:, 1, :] for s in range(2)]

        def order_c(hidden, down):
            for n in range(2 * NBLKC + 1):
                if n < 2 * NBLKC:
                    hidden(n)
                if n >= 1:
                    down(n - 1)

        BTURNS = NSEQ // 4

        def four(bufs, lo, w):
            return [x[:] for x in bufs] + [x[:, lo:lo + w] for x in ptf]
        xr_b, xn_b, af_b = four(xr, 0, DM), four(xn, 256, DM), four(af, 512, DM)
        v_b = [x[:, 0:DM] for x in big] + [x[:, 768:1024] for x in ptf]
        xT_b, aT_b = [four([x[:].rearrange("p k t -> p (k t)") for x in bufs], lo, DM)
                      for bufs, lo in ((xT, 1024), (aT, 1280))]
        bst_b, mv_b, rstd_b = four(bst, 1536, 6), four(mv, 1544, 2), four(rstd, 1552, 6)

        def ps_b(u, bank, w=512, o=0):
            return PS[u // 2][:, 2 * (u % 2) + bank, o:o + w]

        def tensor_b(pe, mm, mm3):
            with pe.Fori(0, BTURNS) as it:
                def W(name, u):
                    pe.wait_ge(sig(name, u), at(name, it, u))

                def tr(u, name, ready, bank, src):
                    W(ready, u)
                    for k in range(KT_):
                        m = pe.transpose(ps_b(u, bank, P, k * P), src[u][:, k * P:(k + 1) * P], ident[:])
                    m.then_inc(sig(name, u), 1)

                def b1(u):
                    W("b_xT", u)
                    pe.wait_ge(sig("mixT"), 1)
                    for h in range(2):
                        mm(ps_b(u, 0, P, h * P), mixT[:, h, :], v_b[u][:, h * P:(h + 1) * P], True, True)
                    for k in range(KT_):
                        m = mm(ps_b(u, 0, DM, DM), xT_b[u][:, k * P:(k + 1) * P], wgo[:, 0, k, :], k == 0, k == KT_ - 1)
                    m.then_inc(sig("b_mix", u), 1)

                def b2(u):
                    W("b_aT", u)
                    for k in range(KT_):
                        m = mm(ps_b(u, 0, DM), aT_b[u][:, k * P:(k + 1) * P], wgo[:, 1, k, :], k == 0, k == KT_ - 1)
                    m.then_inc(sig("b_wo", u), 1)

                def b3(u):
                    W("b_xT5", u)
                    for k in range(KT_):
                        m = mm(ps_b(u, 0, NE), xT_b[u][:, k * P:(k + 1) * P], gw[:, k, :], k == 0, k == KT_ - 1)
                    m.then_inc(sig("b_gate", u), 1)

                for s in (lambda u: tr(u, "b_tr", "b_ln", 1, xn_b), b1, lambda u: tr(u, "b_atr", "b_a", 1, af_b), b2,
                          lambda u: tr(u, "b_tr5", "b_ln5", 1, xn_b), b3):
                    for u in range(4):
                        s(u)

            pe.wait_ge(sig("w0_lo"), 1)
            for u in range(4):
                pe.wait_ge(sig("xa_lo", u), BTURNS)
            pe.sem_inc(sig("c_down"), 1)
            with pe.Fori(0, NE // 2) as it:
                def hidden(n):
                    p, j = n // NBLKC, n % NBLKC
                    if j == 0:
                        pe.wait_ge(sig(f"w{p}_lo"), it + 1)
                    gh, gl = [w[p][:, 0:2048].rearrange("p (k n) -> p k n", k=KT_) for w in (eh, el)]
                    tok = slice(j * TB, (j + 1) * TB)
                    for i in range(4):
                        q = n * 4 + i
                        pe.wait_ge(sig("c_prod"), it * 32 + max(q - 1, 0) + 1)
                        for g in range(2):
                            c = slice(g * NI + i * P, g * NI + (i + 1) * P)
                            for k in range(KT_):
                                m = mm3(ps_f(0, 2 * (q % 2) + g), gh[:, k, c], gl[:, k, c],
                                        xa_h[:, k, tok], xa_l[:, k, tok], k == 0, k == KT_ - 1)
                        m.then_inc(sig("c_hid"), 1)

                def down(n):
                    p, m_ = n // NBLKC, n % 2
                    dh, dl = [w[p][:, 2048:3072].rearrange("p (k n) -> p k n", k=4) for w in (eh, el)]
                    pe.wait_ge(sig("c_hl"), it * 32 + 4 * n + 5)
                    pe.wait_ge(sig("c_acc"), it * 8 + max(n - 1, 0) + 1)
                    for t in range(4):
                        o = ps_f(1, 2 * m_ + t // 2, DM, (t % 2) * DM)
                        for i in range(4):
                            c = slice(i * TB + t * P, i * TB + (t + 1) * P)
                            m = mm3(o, pt_h[m_][:, c], pt_l[m_][:, c], dh[:, i, :], dl[:, i, :], i == 0, i == 3)
                    m.then_inc(sig("c_down"), 1)

                order_c(hidden, down)

        def scalar_b(act, own, f):
            own_b = Own(act, "act_own_b", PER["act_b"])
            with act.Fori(0, BTURNS) as it:
                own_b.enter(it)

                def W(name, u):
                    act.wait_ge(sig(name, u), at(name, it, u))

                def rs(u, n, e=0):
                    W(f"b_var{n}", u)
                    own_b.link(f(rstd_b[u][:, 0:1], mv_b[u][:, 1:2], ACT.Ln, bias=eps[:, e:e + 1]))
                    f(rstd_b[u][:, 0:1], rstd_b[u][:, 0:1], ACT.Exp, scale=-0.5).then_inc(sig(f"b_rstd{n}", u), 1)

                def hi(u):
                    W("b_tr5", u)
                    f(xa_h[:].rearrange("p k (i u t) -> p k i u t", i=BTURNS, u=4)[:, :, bass.ds(it, 1), u, :]
                      .rearrange("p k o t -> p k (o t)"),
                      ps_b(u, 1, DM).rearrange("p (k t) -> p k t", k=2), ACT.Copy).then_inc(sig("xa_hi", u), 1)

                for s in (lambda u: rs(u, ""), lambda u: rs(u, "g", 2), lambda u: rs(u, "5"), hi):
                    for u in range(4):
                        s(u)
                own_b.leave(BTURNS)

            def w_high(p, count):
                act.wait_ge(sig(f"w{p}_in"), count * 32)
                f(eh[p][:, 0:2048], gu_f[p], ACT.Copy)
                f(eh[p][:, 2048:3072], dn_f[p], ACT.Copy).then_inc(sig(f"w{p}_hi"), 1)
            w_high(0, 1)
            act.wait_ge(sig("gate_gap"), 1)
            f(gate_w[:, 0], gate_w[:, 0], ACT.Exp).then_inc(sig("gate_exp"), 1)
            with act.Fori(0, NE // 2) as it:
                def hidden(n):
                    for i in range(4):
                        q = n * 4 + i
                        act.wait_ge(sig("c_hid"), it * 32 + q + 1)
                        f(sil[q % 2], ps_f(0, 2 * (q % 2)), ACT.Silu).then_inc(sig("c_silu"), 1)
                        act.wait_ge(sig("c_prod"), it * 32 + q + 2)
                        if i == 0:
                            act.wait_ge(sig("c_down"), it * 8 + max(n - 1, 0) + 1)
                        f(pt_h[n % 2][:, i * TB:(i + 1) * TB], prod[q % 2], ACT.Copy).then_inc(sig("c_hh"), 1)
                    if n == 0:
                        act.wait_ge(sig("c_down"), it * 8 + 1)
                        w_high(1, it + 1)
                    if n == 5:
                        act.wait_ge(sig("c_down"), it * 8 + 4 + 1)
                        w_high(0, it + 2)

                order_c(hidden, lambda n: None)

        def vector_b(dve, own, prepare, refine):
            tt, ts, cp, red = dve.tensor_tensor, dve.tensor_scalar, dve.tensor_copy, dve.tensor_reduce
            stt = dve.scalar_tensor_tensor
            accf = acc[:].rearrange("p h t -> p (h t)")
            own.link(tt(accf, accf, decay[:].rearrange("p h t -> p (h t)"), ALU.mult))
            mixf = mixT[:].rearrange("p h t -> p (h t)")
            own.link(stt(mixf, accf, -1.0, accf, ALU.mult, ALU.max))
            ts(mixf, mixf, 1.0, None, ALU.max).then_inc(sig("mixT"), 1)
            own_b = Own(dve, "dve_own_b", PER["dve_b"])
            link, mark = own_b.link, own_b.mark
            xs = xall[:].rearrange("p (i u) d -> p i u d", u=4)
            vs = vall[:].rearrange("p (i u) h e -> p i u (h e)", u=4)
            gates = logits[:].rearrange("p (i u) e -> p i u e", u=4)
            with dve.Fori(0, BTURNS) as it:
                own_b.enter(it)
                own = own_b

                def W(name, u):
                    dve.wait_ge(sig(name, u), at(name, it, u))

                def S(u, ins, name):
                    ins.then_inc(sig(name, u), 1)

                def stats(u, n, x):
                    link(dve.bn_stats(bst_b[u], x))
                    apart(dve)
                    S(u, dve.bn_aggr(mv_b[u], bst_b[u]), f"b_var{n}")
                    W(f"b_var{n}", u)
                    prepare(mark, rstd_b[u], mv_b[u][:, 1:2], 1.0, EPS_GN if n == "g" else EPS_LN)

                def norm(u, n, x):
                    W(f"b_rstd{n}", u)
                    refine(own_b, rstd_b[u])
                    return ts(xn_b[u], x, mv_b[u][:, 0:1], rstd_b[u][:, 0:1], ALU.subtract, ALU.mult)

                def b0(u):
                    apart(dve)
                    link(cp(xr_b[u][:, None, :], xs[:, bass.ds(it, 1), u, :]))
                    stats(u, "", xr_b[u])

                def b0n(u):
                    S(u, norm(u, "", xr_b[u]), "b_ln")

                def b1(u):
                    W("b_tr", u)
                    apart(dve)
                    mark(cp(v_b[u][:, None, :], vs[:, bass.ds(it, 1), u, :]))
                    S(u, cp(xT_b[u], ps_b(u, 1, DM)), "b_xT")

                def b2(u):
                    W("b_mix", u)
                    stats(u, "g", ps_b(u, 0, DM))

                def b2n(u):
                    link(norm(u, "g", ps_b(u, 0, DM)))
                    link(tt(xn_b[u], xn_b[u], rows[:, GAM, :], ALU.mult))
                    link(tt(xn_b[u], xn_b[u], rows[:, BET, :], ALU.add))
                    S(u, stt(af_b[u], ps_b(u, 0, DM, DM), 0.0, xn_b[u], ALU.max, ALU.mult), "b_a")

                def b3(u):
                    W("b_atr", u)
                    S(u, cp(aT_b[u], ps_b(u, 1, DM)), "b_aT")

                def b4(u):
                    W("b_wo", u)
                    link(tt(xr_b[u], ps_b(u, 0, DM), xr_b[u], ALU.add))
                    apart(dve)
                    mark(cp(xs[:, bass.ds(it, 1), u, :], xr_b[u][:, None, :]))
                    stats(u, "5", xr_b[u])

                def b4n(u):
                    S(u, norm(u, "5", xr_b[u]), "b_ln5")

                def b5(u):
                    W("xa_hi", u)
                    S(u, cp(xT_b[u], ps_b(u, 1, DM)), "b_xT5")
                    v = [b[:].rearrange("p k (i u t) -> p k i u t", i=BTURNS, u=4)[:, :, bass.ds(it, 1), u, :]
                         .rearrange("p k o t -> p k (o t)") for b in (xa_l, xa_h)]
                    S(u, tt(v[0], ps_b(u, 1, DM).rearrange("p (k t) -> p k t", k=2), v[1], ALU.subtract), "xa_lo")

                def b6(u):
                    W("b_gate", u)
                    apart(dve)
                    mark(cp(gates[:, bass.ds(it, 1), u, :], ps_b(u, 0, NE)[:, None, :]))

                for s in (b0, b0n, b1, b2, b2n, b3, b4, b4n, b5, b6):
                    for u in range(4):
                        s(u)
                own_b.leave(BTURNS)

            own_b.wait()
            link = own_b.link
            shape = [P, NSEQ, NE]
            quarters = [af[n // 2][:, P * (n % 2):P * (n % 2) + P] for n in range(4)]
            picked, rest, where, second = [q.rearrange("p (b e) -> p b e", e=NE) for q in quarters]
            best, place_, best2, one = [st32[0][:, n, 0:NSEQ] for n in range(4)]

            def wide(v):
                return v[:, :, None].to_broadcast(shape)

            iota = iota8[:, None, :].to_broadcast(shape)

            def first_largest(of, value, chosen):
                link(red(value, of, AX.X, ALU.max))
                link(tt(where, of, wide(value), ALU.is_equal))
                link(stt(where, where, -float(NE), iota, ALU.mult, ALU.add))
                link(red(place_, where, AX.X, ALU.min))
                link(ts(place_, place_, float(NE), None, ALU.add))
                link(tt(chosen, iota, wide(place_), ALU.is_equal))
            first_largest(logits[:], best, picked)
            link(stt(rest, picked, MASKED, logits[:], ALU.mult, ALU.add))
            first_largest(rest, best2, second)
            tt(gate_w[:, 0], best2, best, ALU.subtract).then_inc(sig("gate_gap"), 1)
            dve.wait_ge(sig("gate_exp"), 1)
            link(ts(one, gate_w[:, 0], 1.0, None, ALU.add))
            link(dve.reciprocal(gate_w[:, 1], one))
            link(tt(one, gate_w[:, 1], gate_w[:, 0], ALU.mult))
            own_b.mark(tt(picked, picked, wide(gate_w[:, 1]), ALU.mult))
            link(tt(second, second, wide(one), ALU.mult))
            link(tt(cw[:], picked, second, ALU.add))

            def w_low(p, count):
                dve.wait_ge(sig(f"w{p}_hi"), count)
                tt(el[p][:, 0:2048], gu_f[p], eh[p][:, 0:2048], ALU.subtract)
                tt(el[p][:, 2048:3072], dn_f[p], eh[p][:, 2048:3072], ALU.subtract).then_inc(sig(f"w{p}_lo"), 1)
            w_low(0, 1)
            own_c = Own(dve, "dve_own_c", PER["dve_c"])
            cwe = cw[:].rearrange("p b (i g) -> p b i g", g=2)
            for name in ("c_prod", "c_acc"):
                dve.sem_inc(sig(name), 1)
            with dve.Fori(0, NE // 2) as it:
                own_c.enter(it)
                dve.wait_ge(sig("c_acc"), it * 8 + 1)
                apart(dve)
                for g in range(2):
                    own_c.mark(cp(ecw[g][:, :, None], cwe[:, :, bass.ds(it, 1), g]))
                own_c.wait()

                def hidden(n):
                    for i in range(4):
                        q = n * 4 + i
                        dve.wait_ge(sig("c_silu"), it * 32 + q + 1)
                        dve.wait_ge(sig("c_hl"), it * 32 + max(q - 1, 0) + 1)
                        tt(prod[q % 2], sil[q % 2], ps_f(0, 2 * (q % 2) + 1), ALU.mult).then_inc(sig("c_prod"), 1)
                    if n == 0:
                        w_low(1, it + 1)
                    if n == 5:
                        w_low(0, it + 2)

                def down(n):
                    p, j = n // NBLKC, n % NBLKC
                    dve.wait_ge(sig("c_down"), it * 8 + n + 2)
                    for t in range(4):
                        b = 4 * j + t
                        last = stt(xall[:, b, :], ps_f(1, 2 * (n % 2) + t // 2, DM, (t % 2) * DM),
                                   ecw[p][:, b:b + 1], xall[:, b, :], ALU.mult, ALU.add)
                        if t < 3:
                            own_c.mark(last)
                        else:
                            last.then_inc(sig("c_acc"), 1)

                order_c(hidden, down)
                own_c.leave(NE // 2)

        def pool_b(pool):
            pool.sem_inc(sig("c_hl"), 1)
            with pool.Fori(0, NE // 2) as it:
                def hidden(n):
                    for i in range(4):
                        q = n * 4 + i
                        pool.wait_ge(sig("c_hh"), it * 32 + q + 1)
                        c = slice(i * TB, (i + 1) * TB)
                        pool.tensor_tensor(pt_l[n % 2][:, c], prod[q % 2], pt_h[n % 2][:, c],
                                           ALU.subtract).then_inc(sig("c_hl"), 1)
                order_c(hidden, lambda n: None)

        def sync_b(sp):
            def load(p, e):
                sp.dma_start(gu_f[p], A["gu"][e]).then_inc(sig(f"w{p}_in"), 16)
                sp.dma_start(dn_f[p], A["dn"][e]).then_inc(sig(f"w{p}_in"), 16)
            for u in range(4):
                sp.wait_ge(sig("b_mix", u), at("b_mix", BTURNS - 1, u))
            load(0, 0)
            load(1, 1)
            for it in range(NE // 2):
                if it == 0:
                    sp.wait_ge(sig("w0_lo"), 1)
                    load(0, 2)
                if it + 1 < NE // 2:
                    sp.wait_ge(sig("w1_lo"), it + 1)
                    load(1, 2 * it + 3)
                    sp.wait_ge(sig("w0_lo"), it + 2)
                    load(0, (2 * it + 4) % NE)
            sp.wait_ge(sig("c_acc"), 8 * NE // 2 + 1)
            sp.dma_start(out.rearrange("b t d -> t b d"), xall[:]).then_inc(sig("stored"), 16)
            sp.wait_ge(sig("stored"), 16)

        block = ctx.enter_context(nc.Block())

        @block.sync
        def _(sp):
            def load(dst, src, name="consts"):
                sp.dma_start(dst, src).then_inc(sig(name), 16)
            for u in range(2):
                sp.dma_start(xin[u][:], A["x"][u]).then_inc(sig(f"x_in{u}"), 16)
                sp.dma_start(cin[u][:], A["ctx"][u]).then_inc(sig(f"x_in{u}"), 16)
            load(big[0][:], A["wq"][:, 0, :], "w_in")
            load(big[1][:], A["wq"][:, 1, :], "w_in")
            load(kf[0][:], A["wk"], "w_in")
            load(kf[1][:], A["wv"], "w_in")
            load(ptf[0][0:64, 0:1152], A["b0"], "w_in")
            load(ptf[1][0:64, 0:1152], A["spread"], "w_in")
            consts = [(ident, "ident"), (cosI, "cosI"), (sinI, "sinI"), (sinkT, "sinkT"),
                      (decay, "decay"), (iota8, "iota8"), (wo, "wo"), (wx, "wx"), (rw, "rw"),
                      (ebias, "ebias"), (wm, "wm"), (wh, "wh"), (wgo, "wgo"), (gw, "gw")]
            for t, n in consts:
                load(t[:], A[n])
            load(mem[0:64, :], A["mem"])
            load(mem[64:128, :], A["mem"])
            for i in range(9):
                load(rows[:, i, :], A["rows"][i:i + 1, :].to_broadcast([P, DM]))
            load(xn[0][:], A["mask"])
            load(rb[:], A["rb"].to_broadcast([P, E0]))
            load(memw[:, 0:1], A["memw"].to_broadcast([P, 1]))
            assert len(consts) + 2 + 9 + 3 == n_consts
            xs = A["x"].rearrange("(i u) p d -> i u p d", u=2)
            cs = A["ctx"].rearrange("(i u) p d -> i u p d", u=2)
            with sp.Fori(0, NSEQ // 2 - 1) as it:
                for u in range(2):
                    sp.wait_ge(sig("ln0", u), at("ln0", it, u))
                    sp.wait_ge(sig("tr0", u), at("tr0", it, u))
                    nx = bass.ds(it + 1, 1)
                    sp.dma_start(xin[u][:], xs[nx, u].rearrange("o p d -> (o p) d")).then_inc(sig(f"x_in{u}"), 16)
                    sp.dma_start(cin[u][:], cs[nx, u].rearrange("o p d -> (o p) d")).then_inc(sig(f"x_in{u}"), 16)
            sync_b(sp)

        @block.tensor
        def _(pe):
            def mm(o, l, r, start, stop):
                return pe.matmul(o, l, r, start=start, stop=stop)

            def add(o, l, r, start=False):
                return pe.matmul(o, l, r, start=start, stop=False, skip_group_check=True)

            def add3(o, lh, ll, rh, rl):
                add(o, lh, rh)
                add(o, ll, rh)
                return add(o, lh, rl)

            def mm3(o, lh, ll, rh, rl, start=True, stop=True):
                mm(o, lh, rh, start, False)
                mm(o, ll, rh, False, False)
                return mm(o, lh, rl, False, stop)

            pe.wait_ge(sig("consts"), 16 * n_consts)
            pe.wait_ge(sig("w_ready"), 3)
            turn = [None, None]
            def W(name, u):
                pe.wait_ge(sig(name, u), at(name, turn[u], u))

            def transposes_x(u, name, bank, src, ready):
                W(ready, u)
                for k in range(KT_):
                    m = pe.transpose(ps_f(u, bank, P, k * P), src[u][:, k * P:(k + 1) * P], ident[:])
                m.then_inc(sig(name, u), 1)

            def a0(u):
                W("ln0", u)
                pe.wait_ge(sig(f"x_in{u}"), turn[u] * 32 + 32)
                for k in range(KT_):
                    pe.transpose(ps_f(u, 0, P, k * P), xn[u][:, k * P:(k + 1) * P], ident[:])
                    m = pe.transpose(ps_f(u, 0, P, 256 + k * P), cin[u][:, k * P:(k + 1) * P], ident[:])
                m.then_inc(sig("tr0", u), 1)

            def keys(u):
                W("xT0", u)
                add(ps_f(u, 1), b0[:, 512:640], spread[:, 512:1024], True)
                for t in range(4):
                    for k in range(KT_):
                        c = slice(t * P, (t + 1) * P)
                        m = add3(ps_f(u, 1, P, t * P), wk_h[:, k, c], wk_l[:, k, c],
                                 xT_h[u][:, k, 32:160], xT_l[u][:, k, 32:160])
                m.then_inc(sig("keys0", u), 1)

            def values(u, p):
                add(ps_f(u, 2 + p), spread[:, 1024:1152], b0[:, 640:1152], True)
                for k in range(KT_):
                    c = slice(k * 256 + p * P, k * 256 + (p + 1) * P)
                    m = add3(ps_f(u, 2 + p), q_h[u][:, c], q_l[u][:, c], wv_h[:, k, :], wv_l[:, k, :])
                if p == 1:
                    m.then_inc(sig("kv0", u), 1)

            def queries(u, b):
                if b == 1:
                    W("k0r", u)
                if b == 2:
                    W("v0", u)
                add(ps_f(u, b), b0[:, b * P:(b + 1) * P], spread[:, 0:512], True)
                for t in range(4 * b, 4 * b + 4):
                    o = ps_f(u, t // 4).rearrange("p (i g r) -> p g i r", i=NBLK, g=G0)[:, t % 4]
                    for k in range(KT_):
                        c = slice(t * P, (t + 1) * P)
                        m = add3(o, wq_h[:, k, c], wq_l[:, k, c], xT_h[u][:, k, 32:160], xT_l[u][:, k, 32:160])
                if b % 2 == 1:
                    m.then_inc(sig("q0" + "ab"[b // 2], u), 1)

            def masks(u):
                W("q0r0", u)
                for b in range(4):
                    for hf in range(2):
                        add(ps_f(u, b, 256, hf * 256), identm[:], mask[:], hf == 0)

            def scores0(u, part):
                pair, hf = part // 2, part % 2
                if pair == 0:
                    if hf == 0:
                        W("kv0_out", u)
                    W(f"q0_out{hf}", u)
                qv = [b[u].rearrange("p (a h i m) -> p a h i m", a=2, h=2, i=NBLK) for b in (q_h, q_l)]
                for i in range(NBLK):
                    for kvl in (2 * pair, 2 * pair + 1):
                        r = slice(32 * kvl, 32 * kvl + 32)
                        o = ps_f(u, kvl, 64, hf * 256 + i * 64)
                        for ab in range(2):
                            q1, q2 = [v[r, ab, hf, i, :] for v in qv]
                            k1, k2 = [b[u][r, ab * 2 + hf, 32 * i:32 * i + 64] for b in (k_h, k_l)]
                            m = add3(o, q1, q2, k1, k2)
                if hf == 1:
                    m.then_inc(sig(f"s0p{pair}", u), 1)

            def p_transposes(u, n, h):
                W(f"n0{h}" if n == "0" else f"e{n}{h}", u)
                for j in range(8 * h, 8 * h + 8):
                    m = pe.transpose(ps_f(u, j // 4, P, (j % 4) * P), big[u][:, j * P:(j + 1) * P], ident[:])
                m.then_inc(sig(f"pT{n}{h}", u), 1)

            def weighted0(u, kvl):
                if kvl == 0:
                    W("pt0", u)
                    W("v0", u)
                    apart(pe)
                for hf in range(2):
                    kvp, par = hf * 2 + kvl // 2, kvl % 2
                    kv = hf * 4 + kvl
                    for i in range(NBLK):
                        ip, i2 = i // 2, i % 2
                        blk = (kvl * 2 + hf) * 2 + ip
                        r = slice(64 * i2, 64 * i2 + 64)
                        o = PS[u][64 * par:64 * par + 64, i, kvp * P:(kvp + 1) * P]
                        c = slice(ip * 512 + kv * 64, ip * 512 + kv * 64 + 64)
                        m = mm3(o, v_h[u][r, c], v_l[u][r, c], pt_h[u][r, blk * P:(blk + 1) * P],
                                pt_l[u][r, blk * P:(blk + 1) * P])
                if kvl == 3:
                    m.then_inc(sig("pv0", u), 1)

            def projected0(u, half):
                if half == 0:
                    W("o0a", u)
                    W("o0b", u)
                for t in range(8 * half, 8 * half + 8):
                    m = mm(ps_f(u, 0, DM), qhl[u][:, t * P:(t + 1) * P], wo[:, t, :], t == 0, t == 15)
                if half == 1:
                    m.then_inc(sig("wo0", u), 1)

            def a7(u):
                W("xT1", u)
                for i, src in enumerate((xT, cT, cT)):
                    o = ps_f(u, i // 2, DM, (i % 2) * DM)
                    for k in range(KT_):
                        m = mm(o, src[u][:, k, :], wx[:, i, k, :], k == 0, k == KT_ - 1)
                m.then_inc(sig("qkv1", u), 1)

            def pack_transposes(u, name, ready, nk):
                W(ready, u)
                for j in range(8):
                    pe.transpose(psb(u, 0)[:, j * P:(j + 1) * P], qp[u][:, j * P:(j + 1) * P], identb[:])
                for j in range(nk):
                    m = pe.transpose(psb(u, 1)[:, j * P:(j + 1) * P], kp[u][:, j * P:(j + 1) * P], identb[:])
                return m

            def scores1(u, half):
                if half == 0:
                    W("qkT1", u)
                for j in range(8 * half, 8 * half + 8):
                    h = head_at(j, 2)
                    r = slice(64 * (h % 2), 64 * (h % 2) + 64)
                    c = slice((h // 2) * P, (h // 2 + 1) * P)
                    m = mm(ps_f(u, j // 4, P, (j % 4) * P), pt_h[u][r, c], pt_l[u][r, c], True, True)
                m.then_inc(sig(f"s1p{half}", u), 1)

            def pv(u, name, ready, tiles, vp):
                nkh, dv = vp[0][u].shape[1:3]
                W(ready, u)
                for j in range(16):
                    c = slice(j * P, (j + 1) * P)
                    h = head_at(j, tiles)
                    m = mm3(ps_f(u, 0, dv, h * 32), pt_h[u][:, c], pt_l[u][:, c],
                            vp[0][u][:, h % nkh, :], vp[1][u][:, h % nkh, :])
                m.then_inc(sig(name, u), 1)

            def proj_x(u):
                W("aT1", u)
                for k in range(KT_):
                    m = mm(ps_f(u, 0, DM), aT[u][:, k, :], wx[:, 3, k, :], k == 0, k == KT_ - 1)
                m.then_inc(sig("wo1", u), 1)

            def a15(u):
                W("xT2", u)
                for k in range(KT_):
                    m = mm(ps_f(u, 0, E0), xT[u][:, k, :], rw[:, k, :], k == 0, k == KT_ - 1)
                m.then_inc(sig("rl", u), 1)

            def a16(u):
                W("rw", u)
                apart(pe)
                pe.transpose(PS[u][0:E0, 1, 0:P], lg[u][:, 0, :], ident[:]).then_inc(sig("rwT", u), 1)

            def a17(u):
                W("rwT_out", u)
                mm(ps_f(u, 0, DM), wt[u][0:E0, :], ebias[:], True, True).then_inc(sig("eb", u), 1)

            def a19(u):
                W("xT3", u)
                for k in range(KT_):
                    m = mm(ps_f(u, 0, 384), xT[u][:, k, :], wm[:, k, :], k == 0, k == KT_ - 1)
                m.then_inc(sig("qkv3", u), 1)

            def a20(u):
                pack_transposes(u, "", "pk3", 2)
                for k in range(2):
                    m = pe.transpose(ps_f(u, 2, P, k * P), af[u][:, k * P:(k + 1) * P], ident[:])
                m.then_inc(sig("tr3b", u), 1)

            def a20m(u):
                W("qkT3", u)
                for qi in range(NQM):
                    r = slice(64 * (qi % 2), 64 * (qi % 2) + 64)
                    m = mm(ps_f(u, 2 + qi % 2, 65, (qi // 2) * P), aT[u][r, qi // 2, :], mem[r, :], True, True)
                m.then_inc(sig("mem", u), 1)

            def scores3(u, sixteen, half):
                if half == 0:
                    W("mem_out" if sixteen == 0 else "pv3a_out", u)
                for j in range(8 * half, 8 * half + 8):
                    hh = 16 * sixteen + head_at(j, 4)
                    h = hh % NHM
                    r = slice(32 * (hh % 4), 32 * (hh % 4) + 32)
                    m = mm(ps_f(u, j // 4, P, (j % 4) * P), qp[u][r, (hh // 4) * P:(hh // 4 + 1) * P],
                           kp[u][r, (h // 4) * P:(h // 4 + 1) * P], True, True)
                m.then_inc(sig(f"s3{'ab'[sixteen]}p{half}", u), 1)

            def a31(u):
                W("xT4", u)
                for h in range(2):
                    mm(ps_f(u, 0, P, h * P), wh[:, h, :], xT[u][:, h, :], True, True)
                    mm(ps_f(u, 0, P, 256 + h * P), wh[:, h, :], cT[u][:, h, :], True, True)
                    m = mm(ps_f(u, 1, P, 256 + h * P), cT[u][:, h, :], wh[:, h, :], True, True)
                m.then_inc(sig("mixqkv", u), 1)

            def a32(u):
                W("mixqkv_out", u)
                for h in range(2):
                    m = mm(ps_f(u, 2, P, h * P), big[u][:, 256 + h * P:256 + (h + 1) * P],
                           big[u][:, h * P:(h + 1) * P], True, True)
                m.then_inc(sig("mixs", u), 1)

            stages = {
                "a0": a0, "a1a": keys, "a1b": lambda u: values(u, 0), "a1c": lambda u: values(u, 1),
                "a20": lambda u: queries(u, 0), "a21": lambda u: queries(u, 1), "a22": lambda u: queries(u, 2),
                "a23": lambda u: queries(u, 3), "a3m": masks, "a30": lambda u: scores0(u, 0),
                "a31": lambda u: scores0(u, 1), "a32": lambda u: scores0(u, 2), "a33": lambda u: scores0(u, 3),
                "T00": lambda u: p_transposes(u, "0", 0), "T01": lambda u: p_transposes(u, "0", 1),
                "a50": lambda u: weighted0(u, 0), "a51": lambda u: weighted0(u, 1),
                "a52": lambda u: weighted0(u, 2), "a53": lambda u: weighted0(u, 3),
                "a60": lambda u: projected0(u, 0), "a61": lambda u: projected0(u, 1),
                "tr1": lambda u: transposes_x(u, "tr1", 1, xn, "ln1"), "a7": a7,
                "pk1": lambda u: pack_transposes(u, "", "pk1", 8).then_inc(sig("qkT1p", u), 1),
                "c10": lambda u: scores1(u, 0), "c11": lambda u: scores1(u, 1),
                "T10": lambda u: p_transposes(u, "1", 0), "T11": lambda u: p_transposes(u, "1", 1),
                "pv1": lambda u: pv(u, "pv1", "pt1", 2, vp1),
                "atr": lambda u: transposes_x(u, "atr1", 1, af, "a1"), "prj": proj_x,
                "tr2": lambda u: transposes_x(u, "tr2", 1, xn, "ln2"), "a15": a15, "a16": a16, "a17": a17,
                "tr3": lambda u: transposes_x(u, "tr3", 1, xn, "ln3"), "a19": a19, "pk3": a20, "memp": a20m,
                "c3a0": lambda u: scores3(u, 0, 0), "c3a1": lambda u: scores3(u, 0, 1),
                "T3a0": lambda u: p_transposes(u, "3a", 0),
                "T3a1": lambda u: p_transposes(u, "3a", 1), "pv3a": lambda u: pv(u, "pv3a", "pt3a", 4, vp3),
                "c3b0": lambda u: scores3(u, 1, 0), "c3b1": lambda u: scores3(u, 1, 1),
                "T3b0": lambda u: p_transposes(u, "3b", 0),
                "T3b1": lambda u: p_transposes(u, "3b", 1), "pv3b": lambda u: pv(u, "pv3b", "pt3b", 4, vp3),
                "tr4": lambda u: transposes_x(u, "tr4", 1, xn, "ln4"), "mx1": a31, "mx2": a32}
            all_turns(pe, Own(pe, "pe_own", 0), TENSOR_TURN, stages, turn)
            tensor_b(pe, mm, mm3)

        @block.scalar
        def _(act):
            own = Own(act, "act_own", PER["act"])
            f = act.activation
            act.wait_ge(sig("w_in"), 6 * 16)
            for n in range(2):
                f(wq_h[:, n, :], big[n][:], ACT.Copy)
                f((b0, spread)[n][:], ptf[n][0:64, 0:1152], ACT.Copy)
            f(wk_h[:], kf[0][:], ACT.Copy)
            f(wv_h[:], kf[1][:], ACT.Copy).then_inc(sig("w_high"), 1)
            act.wait_ge(sig("consts"), 16 * n_consts)
            act.wait_ge(sig("w_ready"), 2)
            f(identm[:], ident[:], ACT.Copy)
            f(mask[:], xn[0][:], ACT.Copy)
            f(identb[:], ident[:], ACT.Copy).then_inc(sig("w_ready"), 1)
            f(memw[:, 1:2], memw[:, 0:1], ACT.Exp, scale=-1.0).then_inc(sig("memw"), 1)
            act.preload_act_table_set("natural_log_exp_and_others")
            turn = [None, None]

            def W(name, u):
                act.wait_ge(sig(name, u), at(name, turn[u], u))

            def rs(u, n, e=0, scale=1.0, src=None):
                W(f"var{n}", u)
                own.link(f(rstd[u][:, 0:1], mv[u][:, 1:2] if src is None else src, ACT.Ln,
                           bias=eps[:, e:e + 1], scale=scale))
                f(rstd[u][:, 0:1], rstd[u][:, 0:1], ACT.Exp, scale=-0.5).then_inc(sig(f"rstd{n}", u), 1)

            def a0(u):
                W("tr0", u)
                f(xT_h[u][:, :, 32:160], ps_f(u, 0, 256).rearrange("p (k t) -> p k t", k=2), ACT.Copy)\
                    .then_inc(sig("xT0h", u), 1)
                f(cT[u][:].rearrange("p k t -> p (k t)"), ps_f(u, 0, 256, 256), ACT.Copy)\
                    .then_inc(sig("cT0", u), 1)

            def v0h(u):
                W("kv0", u)
                f(v_h[u][:], ps_all[u][:, 1024:2048], ACT.Copy).then_inc(sig("v0h", u), 1)

            def k0h(u):
                W("k0r", u)
                f(k_h[u][:, :, 32:160], kf[u][:, 0, :].rearrange("p (a t) -> p a t", a=4), ACT.Copy)\
                    .then_inc(sig("k0h", u), 1)

            def q_high(u, h):
                W(f"q0r{h}", u)
                d, b = [x.rearrange("p (a h m) -> p a h m", a=2, h=2)[:, :, h, :] for x in (q_h[u], big[u][:])]
                f(d, b, ACT.Copy).then_inc(sig(f"q0h{h}", u), 1)

            def exps(u, n, h, scale):
                W(f"s{n}m{h}", u)
                if n == "0":
                    k = slice(16 * h, 16 * h + 16)
                    f(st32[u][:, 1, k], st32[u][:, 1, k], ACT.Exp, scale=scale)
                    c = slice(1024 * h, 1024 * h + 1024)
                    m = f(big[u][:, c], big[u][:, c], ACT.Exp, scale=scale)
                else:
                    for j in range(8 * h, 8 * h + 8):
                        c = slice(j * P, (j + 1) * P)
                        m = f(big[u][:, c], ps_all[u][:, c], ACT.Exp, scale=scale, bias=st32[u][:, 3, j:j + 1])
                m.then_inc(sig(f"e{n}{h}", u), 1)

            def turned_high(u, n, h):
                W(f"pT{n}{h}", u)
                c = slice(1024 * h, 1024 * h + 1024)
                f(pt_h[u][:, c], ps_all[u][:, c], ACT.Copy).then_inc(sig(f"pt{n}h{h}", u), 1)

            def a5(u):
                W("pv0", u)
                for i in range(2):
                    m = f(by_token(qhl[u][:])[:, :, i, :], by_block(u)[:, :, i, :], ACT.Copy)
                m.then_inc(sig("o0a", u), 1)

            def rms(u, n, src, y):
                W(f"{n}f", u)
                own.link(f(af2[u], src, ACT.Square, accum_out=y[:, 1:2]))
                own.link(f(y[:, 0:1], y[:, 1:2], ACT.Ln, bias=eps[:, 1:2], scale=1.0 / DM))
                f(y[:, 0:1], y[:, 0:1], ACT.Exp, scale=-0.5).then_inc(sig(f"{n}rstd", u), 1)

            def qkT(u, tr, nm, nk):
                W(tr, u)
                f((pt_h if nk == 8 else qp)[u][:, 0:1024], psb(u, 0), ACT.Copy).then_inc(sig(nm, u), 1)

            def a15(u):
                W("rlm", u)
                f(lg[u][:, 0, :], lg[u][:, 0, :], ACT.Exp, accum_out=sm[u][:, 8:9]).then_inc(sig("rle", u), 1)

            def a19(u):
                act.preload_act_table_set("exp_and_others")
                W("sgm", u)
                f(af2[u], af2[u], ACT.Tanh, scale=0.5).then_inc(sig("sge", u), 1)
                act.preload_act_table_set("natural_log_exp_and_others")

            def a31(u):
                W("mixqkv", u)
                f(big[u][:, 0:512], ps_f(u, 0), ACT.Copy).then_inc(sig("mixqkv_out", u), 1)

            stages = {
                "rs0": lambda u: rs(u, 0), "a0s": a0, "v0h": v0h, "k0h": k0h, "qh0": lambda u: q_high(u, 0),
                "qh1": lambda u: q_high(u, 1), "e00": lambda u: exps(u, "0", 0, SCALE0),
                "e01": lambda u: exps(u, "0", 1, SCALE0), "h00": lambda u: turned_high(u, "0", 0),
                "h01": lambda u: turned_high(u, "0", 1), "o0a": a5, "rs1": lambda u: rs(u, 1),
                "rq": lambda u: rms(u, "q1", qf[u], rstd[u][:, 0:3]),
                "rk": lambda u: rms(u, "k1", kvf[u][:, 0, :], rstd[u][:, 3:6]),
                "qT1": lambda u: qkT(u, "qkT1p", "qT1", 8),
                "e10": lambda u: exps(u, "1", 0, float(DHX) ** -0.5),
                "e11": lambda u: exps(u, "1", 1, float(DHX) ** -0.5), "h10": lambda u: turned_high(u, "1", 0),
                "h11": lambda u: turned_high(u, "1", 1), "rs2": lambda u: rs(u, 2), "a15s": a15,
                "rs3": lambda u: rs(u, 3), "a19s": a19, "qT3": lambda u: qkT(u, "tr3b", "qT3", 2),
                "e3a0": lambda u: exps(u, "3a", 0, float(DHM) ** -0.5),
                "e3a1": lambda u: exps(u, "3a", 1, float(DHM) ** -0.5),
                "h3a0": lambda u: turned_high(u, "3a", 0), "h3a1": lambda u: turned_high(u, "3a", 1),
                "e3b0": lambda u: exps(u, "3b", 0, float(DHM) ** -0.5),
                "e3b1": lambda u: exps(u, "3b", 1, float(DHM) ** -0.5),
                "h3b0": lambda u: turned_high(u, "3b", 0), "h3b1": lambda u: turned_high(u, "3b", 1),
                "rs4": lambda u: rs(u, 4), "a31s": a31}
            all_turns(act, own, SCALAR_TURN, stages, turn)
            scalar_b(act, own, f)

        @block.gpsimd
        def _(pool):
            for n in range(2):
                for b in (xT_h, xT_l, k_h, k_l):
                    pool.memset(b[n][:], 0.0).then_inc(sig("zeros"), 1)
            pool_b(pool)

        @block.vector
        def _(dve):
            own = Own(dve, "dve_own", PER["dve"])
            link, mark = own.link, own.mark
            tt, ts, cp, red = dve.tensor_tensor, dve.tensor_scalar, dve.tensor_copy, dve.tensor_reduce
            stt = dve.scalar_tensor_tensor

            def prepare(mark, y, var, scale, eps_):
                mark(ts(y[:, 2:3], var, -0.5 * scale, -0.5 * eps_, ALU.mult, ALU.add))

            def refine(own, y):
                own.wait()
                own.link(stt(y[:, 2:3], y[:, 0:1], y[:, 0:1], y[:, 2:3], ALU.mult, ALU.mult))
                own.link(stt(y[:, 0:1], y[:, 2:3], 1.5, y[:, 0:1], ALU.add, ALU.mult))

            for i, e in enumerate((EPS_LN, EPS_RMS, EPS_GN, 0.0)):
                mark(dve.memset(eps[:, i:i + 1], e))
            mark(dve.memset(acc[:], 0.0))
            for u in range(2):
                for v in (vp1, vp3):
                    mark(dve.memset(v[0][u][:], 1.0))
                    mark(dve.memset(v[1][u][:], 0.0))
            dve.wait_ge(sig("w_high"), 1)
            for n in range(2):
                mark(tt(wq_l[:, n, :], big[n][:], wq_h[:, n, :], ALU.subtract))
            mark(tt(b0[32:64, :], ptf[0][32:64, 0:1152], b0[32:64, :], ALU.subtract))
            mark(tt(wk_l[:], kf[0][:], wk_h[:], ALU.subtract))
            link(tt(wv_l[:], kf[1][:], wv_h[:], ALU.subtract))
            dve.wait_ge(sig("zeros"), 8)
            dve.memset(sm[0][:], 0.0).then_inc(sig("w_ready"), 1)
            dve.wait_ge(sig("consts"), 16 * n_consts)
            dve.memset(sm[1][:], 0.0).then_inc(sig("w_ready"), 1)
            dve.wait_ge(sig("w_ready"), 3)
            dve.wait_ge(sig("memw"), 1)
            link(ts(sinkT[:], sinkT[:], 1.0 / SCALE0, None, ALU.mult))
            link(ts(memw[:, 2:3], memw[:, 1:2], 1.0, None, ALU.add))
            link(dve.reciprocal(memw[:, 2:3], memw[:, 2:3]))
            link(ts(memw[:, 3:4], memw[:, 2:3], -1.0, 1.0, ALU.mult, ALU.add))

            turn = [None, None]

            def W(name, u):
                dve.wait_ge(sig(name, u), at(name, turn[u], u))

            def S(u, ins, name):
                ins.then_inc(sig(name, u), 1)

            def stats(u, n, x):
                link(dve.bn_stats(bst[u][:], x))
                apart(dve)
                S(u, dve.bn_aggr(mv[u][:], bst[u][:]), f"var{n}")
                W(f"var{n}", u)
                prepare(mark, rstd[u], mv[u][:, 1:2], 1.0, EPS_LN)

            def norm(u, n, x):
                W(f"rstd{n}", u)
                refine(own, rstd[u])
                S(u, ts(xn[u][:], x, mv[u][:, 0:1], rstd[u][:, 0:1], ALU.subtract, ALU.mult), f"ln{n}")

            def l0(u):
                dve.wait_ge(sig(f"x_in{u}"), turn[u] * 32 + 32)
                link(tt(xr[u][:], xin[u][:], rows[:, BO, :], ALU.add))
                stats(u, 0, xin[u][:])

            def a0(u):
                W("tr0", u)
                W("xT0h", u)
                W("cT0", u)
                link(tt(xT_l[u][:, :, 32:160], ps_f(u, 0, 256).rearrange("p (k t) -> p k t", k=2),
                        xT_h[u][:, :, 32:160], ALU.subtract))
                for d, b in ((q_h, xT_h), (q_l, xT_l)):
                    v = b[u][:]
                    last = cp(d[u][:, 0:512].rearrange("p (k i c) -> p k i c", k=KT_, i=NBLK),
                              bass.AP(v.tensor, v.offset, [v.ap[0], [160, KT_], [WIN, NBLK], [1, 2 * WIN]]))
                    if b is xT_h:
                        mark(last)
                S(u, last, "xT0")

            def rope_sin(srcb, dst, shape, sin):
                w = srcb.shape[1] // 2
                A_, B_, dA, dB = [shape(b) for b in (srcb[:, 0:w], srcb[:, w:2 * w], dst[:, 0:w], dst[:, w:2 * w])]
                mark(tt(dA, B_, sin, ALU.mult))
                mark(tt(dB, A_, sin, ALU.mult))

            def a1(u):
                W("keys0", u)
                kb = kf[u][:, 0, :]
                rope_sin(ps_f(u, 1), kf[u][:, 1, :], lambda b: b.rearrange("p (h i r) -> p h i r", h=2, i=NBLK),
                         k_table(sinI, 2))
                link(tt(kb.rearrange("p (a i r) -> p a i r", a=4, i=NBLK),
                        ps_f(u, 1).rearrange("p (a i r) -> p a i r", a=4, i=NBLK), k_table(cosI, 4), ALU.mult))
                mark(tt(kb[:, 0:256], kb[:, 0:256], kf[u][:, 1, 0:256], ALU.subtract))
                S(u, tt(kb[:, 256:512], kb[:, 256:512], kf[u][:, 1, 256:512], ALU.add), "k0r")

            def a1v(u):
                W("v0h", u)
                S(u, tt(v_l[u][:], ps_all[u][:, 1024:2048], v_h[u][:], ALU.subtract), "v0")

            def a1k(u):
                W("k0h", u)
                S(u, tt(k_l[u][:, :, 32:160], kf[u][:, 0, :].rearrange("p (a t) -> p a t", a=4),
                     k_h[u][:, :, 32:160], ALU.subtract), "kv0_out")

            def q_parts(u, h):
                W("q0" + "ab"[h], u)
                c, o = [slice(1024 * x, 1024 * x + 1024) for x in (h, 1 - h)]
                p2, b2, t2 = [b.rearrange("p (h m) -> p h m", h=2) for b in (ps_all[u][:, c], big[u][:, c], ptf[u][:, o])]
                mark(tt(t2, p2, q_table(sinI, 2), ALU.mult))
                mark(tt(b2, p2, q_table(cosI, 2), ALU.mult))

            def of_heads(b, h):
                return b.rearrange("p (a h m) -> p a h m", a=2, h=2)[:, :, h, :]

            def q_turned(u, h):
                if h == 0:
                    own.wait()
                b, t = of_heads(big[u][:], h), of_heads(ptf[u][:], h)
                mark(tt(b[:, 0], b[:, 0], t[:, 0], ALU.subtract))
                S(u, tt(b[:, 1], b[:, 1], t[:, 1], ALU.add), f"q0r{h}")

            def q_low(u, h):
                W(f"q0h{h}", u)
                S(u, tt(of_heads(q_l[u], h), of_heads(big[u][:], h), of_heads(q_h[u], h), ALU.subtract), f"q0_out{h}")

            def shifted0(u, h):
                W(f"s0p{h}", u)
                k = slice(16 * h, 16 * h + 16)
                c = slice(1024 * h, 1024 * h + 1024)
                p16 = ps_all[u][:, c].rearrange("p (a t) -> p a t", a=16)
                b16 = big[u][:, c].rearrange("p (a t) -> p a t", a=16)
                m_ = st32[u][:, 0, k]
                link(red(m_, p16, AX.X, ALU.max))
                link(tt(m_, m_, sinkT[:, k], ALU.max))
                mark(tt(st32[u][:, 1, k], sinkT[:, k], m_, ALU.subtract))
                S(u, tt(b16, p16, m_[:, :, None].to_broadcast([P, 16, 64]), ALU.subtract), f"s0m{h}")


            def normed0(u, h):
                k = slice(16 * h, 16 * h + 16)
                b16 = big[u][:, 1024 * h:1024 * h + 1024].rearrange("p (a t) -> p a t", a=16)
                l_ = st32[u][:, 2, k]
                W(f"e0{h}", u)
                link(red(l_, b16, AX.X, ALU.add))
                link(tt(l_, l_, st32[u][:, 1, k], ALU.add))
                link(dve.reciprocal(l_, l_))
                S(u, tt(b16, b16, l_[:, :, None].to_broadcast([P, 16, 64]), ALU.mult), f"n0{h}")

            def turned_low(u, n, h):
                W(f"pt{n}h{h}", u)
                c = slice(1024 * h, 1024 * h + 1024)
                last = tt(pt_l[u][:, c], ps_all[u][:, c], pt_h[u][:, c], ALU.subtract)
                if h == 0:
                    mark(last)
                else:
                    S(u, last, f"pt{n}")

            def a5(u):
                W("pv0", u)
                mark(cp(by_token(qhl[u][:])[:, :, 2, :], by_block(u)[:, :, 2, :]))
                S(u, cp(by_token(qhl[u][:])[:, :, 3, :], by_block(u)[:, :, 3, :]), "o0b")

            def a6(u):
                W("wo0", u)
                link(tt(xr[u][:], ps_f(u, 0, DM), xr[u][:], ALU.add))
                stats(u, 1, xr[u][:])

            def xTn(u, n):
                W(f"tr{n}", u)
                S(u, cp(xT[u][:].rearrange("p k t -> p (k t)"), ps_f(u, 1, DM)), f"xT{n}")

            def pack(u, dst, srcf, nh, dh, order, done=None):
                d = dst.rearrange("p (h a c d) -> p h a c d" if order == "hlhl" else "p (h c a d) -> p h a c d",
                                  a=2, c=2, d=dh)
                s = srcf.rearrange("p (h d) -> p h d", d=dh)[:, :, None, :].to_broadcast([P, nh, 2, dh])
                link(cp(d[:, :, :, 0, :], s))
                last = tt(d[:, :, :, 1, :], s, d[:, :, :, 0, :], ALU.subtract)
                if done is None:
                    mark(last)
                else:
                    S(u, last, done)

            def pack_values(u, vp, src):
                vh, vl = vp[0][u], vp[1][u]
                dh = vh.shape[2] - 1
                v = src.rearrange("p (h d) -> p h d", d=dh)
                link(cp(vh[:, :, 0:dh], v))
                mark(tt(vl[:, :, 0:dh], v, vh[:, :, 0:dh], ALU.subtract))

            def a7(u):
                W("qkv1", u)
                S(u, tt(qf[u], ps_f(u, 0, DM), rows[:, QB, :], ALU.add), "q1f")
                S(u, tt(kvf[u][:, 0, :], ps_f(u, 0, DM, DM), rows[:, KB, :], ALU.add), "k1f")
                link(tt(kvf[u][:, 1, :], ps_f(u, 1, DM), rows[:, VB, :], ALU.add))
                pack_values(u, vp1, kvf[u][:, 1, :])
                mark(tt(xr[u][:], xr[u][:], rows[:, OB, :], ALU.add))

            def a7q(u):
                W("q1rstd", u)
                link(ts(rstd[u][:, 2:3], rstd[u][:, 1:2], -0.5 / DM, -0.5 * EPS_RMS, ALU.mult, ALU.add))
                refine(own, rstd[u][:, 0:3])
                link(stt(qf[u], qf[u], rstd[u][:, 0:1], rows[:, NQ, :], ALU.mult, ALU.mult))
                pack(u, qp[u][:], qf[u], NHX, DHX, "hlhl")

            def a7k(u):
                W("k1rstd", u)
                link(ts(rstd[u][:, 5:6], rstd[u][:, 4:5], -0.5 / DM, -0.5 * EPS_RMS, ALU.mult, ALU.add))
                refine(own, rstd[u][:, 3:6])
                link(stt(kvf[u][:, 0, :], kvf[u][:, 0, :], rstd[u][:, 3:4], rows[:, NK_, :], ALU.mult, ALU.mult))
                pack(u, kp[u][:], kvf[u][:, 0, :], NHX, DHX, "hhll", "pk1")

            def a8(u):
                W("qkT1p", u)
                W("qT1", u)
                S(u, cp(pt_l[u][:, 0:1024], psb(u, 1)), "qkT1")

            def maxima(u, n, h):
                W(f"s{n}p{h}", u)
                c = slice(1024 * h, 1024 * h + 1024)
                p8 = ps_all[u][:, c].rearrange("p (a t) -> p a t", a=8)
                m_ = st32[u][:, 0, 8 * h:8 * h + 8]
                link(red(m_, p8, AX.X, ALU.max))
                scale = float(DHX if n == "1" else DHM) ** -0.5
                S(u, ts(st32[u][:, 3, 8 * h:8 * h + 8], m_, -scale, None, ALU.mult), f"s{n}m{h}")

            def heads_out(u, n, dst, dh):
                W(f"pv{n}", u)
                o = ps_f(u, 0).rearrange("p (h d) -> p h d", d=32)
                r = st32[u][:, 1, 0:16]
                link(dve.reciprocal(r[:, :, None], o[:, :, dh:dh + 1]))
                return tt(dst.rearrange("p (h d) -> p h d", d=dh), o[:, :, 0:dh],
                          r[:, :, None].to_broadcast([P, 16, dh]), ALU.mult)

            def a11(u):
                S(u, heads_out(u, "1", af[u][:], DHX), "a1")

            def a12(u):
                W("atr1", u)
                S(u, cp(aT[u][:].rearrange("p k t -> p (k t)"), ps_f(u, 1, DM)), "aT1")

            def a13(u):
                W("wo1", u)
                link(tt(xr[u][:], ps_f(u, 0, DM), xr[u][:], ALU.add))
                stats(u, 2, xr[u][:])

            def a15(u):
                W("rl", u)
                l0_ = lg[u][:, 0, :]
                link(tt(l0_, ps_f(u, 0, E0), rb[:], ALU.add))
                link(red(sm[u][:, 9:10], l0_, AX.X, ALU.max))
                S(u, ts(l0_, l0_, sm[u][:, 9:10], None, ALU.subtract), "rlm")

            def a15t(u):
                l0_, l1_ = lg[u][:, 0, :], lg[u][:, 1, :]
                W("rle", u)
                link(dve.reciprocal(sm[u][:, 8:9], sm[u][:, 8:9]))
                link(ts(l0_, l0_, sm[u][:, 8:9], None, ALU.mult))
                apart(dve)
                link(dve.max(sm[u][:, 0:8], l0_))
                apart(dve)
                link(dve.match_replace(l1_, sm[u][:, 0:8], l0_, 0.0))
                link(red(sm[u][:, 9:10], sm[u][:, 0:8], AX.X, ALU.add))
                S(u, tt(l0_, l0_, l1_, ALU.subtract), "rw")

            def a16(u):
                W("rwT", u)
                S(u, cp(wt[u][0:E0, :], PS[u][0:E0, 1, 0:P]), "rwT_out")

            def a17(u):
                W("eb", u)
                link(tt(xr[u][:], ps_f(u, 0, DM), xr[u][:], ALU.add))
                link(stt(xr[u][:], xn[u][:], sm[u][:, 9:10], xr[u][:], ALU.mult, ALU.add))
                stats(u, 3, xr[u][:])

            def a19(u):
                W("qkv3", u)
                mark(cp(qf[u], ps_f(u, 0, DM)))
                mark(cp(kvf[u][:, 0, 0:64], ps_f(u, 0, 64, DM)))
                pack_values(u, vp3, ps_f(u, 0, 64, DM + 64))
                own.wait()
                S(u, ts(af2[u], qf[u], 0.0, None, ALU.min), "sgm")
                pack(u, qp[u][:], qf[u], 32, DHM, "hlhl")
                pack(u, kp[u][:, 0:256], kvf[u][:, 0, 0:64], NHM, DHM, "hhll")

            def a19e(u):
                tmp = big[u][:, 4 * DM:5 * DM]
                W("sge", u)
                link(ts(tmp, af2[u], -0.5, 0.5, ALU.mult, ALU.add))
                link(dve.reciprocal(tmp, tmp))
                mark(ts(af[u][:], qf[u], 0.0, None, ALU.max))
                link(tt(tmp, tmp, af2[u], ALU.mult))
                S(u, tt(af[u][:], af[u][:], tmp, ALU.add), "pk3")

            def a20(u):
                W("tr3b", u)
                mark(cp(kp[u][:, 0:256], psb(u, 1)[:, 0:256]))
                W("qT3", u)
                S(u, cp(aT[u][:].rearrange("p k t -> p (k t)"), ps_f(u, 2, DM)), "qkT3")

            def a20m(u):
                W("mem", u)
                m4 = PS[u][:, 2:4, 0:256].rearrange("p b (s d) -> p s b d", s=2)
                den = sm[u][:, 8:12].rearrange("p (s b) -> p s b", s=2)[:, :, :, None]
                link(dve.reciprocal(den, m4[:, :, :, 64:65]))
                link(ts(sm[u][:, 8:12], sm[u][:, 8:12], memw[:, 2:3], None, ALU.mult))
                link(tt(af2[u].rearrange("p (s b d) -> p s b d", s=2, b=2), m4[:, :, :, 0:64],
                        den.to_broadcast([P, 2, 2, 64]), ALU.mult))
                S(u, tt(xr[u][:], xr[u][:], af2[u], ALU.add), "mem_out")

            def a22(u, half):
                n = "3" + "ab"[half]
                last = heads_out(u, n, af[u][:, half * P:(half + 1) * P], DHM)
                if half == 0:
                    S(u, last, "pv3a_out")
                    return
                link(last)
                link(stt(xr[u][:], af[u][:], memw[:, 3:4], xr[u][:], ALU.mult, ALU.add))
                apart(dve)
                link(cp(xall[:].rearrange("p (i u) d -> p i u d", u=2)[:, bass.ds(turn[u], 1), u, :], xr[u][:, None, :]))
                stats(u, 4, xr[u][:])

            def a31(u):
                W("mixqkv", u)
                apart(dve)
                mark(cp(vall[:].rearrange("p (i u) h d -> p i u (h d)", u=2)[:, bass.ds(turn[u], 1), u, :],
                        ps_f(u, 1, DM, DM)[:, None, :]))

            def a32(u):
                W("mixs", u)
                link(tt(acc[:].rearrange("p h t -> p (h t)"), ps_f(u, 2, DM), acc[:].rearrange("p h t -> p (h t)"),
                        ALU.add))

            stages = {
                "l0": l0, "n0": lambda u: norm(u, 0, xin[u][:]), "a0v": a0, "k0": a1, "v0": a1v, "k0l": a1k,
                "q1": lambda u: q_parts(u, 0), "q2": lambda u: q_parts(u, 1), "q3": lambda u: q_turned(u, 0),
                "q4": lambda u: q_turned(u, 1),
                "ql0": lambda u: q_low(u, 0), "ql1": lambda u: q_low(u, 1), "s00": lambda u: shifted0(u, 0),
                "s01": lambda u: shifted0(u, 1), "n00": lambda u: normed0(u, 0),
                "n01": lambda u: normed0(u, 1), "l00": lambda u: turned_low(u, "0", 0),
                "l01": lambda u: turned_low(u, "0", 1), "o0b": a5, "a6v": a6,
                "n1": lambda u: norm(u, 1, xr[u][:]), "xT1": lambda u: xTn(u, 1), "a7v": a7, "a7q": a7q,
                "a7k": a7k, "a8": a8, "s10": lambda u: maxima(u, "1", 0), "s11": lambda u: maxima(u, "1", 1),
                "l10": lambda u: turned_low(u, "1", 0), "l11": lambda u: turned_low(u, "1", 1), "a11": a11,
                "a12": a12, "a13": a13, "n2": lambda u: norm(u, 2, xr[u][:]), "xT2": lambda u: xTn(u, 2),
                "a15v": a15, "a15t": a15t, "a16v": a16, "a17v": a17, "n3": lambda u: norm(u, 3, xr[u][:]),
                "xT3": lambda u: xTn(u, 3), "a19v": a19, "a19e": a19e, "pk3v": a20, "mv": a20m,
                "s3a0": lambda u: maxima(u, "3a", 0), "s3a1": lambda u: maxima(u, "3a", 1),
                "l3a0": lambda u: turned_low(u, "3a", 0), "l3a1": lambda u: turned_low(u, "3a", 1),
                "a22a": lambda u: a22(u, 0), "s3b0": lambda u: maxima(u, "3b", 0),
                "s3b1": lambda u: maxima(u, "3b", 1), "l3b0": lambda u: turned_low(u, "3b", 0),
                "l3b1": lambda u: turned_low(u, "3b", 1), "a22b": lambda u: a22(u, 1),
                "n4": lambda u: norm(u, 4, xr[u][:]), "xT4": lambda u: xTn(u, 4), "a31v": a31, "a32v": a32}
            all_turns(dve, own, VECTOR_TURN, stages, turn)
            vector_b(dve, own, prepare, refine)


def shape_constants():
    f = np.float32
    inv = (f(1.0) / (f(10000.0) ** (np.arange(0, D0, 2, dtype=f) / f(D0)))).astype(f)
    ang = (np.arange(T, dtype=f)[None, :] * np.tile(inv, 4)[:, None]).astype(f).astype(np.float64)

    def cols(m):
        return np.broadcast_to(m.reshape(P, NBLK, 1, WIN), (P, NBLK, G0, WIN)).reshape(P, 512).astype(f)
    r, c = np.arange(P)[:, None] % WIN, np.arange(64)[None, :]
    seen = (c > r) & (c <= r + WIN)
    masks = np.stack([seen & (c >= WIN)] + [seen] * (NBLK - 1), 1)
    gam = 1.0 - 2.0 ** (-5.0 - np.arange(2))
    expo = np.arange(T)[None, :] - np.arange(T)[:, None]
    d = np.where(expo[None] <= 0, gam[:, None, None] ** expo[None], 0.0)
    dn = d / np.sqrt(d.sum(-1))[:, None, :] / np.sqrt(float(P))
    spread = np.zeros((64, 1152), f)
    for row in (0, 32):
        for g in range(4):
            spread[row + g, 0:512].reshape(NBLK, G0, WIN)[:, g] = 1
            spread[row + g, 512 + g * P:512 + (g + 1) * P] = 1
        spread[row, 1024:1152] = 1
    return {
        "spread": spread, "ident": np.eye(P, dtype=f), "cosI": cols(np.cos(ang)), "sinI": cols(np.sin(ang)),
        "mask": np.where(masks, f(0), f(MASKED)).reshape(P, NBLK * 64).astype(f),
        "decay": np.ascontiguousarray(dn.transpose(2, 0, 1)).astype(f),
        "iota8": np.broadcast_to(np.arange(NE, dtype=f), (P, NE)).copy(),
    }


def layout(x, ctx_2048, **w):
    def tiles(m):
        return m.reshape(-1, P, m.shape[1]).transpose(1, 0, 2)
    L0, X0, M = "L0_attn_", "L0_xattn_", "L1_attn_"
    wq = w[L0 + "Wq"].reshape(DM, 2, 4, G0, 2, 32).transpose(0, 4, 1, 3, 2, 5).reshape(DM, 2048)
    wk = w[L0 + "Wk"].reshape(DM, 2, 4, 2, 32).transpose(0, 3, 1, 2, 4).reshape(DM, 512)
    bq = w[L0 + "bq"].reshape(2, 4, G0, 2, 32).transpose(2, 3, 0, 1, 4).reshape(G0, 4 * P)
    bk = w[L0 + "bk"].reshape(2, 4, 2, 32).transpose(2, 0, 1, 3).reshape(4, P)
    wo = w[L0 + "Wo"].reshape(4, 2, G0, D0, DM).transpose(1, 3, 0, 2, 4).reshape(P, 16, DM)
    sinks = w[L0 + "sinks"].reshape(2, 4, G0).transpose(2, 1, 0)
    sinks = np.broadcast_to(sinks[:, None, :, :, None], (G0, WIN, 4, 2, NBLK)).reshape(P, 32)
    b0 = np.zeros((64, 1152), np.float32)
    for row in (0, 32):
        b0[row:row + 4, 0:512], b0[row:row + 4, 512:640], b0[row, 640:1152] = bq, bk, w[L0 + "bv"]
    mem = np.concatenate([w[M + "memory"], w[M + "memory_norm"]], 1)
    d = {
        "x": x, "ctx": ctx_2048, "wq": tiles(wq), "wk": tiles(wk), "wv": tiles(w[L0 + "Wv"]), "wo": wo,
        "b0": b0, "sinkT": sinks,
        "wx": np.stack([tiles(w[X0 + n].T) for n in ("q_w", "k_img_w", "v_img_w", "o_w")], 1),
        "rows": np.stack([w[L0 + "bo"], w[X0 + "q_b"], w[X0 + "k_img_b"], w[X0 + "v_img_b"], w[X0 + "o_b"],
                          w[X0 + "norm_q_w"], w[X0 + "norm_k_img_w"], w["L1_xattn_gn_gamma"],
                          w["L1_xattn_gn_beta"]]),
        "rw": tiles(w["L0_ffn_router_weight"].T), "rb": w["L0_ffn_router_bias"][None],
        "ebias": w["L0_ffn_expert_bias"],
        "wm": tiles(np.concatenate([w[M + "Wq"].T, w[M + "Wk"].T, w[M + "Wv"].T], 1)),
        "mem": mem, "memw": w[M + "memory_weight"][None],
        "wh": w["L1_xattn_Wh"].transpose(1, 0, 2),
        "wgo": np.stack([tiles(w["L1_xattn_wg_w"]), tiles(w["L1_xattn_wo_w"])], 1),
        "gw": tiles(w["L1_ffn_gate_weight"].T),
        "gu": w["L1_ffn_gate_up_proj"].transpose(0, 2, 1).reshape(NE, KT_, P, 2 * NI).transpose(0, 2, 1, 3)
        .reshape(NE, P, KT_ * 2 * NI),
        "dn": w["L1_ffn_down_proj"].transpose(0, 2, 1).reshape(NE, 4, P, DM).transpose(0, 2, 1, 3)
        .reshape(NE, P, 4 * DM),
    }
    d.update(shape_constants())
    return {k: np.ascontiguousarray(v) for k, v in d.items()}


def kernel(**inputs):
    import concourse.bacc as _bacc
    from concourse.bass_utils import run_bass_kernel_spmd as _run

    nc = _bacc.Bacc("TRN2", target_bir_lowering=False, num_devices=1)
    data = layout(**{k: np.asarray(v) for k, v in inputs.items()})
    arrays, args = {}, {}
    for name, v in data.items():
        arrays[f"in_{name}"] = v
        args[name] = nc.dram_tensor(f"in_{name}", v.shape, mybir.dt.from_np(v.dtype), kind="ExternalInput").ap()
    out = nc.dram_tensor("out_0", (NSEQ, T, DM), F32, kind="ExternalOutput").ap()
    program(nc, args, out)
    return _run(nc, [arrays], core_ids=[0]).results[0]["out_0"]
```
